# Optimizing a Trainium2 kernel written in Bass

```python
import numpy as np
import jax
import jax.numpy as jnp

def _softmax(x, axis=-1):
    return jax.nn.softmax(x, axis=axis)

def _gelu(x):
    return jax.nn.gelu(x, approximate=True)

def _silu(x):
    return jax.nn.silu(x)

def _sigmoid(x):
    return jax.nn.sigmoid(x)

def _layernorm(x, axis=-1, eps=1e-05):
    m = jnp.mean(x, axis=axis, keepdims=True)
    v = jnp.var(x, axis=axis, keepdims=True)
    return (x - m) / jnp.sqrt(v + eps)

def _scatter_add(tgt, idx, src, axis=0):
    return tgt.at[idx].add(src)

def _segment_sum(src, seg, n):
    return jax.ops.segment_sum(src, seg, n)
kernel_name = 'mk_gnn_resnorm_d4_gnn_r32_212793'

def setup_inputs(seed: int=0):
    np.random.seed(seed)
    _w = jnp.asarray

    def _rec_inputs():
        import jax
        import jax.numpy as jnp
        _gk = jax.random.key(seed)
        x = -0.0005121 + 1.001 * jax.random.normal(jax.random.fold_in(_gk, 1), (3125, 64), jnp.float32)
        src = jax.random.randint(jax.random.fold_in(_gk, 2), (100000,), 0, 3125, jnp.int32)
        dst = jnp.minimum((3125 * jax.random.uniform(jax.random.fold_in(_gk, 3), (100000,)) ** 2.0).astype(jnp.int32), 99999)
        _o = jnp.argsort(dst, stable=True)
        src = src[_o]
        dst = dst[_o]
        edge_attr_2 = -0.000414295 + 0.999828 * jax.random.normal(jax.random.fold_in(_gk, 13), (100000, 2), jnp.float32)
        return (x, src, dst, edge_attr_2)
    x, src, dst, edge_attr_2 = _rec_inputs()

    def _L0_gnn_setup():
        import jax, jax.numpy as jnp
        import numpy as np
        NEG_SLOPE = 0.2

        def _gat_layer(x, src, dst, n_nodes, W, a_src, a_dst, b):
            h = x @ W
            alpha_s = h @ a_src
            alpha_d = h @ a_dst
            e = jax.nn.leaky_relu(alpha_s[src] + alpha_d[dst], NEG_SLOPE)
            m = jax.ops.segment_max(e, dst, num_segments=n_nodes)
            w = jnp.exp(e - m[dst])
            z = jax.ops.segment_sum(w, dst, num_segments=n_nodes)
            alpha = w / (z[dst] + 1e-16)
            out = jax.ops.segment_sum(alpha[:, None] * h[src], dst, num_segments=n_nodes)
            return out + b
        key = jax.random.key(seed)
        N, E, D_IN, D_H, D_OUT = (50000, 25000, 64, 64, 64)
        ks = jax.random.split(key, 12)
        x = jax.random.normal(ks[0], (N, D_IN), dtype=jnp.float32)
        edge_index = jax.random.randint(ks[1], (2, E), 0, N, dtype=jnp.int64)
        s = 1.0 / np.sqrt(D_IN)
        W1 = jax.random.normal(ks[2], (D_IN, D_H), dtype=jnp.float32) * s
        a_src1 = jax.random.normal(ks[3], (D_H,), dtype=jnp.float32) * s
        a_dst1 = jax.random.normal(ks[4], (D_H,), dtype=jnp.float32) * s
        b1 = jnp.zeros((D_H,), dtype=jnp.float32)
        s2 = 1.0 / np.sqrt(D_H)
        W2 = jax.random.normal(ks[5], (D_H, D_OUT), dtype=jnp.float32) * s2
        a_src2 = jax.random.normal(ks[6], (D_OUT,), dtype=jnp.float32) * s2
        a_dst2 = jax.random.normal(ks[7], (D_OUT,), dtype=jnp.float32) * s2
        b2 = jnp.zeros((D_OUT,), dtype=jnp.float32)
        return {'x': x, 'edge_index': edge_index, 'W1': W1, 'a_src1': a_src1, 'a_dst1': a_dst1, 'b1': b1, 'W2': W2, 'a_src2': a_src2, 'a_dst2': a_dst2, 'b2': b2}
    _L0_gnn_all = _L0_gnn_setup()
    _L0_gnn_in = {k: v for k, v in _L0_gnn_all.items() if k in ('W1', 'a_src1', 'a_dst1', 'b1', 'W2', 'a_src2', 'a_dst2', 'b2')}
    del _L0_gnn_all

    def _L1_gnn_setup():
        import jax, jax.numpy as jnp
        import numpy as np
        K = 3
        SLOPE = 0.01
        N_NODES = 50000
        N_EDGES = 25000
        D_IN = 64
        D_OUT = 64
        E_DIM = 2

        def _moments(z_e, Wm_list):
            moms = [z_e]
            mu = z_e.mean(axis=0, keepdims=True)
            for k in range(2, K + 1):
                mk = jnp.mean((z_e - mu) ** k, axis=0)
                mk = jnp.sign(mk) * jnp.abs(mk) ** (1.0 / k)
                moms.append(mk @ Wm_list[k - 2].T)
            return moms
        key = jax.random.key(seed)
        ks = jax.random.split(key, 10)
        s = 0.1
        return {'h': jax.random.normal(ks[0], (N_NODES, D_IN), dtype=jnp.float32), 'e': jax.random.normal(ks[1], (N_EDGES, E_DIM), dtype=jnp.float32), 'src': jax.random.randint(ks[2], (N_EDGES,), 0, N_NODES), 'dst': jax.random.randint(ks[3], (N_EDGES,), 0, N_NODES), 'W_fc': jax.random.normal(ks[4], (D_OUT, D_IN), dtype=jnp.float32) * s, 'W_attn': jax.random.normal(ks[5], (1, 2 * D_OUT * K + E_DIM), dtype=jnp.float32) * s, 'W_edge': jax.random.normal(ks[6], (E_DIM, E_DIM), dtype=jnp.float32) * s, 'W_e2n': jax.random.normal(ks[7], (D_OUT, E_DIM), dtype=jnp.float32) * s, 'W_m1': jax.random.normal(ks[8], (D_OUT, D_OUT), dtype=jnp.float32) * s, 'W_m2': jax.random.normal(ks[9], (D_OUT, D_OUT), dtype=jnp.float32) * s}
    _L1_gnn_all = _L1_gnn_setup()
    _L1_gnn_in = {k: v for k, v in _L1_gnn_all.items() if k in ('W_fc', 'W_attn', 'W_edge', 'W_e2n', 'W_m1', 'W_m2')}
    del _L1_gnn_all

    def _L2_gnn_setup():
        import jax, jax.numpy as jnp
        import numpy as np
        N_NODES = 3125
        N_EDGES = 1250000
        D = 64
        L = 2
        BN_EPS = 1e-05

        def _res_gated_conv(x, src, dst, Wk, bk, Wq, bq, Wv, bv, Ws, bs, b):
            k = x @ Wk + bk
            q = x @ Wq + bq
            v = x @ Wv + bv
            msg = jax.nn.sigmoid(k[dst] + q[src]) * v[src]
            agg = jnp.zeros_like(k).at[dst].add(msg)
            return agg + x @ Ws + bs + b

        def _batch_norm(x, gamma, beta):
            mean = jnp.mean(x, axis=0)
            var = jnp.mean(jnp.square(x - mean), axis=0)
            return (x - mean) * jax.lax.rsqrt(var + BN_EPS) * gamma + beta
        key = jax.random.key(seed)
        ks = jax.random.split(key, 16)
        s = 1.0 / np.sqrt(D)
        inp = {'x': jax.random.normal(ks[0], (N_NODES, D), dtype=jnp.float32), 'edge_index': jax.random.randint(ks[1], (2, N_EDGES), 0, N_NODES, dtype=jnp.int32), 'batch': jnp.zeros((N_NODES,), dtype=jnp.int32), 'Wk': jax.random.uniform(ks[2], (L, D, D), jnp.float32, -s, s), 'bk': jax.random.uniform(ks[3], (L, D), jnp.float32, -s, s), 'Wq': jax.random.uniform(ks[4], (L, D, D), jnp.float32, -s, s), 'bq': jax.random.uniform(ks[5], (L, D), jnp.float32, -s, s), 'Wv': jax.random.uniform(ks[6], (L, D, D), jnp.float32, -s, s), 'bv': jax.random.uniform(ks[7], (L, D), jnp.float32, -s, s), 'Ws': jax.random.uniform(ks[8], (L, D, D), jnp.float32, -s, s), 'bs': jax.random.uniform(ks[9], (L, D), jnp.float32, -s, s), 'bias': jnp.zeros((L, D), dtype=jnp.float32), 'gamma': jnp.ones((L, D), dtype=jnp.float32), 'beta': jnp.zeros((L, D), dtype=jnp.float32)}
        return inp
    _L2_gnn_all = _L2_gnn_setup()
    _L2_gnn_in = {k: v for k, v in _L2_gnn_all.items() if k in ('Wk', 'bk', 'Wq', 'bq', 'Wv', 'bv', 'Ws', 'bs', 'bias', 'gamma', 'beta')}
    del _L2_gnn_all

    def _L3_gnn_setup():
        import jax, jax.numpy as jnp
        import numpy as np
        N_NODES = 3125
        N_EDGES = 50000
        D = 64
        H = 64
        key = jax.random.key(seed)
        k1, k2, k3, k4, k5, k6 = jax.random.split(key, 6)
        x = jax.random.normal(k1, (N_NODES, D), dtype=jnp.float32)
        edge_index = jax.random.randint(k2, (2, N_EDGES), 0, N_NODES, dtype=jnp.int64)
        s1 = 1.0 / np.sqrt(2 * D)
        s2 = 1.0 / np.sqrt(H)
        W1 = jax.random.uniform(k3, (H, 2 * D), dtype=jnp.float32, minval=-s1, maxval=s1)
        b1 = jax.random.uniform(k4, (H,), dtype=jnp.float32, minval=-s1, maxval=s1)
        W2 = jax.random.uniform(k5, (D, H), dtype=jnp.float32, minval=-s2, maxval=s2)
        b2 = jax.random.uniform(k6, (D,), dtype=jnp.float32, minval=-s2, maxval=s2)
        return {'x': x, 'W1': W1, 'b1': b1, 'W2': W2, 'b2': b2, 'edge_index': edge_index}
    _L3_gnn_all = _L3_gnn_setup()
    _L3_gnn_in = {k: v for k, v in _L3_gnn_all.items() if k in ('W1', 'b1', 'W2', 'b2')}
    del _L3_gnn_all
    return {'x': x, 'src': src, 'dst': dst, 'edge_attr_2': edge_attr_2, 'L0_gnn_W1': _L0_gnn_in['W1'], 'L0_gnn_a_src1': _L0_gnn_in['a_src1'], 'L0_gnn_a_dst1': _L0_gnn_in['a_dst1'], 'L0_gnn_b1': _L0_gnn_in['b1'], 'L0_gnn_W2': _L0_gnn_in['W2'], 'L0_gnn_a_src2': _L0_gnn_in['a_src2'], 'L0_gnn_a_dst2': _L0_gnn_in['a_dst2'], 'L0_gnn_b2': _L0_gnn_in['b2'], 'L1_gnn_W_fc': _L1_gnn_in['W_fc'], 'L1_gnn_W_attn': _L1_gnn_in['W_attn'], 'L1_gnn_W_edge': _L1_gnn_in['W_edge'], 'L1_gnn_W_e2n': _L1_gnn_in['W_e2n'], 'L1_gnn_W_m1': _L1_gnn_in['W_m1'], 'L1_gnn_W_m2': _L1_gnn_in['W_m2'], 'L2_gnn_Wk': _L2_gnn_in['Wk'], 'L2_gnn_bk': _L2_gnn_in['bk'], 'L2_gnn_Wq': _L2_gnn_in['Wq'], 'L2_gnn_bq': _L2_gnn_in['bq'], 'L2_gnn_Wv': _L2_gnn_in['Wv'], 'L2_gnn_bv': _L2_gnn_in['bv'], 'L2_gnn_Ws': _L2_gnn_in['Ws'], 'L2_gnn_bs': _L2_gnn_in['bs'], 'L2_gnn_bias': _L2_gnn_in['bias'], 'L2_gnn_gamma': _L2_gnn_in['gamma'], 'L2_gnn_beta': _L2_gnn_in['beta'], 'L3_gnn_W1': _L3_gnn_in['W1'], 'L3_gnn_b1': _L3_gnn_in['b1'], 'L3_gnn_W2': _L3_gnn_in['W2'], 'L3_gnn_b2': _L3_gnn_in['b2']}

def reference(x, src, dst, edge_attr_2, L0_gnn_W1, L0_gnn_a_src1, L0_gnn_a_dst1, L0_gnn_b1, L0_gnn_W2, L0_gnn_a_src2, L0_gnn_a_dst2, L0_gnn_b2, L1_gnn_W_fc, L1_gnn_W_attn, L1_gnn_W_edge, L1_gnn_W_e2n, L1_gnn_W_m1, L1_gnn_W_m2, L2_gnn_Wk, L2_gnn_bk, L2_gnn_Wq, L2_gnn_bq, L2_gnn_Wv, L2_gnn_bv, L2_gnn_Ws, L2_gnn_bs, L2_gnn_bias, L2_gnn_gamma, L2_gnn_beta, L3_gnn_W1, L3_gnn_b1, L3_gnn_W2, L3_gnn_b2):
    import jax
    import jax.numpy as jnp

    def _L0_gnn_ref(x, edge_index, W1, a_src1, a_dst1, b1, W2, a_src2, a_dst2, b2):
        import jax, jax.numpy as jnp
        import numpy as np
        NEG_SLOPE = 0.2

        def _gat_layer(x, src, dst, n_nodes, W, a_src, a_dst, b):
            h = x @ W
            alpha_s = h @ a_src
            alpha_d = h @ a_dst
            e = jax.nn.leaky_relu(alpha_s[src] + alpha_d[dst], NEG_SLOPE)
            m = jax.ops.segment_max(e, dst, num_segments=n_nodes)
            w = jnp.exp(e - m[dst])
            z = jax.ops.segment_sum(w, dst, num_segments=n_nodes)
            alpha = w / (z[dst] + 1e-16)
            out = jax.ops.segment_sum(alpha[:, None] * h[src], dst, num_segments=n_nodes)
            return out + b
        n_nodes = x.shape[0]
        loops = jnp.arange(n_nodes, dtype=edge_index.dtype)
        src = jnp.concatenate([edge_index[0], loops])
        dst = jnp.concatenate([edge_index[1], loops])
        h = _gat_layer(x, src, dst, n_nodes, W1, a_src1, a_dst1, b1)
        h = jax.nn.relu(h)
        out = _gat_layer(h, src, dst, n_nodes, W2, a_src2, a_dst2, b2)
        return out

    def _L1_gnn_ref(h, e, src, dst, W_fc, W_attn, W_edge, W_e2n, W_m1, W_m2):
        import jax, jax.numpy as jnp
        import numpy as np
        K = 3
        SLOPE = 0.01
        N_NODES = 50000
        N_EDGES = 25000
        D_IN = 64
        D_OUT = 64
        E_DIM = 2

        def _moments(z_e, Wm_list):
            moms = [z_e]
            mu = z_e.mean(axis=0, keepdims=True)
            for k in range(2, K + 1):
                mk = jnp.mean((z_e - mu) ** k, axis=0)
                mk = jnp.sign(mk) * jnp.abs(mk) ** (1.0 / k)
                moms.append(mk @ Wm_list[k - 2].T)
            return moms
        N = h.shape[0]
        D = W_fc.shape[0]
        z = h @ W_fc.T
        z_src = z[src]
        z_dst = z[dst]
        ex = e @ W_edge.T
        wm = [W_m1, W_m2]
        src_m = _moments(z_src, wm)
        dst_m = _moments(z_dst, wm)
        wa = W_attn[0]
        blk = [wa[i * D:(i + 1) * D] for i in range(2 * K)]
        w_e = wa[2 * K * D:]
        a = z_src @ blk[0] + z_dst @ blk[K] + ex @ w_e
        for k in range(1, K):
            a = a + src_m[k] @ blk[k] + dst_m[k] @ blk[K + k]
        att = jnp.where(a > 0, a, SLOPE * a)
        m = jax.ops.segment_max(att, dst, num_segments=N)
        expv = jnp.exp(att - m[dst])
        denom = jax.ops.segment_sum(expv, dst, num_segments=N)
        w = expv / denom[dst]
        ez = ex @ W_e2n.T
        msg = w[:, None] * (z_src + ez)
        return jax.ops.segment_sum(msg, dst, num_segments=N)

    def _L2_gnn_ref(x, edge_index, batch, Wk, bk, Wq, bq, Wv, bv, Ws, bs, bias, gamma, beta):
        import jax, jax.numpy as jnp
        import numpy as np
        N_NODES = 3125
        N_EDGES = 1250000
        D = 64
        L = 2
        BN_EPS = 1e-05

        def _res_gated_conv(x, src, dst, Wk, bk, Wq, bq, Wv, bv, Ws, bs, b):
            k = x @ Wk + bk
            q = x @ Wq + bq
            v = x @ Wv + bv
            msg = jax.nn.sigmoid(k[dst] + q[src]) * v[src]
            agg = jnp.zeros_like(k).at[dst].add(msg)
            return agg + x @ Ws + bs + b

        def _batch_norm(x, gamma, beta):
            mean = jnp.mean(x, axis=0)
            var = jnp.mean(jnp.square(x - mean), axis=0)
            return (x - mean) * jax.lax.rsqrt(var + BN_EPS) * gamma + beta
        src = edge_index[0]
        dst = edge_index[1]
        for l in range(L):
            x = _res_gated_conv(x, src, dst, Wk[l], bk[l], Wq[l], bq[l], Wv[l], bv[l], Ws[l], bs[l], bias[l])
            x = jax.nn.relu(x)
            x = _batch_norm(x, gamma[l], beta[l])
        return x

    def _L3_gnn_ref(x, W1, b1, W2, b2, edge_index):
        import jax, jax.numpy as jnp
        import numpy as np
        N_NODES = 3125
        N_EDGES = 50000
        D = 64
        H = 64
        src = edge_index[0]
        dst = edge_index[1]
        xi = x[dst]
        xj = x[src]
        m = jnp.concatenate([xi, xj - xi], axis=-1)
        h = jax.nn.relu(m @ W1.T + b1)
        e = h @ W2.T + b2
        agg = jax.ops.segment_max(e, dst, num_segments=x.shape[0])
        return jnp.where(jnp.isneginf(agg), jnp.float32(0.0), agg)
    edge_index = jnp.stack([src, dst])
    batch0 = jnp.zeros((3125,), jnp.int32)
    x = _layernorm(x + _L0_gnn_ref(x, edge_index, L0_gnn_W1, L0_gnn_a_src1, L0_gnn_a_dst1, L0_gnn_b1, L0_gnn_W2, L0_gnn_a_src2, L0_gnn_a_dst2, L0_gnn_b2), axis=-1)
    x = _layernorm(x + _L1_gnn_ref(x, edge_attr_2, src, dst, L1_gnn_W_fc, L1_gnn_W_attn, L1_gnn_W_edge, L1_gnn_W_e2n, L1_gnn_W_m1, L1_gnn_W_m2), axis=-1)
    x = _layernorm(x + _L2_gnn_ref(x, edge_index, batch0, L2_gnn_Wk, L2_gnn_bk, L2_gnn_Wq, L2_gnn_bq, L2_gnn_Wv, L2_gnn_bv, L2_gnn_Ws, L2_gnn_bs, L2_gnn_bias, L2_gnn_gamma, L2_gnn_beta), axis=-1)
    x = _layernorm(x + _L3_gnn_ref(x, L3_gnn_W1, L3_gnn_b1, L3_gnn_W2, L3_gnn_b2, edge_index), axis=-1)
    return x

_drawn_inputs = setup_inputs


def setup_inputs(seed=0):
    import zlib

    import numpy as np

    out = dict(_drawn_inputs(seed))
    spreads = {'L0_gnn_b1': (0.0, 0.1),
     'L0_gnn_b2': (0.0, 0.1),
     'L2_gnn_bias': (0.0, 0.1),
     'L2_gnn_gamma': (1.0, 0.2),
     'L2_gnn_beta': (0.0, 0.1)}
    factors = {'edge_attr_2': 8.0,
     'L0_gnn_a_dst1': 2.959,
     'L0_gnn_a_dst2': 6.538,
     'L1_gnn_W_edge': 8.0,
     'L1_gnn_W_e2n': 8.0,
     'L1_gnn_W_m2': 5.747}
    for name, (base, spread) in spreads.items():
        noise = np.random.default_rng([zlib.crc32(name.encode()), seed]).standard_normal(out[name].shape)
        drawn = base * np.exp(spread * noise) if base else spread * noise
        out[name] = jnp.asarray(drawn.astype(out[name].dtype))
    for name, factor in factors.items():
        out[name] = (out[name] * factor).astype(out[name].dtype)
    return out
```

```python
import concourse.bass as bass
from concourse import mybir
from contextlib import ExitStack

f32 = mybir.dt.float32
i32 = mybir.dt.int32
u32 = mybir.dt.uint32
bf16 = mybir.dt.bfloat16
ALU = mybir.AluOpType
ACT = mybir.ActivationFunctionType
AX = mybir.AxisListType

P = 128
N, E, D = 3125, 100000, 64
TILES = -(-N // P)
LASTN = N - (TILES - 1) * P
CHUNKS = -(-E // P)
LASTE = E - (CHUNKS - 1) * P
VISITS = CHUNKS + TILES - 1
Q = 4
U = 4
NG = -(-(-(-VISITS // Q)) // U) * U
VB = -(-NG * Q // P)
VP = VB * P
REC = 6 * P
NF = 10
F_SRC, F_DREL, F_EREL, F_RST, F_A0, F_A1, F_XW, F_SHI, F_DHI, F_SLO = range(NF)
WA = 68
BIG = 1e30
LN_EPS = 1e-5
BN_EPS = 1e-5


class At:

    def __init__(self, c, i=None):
        self.c, self.i = c, i

    def times(self, m, a=0):
        return self.c * m + a if self.i is None else self.i * (m * U) + (self.c * m + a)

    def rounds(self, m, a=0):
        return (self.c // U) * m + a if self.i is None else self.i * m + ((self.c // U) * m + a)

    @property
    def slot(self):
        return self.c % U

    def par(self, n):
        return self.c % n


def steps(e, stages):
    top = max(lag for lag, _ in stages)
    first = -(-(top + U) // U) * U

    def one(c, i=None):
        for lag, fn in stages:
            if i is not None or 0 <= c - lag < NG:
                fn(At(c - lag, i))

    for s in range(first):
        one(s)
    with e.Fori(0, (NG - first) // U) as i:
        for k in range(U):
            one(first + k, i)
    for s in range(NG, NG + top):
        one(s)


def build(nc, A, out):
    ctx = ExitStack()
    with ctx, nc.allow_non_contiguous_dma(reason="small columns and transposed weights"):
        def sb(name, shape, dt=f32):
            return ctx.enter_context(nc.sbuf_tensor(name, shape, dt))

        def pb(name, shape, dt=f32):
            return ctx.enter_context(nc.psum_tensor(name, shape, dt))

        made = {}

        def sem(name):
            if name not in made:
                made[name] = ctx.enter_context(nc.semaphore(name))
            return made[name]

        class Own:

            def __init__(self, e, name):
                self.e, self.sem, self.n = e, sem(name), 0

            def done(self, ins):
                self.n += 1
                ins.then_inc(self.sem, 1)

            def wait(self):
                if self.n:
                    self.e.wait_ge(self.sem, self.n)

            def __call__(self, ins):
                self.done(ins)
                self.wait()

        def gate(e, who, s, val):
            if isinstance(val, int):
                if val > 0:
                    e.wait_ge(s, val)
            else:
                e.wait_ge(s, val)
                e.sem_inc(sem("passed_" + who), 1)

        rec_d = nc.dram_tensor("rec_d", [CHUNKS + 1, REC], i32)
        ohT_d = nc.dram_tensor("ohT_d", [NG, P, Q * P], bf16)
        ohE_d = nc.dram_tensor("ohE_d", [NG, P, Q * P], bf16)
        tv_d = nc.dram_tensor("tv_d", [VB, P], i32)
        tabs = [nc.dram_tensor(f"tab{k}_d", [TILES * P, w], f32) for k, w in enumerate([WA, WA, WA, 128, 128, 64])]

        X = sb("X", [P, TILES, D])
        X1 = sb("X1", [P, TILES, D])
        TB = sb("TB", [P, TILES, 128])
        KF = sb("KF", [P, TILES, D])
        KS = sb("KS", [P, TILES, 3, D], bf16)
        ROOT = sb("ROOT", [P, TILES, D])
        ACC = sb("ACC", [P, TILES, WA])
        T1 = sb("T1", [P, TILES, D])
        T2 = sb("T2", [P, TILES, D])
        NV = sb("NV", [P, 8, TILES])
        XT = sb("XT", [D + 1, TILES * P])
        WAUG = [sb(f"WAUG{k}", [D + 1, w]) for k, w in enumerate([69, 69, 69, 256, 256, 128])]
        WIN = sb("WIN", [D, 8, D])
        WTT = sb("WTT", [D, 6, D])
        W2T = sb("W2T", [D, D])
        AV = sb("AV", [D, 10])
        WE = sb("WE", [2, 2 + 1 + D])
        WES = sb("WES", [P, 2 + 2 * D])
        BIASR = sb("BIASR", [D + 1, 2, D])
        ROW = sb("ROW", [P, 7, D])
        UV = sb("UV", [P, 4, D])
        MU = sb("MU", [P, 2, D])
        MK = sb("MK", [P, 4, D])
        MK2 = sb("MK2", [P, 4, D])
        MK3 = sb("MK3", [P, 4, D])
        CONST = sb("CONST", [P, 1])
        BN = sb("BN", [P, 4, D])
        ident = sb("ident", [P, P])
        identb = sb("identb", [P, P], bf16)
        ones = sb("ones", [P, P])
        lastones = sb("lastones", [P, P])
        iotab = sb("iotab", [P, P], bf16)
        iotaf = sb("iotaf", [P, P])
        iopf = sb("iopf", [P, 1])
        FLD = sb("FLD", [P, NF, VP])
        TVR = sb("TVR", [1, VP], i32)
        CNT = sb("CNT", [P, 2, TILES])

        prep = ExitStack()

        def tmp(name, shape, dt=f32):
            return prep.enter_context(nc.sbuf_tensor(name, shape, dt))

        ioi = tmp("ioi", [P, P], i32)
        iop = tmp("iop", [P, 1], i32)
        DST_I = tmp("DST_I", [125, E // 125], i32)
        DST_F = tmp("DST_F", [125, E // 125])
        DST_J = tmp("DST_J", [125, E // 125])
        START = tmp("START", [P, 32])
        VT_F = tmp("VT_F", [P, 32])
        VT_I = tmp("VT_I", [P, 32], i32)
        VIO_I = tmp("VIO_I", [P, VB], i32)
        VIO = tmp("VIO", [P, VB])
        CMP = tmp("CMP", [P, VB, TILES - 1])
        TVP = tmp("TVP", [P, VB])
        TVPI = tmp("TVPI", [P, VB], i32)
        CVF = tmp("CVF", [P, VB])
        CVI = tmp("CVI", [P, VB], u32)
        PADR = tmp("PADR", [1, REC + 1], i32)
        REC_S = tmp("REC_S", [P, VB, REC], i32)
        VF = tmp("VF", [P, NF, VB, P])
        prep.close()

        IDX = sb("IDX", [P, U, Q], u32)
        RS4 = sb("RS4", [P, U, Q])
        G = sb("G", [P, U, Q, 128])
        OT = sb("OT", [P, U, Q * P], bf16)
        OE = sb("OE", [P, U, Q * P], bf16)
        OHD = sb("OHD", [P, 2, Q, P], bf16)
        OHS = sb("OHS", [P, 2, Q, P], bf16)
        HI = sb("HI", [P, 2, 2, Q, 32], bf16)
        OEF = sb("OEF", [P, 2, Q * P])
        SC = sb("SC", [P, 2, Q])
        SCT = sb("SCT", [P, 2, Q])
        MS = sb("MS", [67, 2, Q * P])
        R = sb("R", [67, 2, Q * P + 1])
        QT = sb("QT", [67, Q * P])
        UT = sb("UT", [67, 2, Q * P])
        NT = sb("NT", [67, 2, Q * P])
        RU = sb("RU", [67, Q * P])
        FW = sb("FW", [67, 2, 2, Q * P])
        WH = sb("WH", [67, Q * P])
        SO = sb("SO", [67, 2, Q * P])
        XS = sb("XS", [P, 2, Q, WA])
        PR = sb("PR", [P, 2, Q, D])
        SG = sb("SG", [P, 2, Q, D])
        MSG = sb("MSG", [P, 2, Q, D])
        HT = sb("HT", [D, 2, Q * P])

        B = [pb(f"bank{k}", [P, 512]) for k in range(7)]
        BT = pb("bankT", [P, 1024], bf16)

        block = ctx.enter_context(nc.Block())
        AP_ATT = ["L0a", "L0b", "L1"]
        x_t = A["x"]

        def tiled(ap):
            return ap.rearrange("(t p) w -> p t w", p=P)

        KINDS = ["A", "A", "A", "B", "B", "C"]
        NA_BEFORE = [0, 1, 2, 3, 3, 3]
        ROUNDS = NG // U

        def grp(n, g, per=1, a=0):
            return g.times(per, n * NG * per + per + a * per)

        def ring(n, g, per):
            return g.rounds(per, n * ROUNDS * per + per)

        ENDP = [0, 1, 2, None, None, 3]
        GATP = [None, None, None, 0, 1, None]
        PREP = [None, None, None, 0, 1, 2]

        def rows_free(n, g, a):
            return {"A": ("rows_on_pe", grp(NA_BEFORE[n], g, a=a)), "B": ("msg_ready", grp(GATP[n] or 0, g, a=a)),
                    "C": ("hT_on_pe", grp(0, g, a=a))}[KINDS[n]]

        def spread_free(n, g, a):
            return ("spread_read", grp(NA_BEFORE[n], g, a=a)) if KINDS[n] == "A" else ("pre_ready", grp(PREP[n], g, a=a))

        def pool_pass(e, n):
            w = [WA, WA, WA, 128, 128, 64][n]
            e.wait_ge(sem("table_written"), 16 * (n + 1))

            def gather(g):
                gate(e, "pool", sem("idx_ready"), grp(n, g))
                for q in range(Q):
                    e.indirect_dma_start(
                        out=G[:, g.slot, q, 0:w], out_offset=None, in_=tabs[n][:, :],
                        in_offset=bass.IndirectOffsetOnAxis(ap=IDX[:, g.slot, q:q + 1], axis=0),
                    ).then_inc(sem(f"rows_in{g.slot}"), 16)

            steps(e, [(0, gather)])

        def sp_pass(e, n):
            ends = KINDS[n] != "B"

            def load(g):
                gate(e, "sp", sem("ohT_used"), grp(n, g, a=-U))
                e.dma_start(OT[:, g.slot, :].unsqueeze(1),
                            ohT_d[bass.ds(g.times(1), 1), :, :].rearrange("g p f -> p g f")).then_inc(sem(f"ohT_in{g.slot}"), 16)
                if ends:
                    gate(e, "sp", sem("ohF_ready"), grp(n, g, a=-U))
                    e.dma_start(OE[:, g.slot, :].unsqueeze(1),
                                ohE_d[bass.ds(g.times(1), 1), :, :].rearrange("g p f -> p g f")).then_inc(sem(f"ohE_in{g.slot}"), 16)

            steps(e, [(0, load)])

        def tile_of(e, g, q):
            return e.value_load(TVR[0:1, bass.ds(g.times(Q, q), 1)], min_val=0, max_val=TILES - 1)

        def pe_spread(e, n, w, bank):
            def fn(g):
                gate(e, "pe", sem(f"ohT_in{g.slot}"), ring(n, g, 16))
                free, val = spread_free(n, g, -1)
                gate(e, "pe", sem(free), val)
                for q in range(Q):
                    t = tile_of(e, g, q)
                    for k in range(3):
                        mm = e.matmul(bank[:, q * w:q * w + w], OT[:, g.slot, q * P:(q + 1) * P],
                                      KS[:, bass.ds(t, 1), k, 0:w].rearrange("p a w -> p (a w)"),
                                      start=(k == 0), stop=(k == 2))
                mm.then_inc(sem("ohT_used"), 1)
            return fn

        def pe_pick(e, n, w, src, ready, k):
            def fn(g):
                gate(e, "pe", sem(ready), grp(k, g))
                gate(e, "pe", sem("ohF_ready"), grp(n, g))
                gate(e, "pe", sem("sums_added"), grp(n, g, a=-1, per=Q))
                for q in range(Q):
                    mm = e.matmul(B[6][:, q * w:q * w + w], OEF[:, g.par(2), q * P:(q + 1) * P], src(g, q),
                                  start=True, stop=True)
                mm.then_inc(sem("picked"), 1)
            return fn

        def pe_pass(e, n):
            kind = KINDS[n]
            e.wait_ge(sem("parts_ready"), n + 1)
            m = ENDP[n]

            if kind == "A":
                def score_rows(g):
                    gate(e, "pe", sem("score_ready"), grp(m, g))
                    gate(e, "pe", sem("masks_ready"), grp(m, g))
                    gate(e, "pe", sem("min_done"), grp(m, g, a=-1))
                    gate(e, "pe", sem("wh_done"), grp(NA_BEFORE[n], g, a=-2))
                    gate(e, "pe", sem("mask_copied"), grp(m, g, a=-1))
                    for q in range(Q):
                        e.matmul(B[1][0:67, q * P:(q + 1) * P], SC[:, g.par(2), q:q + 1].to_broadcast([P, 67]),
                                 ident[:, :], start=True, stop=True)
                    for q in range(Q):
                        e.matmul(B[2][0:67, q * P:(q + 1) * P], RS4[:, g.slot, q:q + 1].to_broadcast([P, 67]),
                                 ident[:, :], start=True, stop=True)
                    for q in range(Q):
                        mm = e.transpose(B[3 + g.par(2)][0:67, q * P:(q + 1) * P], G[:, g.slot, q, 0:67], ident[:, :])
                    mm.then_inc(sem("rows_on_pe"), 1)

                def back(g):
                    gate(e, "pe", sem("scanned"), grp(m, g))
                    gate(e, "pe", sem("ends_copied"), grp(m, g, a=-1))
                    for q in range(Q):
                        e.transpose(B[5][:, q * WA:q * WA + 67], SO[:, g.par(2), q * P:(q + 1) * P], ident[0:67, 0:67])
                        mm = e.transpose(B[5][:, q * WA + 67:q * WA + 68], R[0:1, g.par(2), 1 + q * P:1 + (q + 1) * P],
                                         ident[0:1, 0:1])
                    mm.then_inc(sem("back_on_pe"), 1)

                steps(e, [(1, score_rows), (0, pe_spread(e, n, 1, B[0])), (3, back),
                          (4, pe_pick(e, n, WA, lambda g, q: XS[:, g.par(2), q, :], "ends_copied", m))])
            elif kind == "B":
                steps(e, [(0, pe_spread(e, n, D, B[0])),
                          (2, pe_pick(e, n, D, lambda g, q: MSG[:, g.par(2), q, :], "msg_ready", GATP[n]))])
            else:
                def turn(g):
                    gate(e, "pe", sem("hidden_ready"), grp(0, g))
                    gate(e, "pe", sem("masks_ready"), grp(m, g))
                    gate(e, "pe", sem("hT_copied"), grp(0, g, a=-1))
                    gate(e, "pe", sem("mask_copied"), grp(m, g, a=-1))
                    for q in range(Q):
                        e.matmul(B[2][0:D, q * P:(q + 1) * P], RS4[:, g.slot, q:q + 1].to_broadcast([P, D]),
                                 ident[:, :], start=True, stop=True)
                    for q in range(Q):
                        mm = e.transpose(B[3][0:D, q * P:(q + 1) * P], SG[:, g.par(2), q, :], ident[:, :])
                    mm.then_inc(sem("hT_on_pe"), 1)

                def mlp(g):
                    gate(e, "pe", sem("hT_copied"), grp(0, g))
                    gate(e, "pe", sem("scanned"), grp(m, g, a=-1))
                    e.matmul(B[1][0:D, :], W2T[:, :], HT[:, g.par(2), :], start=True, stop=True).then_inc(sem("mlp_on_pe"), 1)

                def back(g):
                    gate(e, "pe", sem("scanned"), grp(m, g))
                    gate(e, "pe", sem("ends_copied"), grp(m, g, a=-1))
                    for q in range(Q):
                        mm = e.transpose(B[5][:, q * D:(q + 1) * D], SO[0:D, g.par(2), q * P:(q + 1) * P], ident[0:D, 0:D])
                    mm.then_inc(sem("back_on_pe"), 1)

                steps(e, [(2, mlp), (1, turn), (0, pe_spread(e, n, D, B[0])), (3, back),
                          (4, pe_pick(e, n, D, lambda g, q: XS[:, g.par(2), q, 0:D], "ends_copied", m))])

        def act_indices(e, n):
            def fn(g):
                free, val = rows_free(n, g, -U)
                gate(e, "act", sem(free), val)
                e.activation(IDX[:, g.slot, :], FLD[:, F_SRC, bass.ds(g.times(Q), Q)], ACT.Copy).then_inc(sem("idx_ready"), 1)
                if ENDP[n] is not None:
                    e.activation(RS4[:, g.slot, :], FLD[:, F_RST, bass.ds(g.times(Q), Q)], ACT.Copy).then_inc(sem("masks_ready"), 1)
            return fn

        def act_ohf(e, n):
            def fn(g):
                gate(e, "act", sem(f"ohE_in{g.slot}"), ring(ENDP[n], g, 16))
                gate(e, "act", sem("picked"), grp(n, g, a=-2))
                e.activation(OEF[:, g.par(2), :], OE[:, g.slot, :], ACT.Copy).then_inc(sem("ohF_ready"), 1)
            return fn

        def act_pass(e, n):
            kind, m = KINDS[n], ENDP[n]
            if kind == "A":
                def mask(g):
                    gate(e, "act", sem("rows_on_pe"), grp(NA_BEFORE[n], g))
                    gate(e, "act", sem("scan_max_done"), grp(m, g, a=-2))
                    e.activation(MS[:, g.par(2), :], B[2][0:67, :], ACT.Copy).then_inc(sem("mask_copied"), 1)

                def weights(g):
                    gate(e, "act", sem("min_done"), grp(m, g))
                    gate(e, "act", sem("scanned"), grp(m, g, a=-2))
                    gate(e, "act", sem("weighted"), grp(NA_BEFORE[n], g, a=-2))
                    e.activation(RU[:, :], UT[:, g.par(2), :], ACT.Relu).then_inc(sem("relu_done"), 1)
                    e.activation(FW[:, g.par(2), 0, :], NT[:, g.par(2), :], ACT.Exp)
                    gate(e, "act", sem("relu_done"), grp(NA_BEFORE[n], g))
                    e.activation(FW[:, g.par(2), 1, :], RU[:, :], ACT.Exp, scale=-1.0).then_inc(sem("weighted"), 1)

                def ends(g):
                    gate(e, "act", sem("back_on_pe"), grp(m, g))
                    gate(e, "act", sem("picked"), grp(n, g, a=-2))
                    e.activation(XS[:, g.par(2), :, :].rearrange("p a w -> p (a w)"), B[5][:, 0:Q * WA], ACT.Copy)\
                        .then_inc(sem("ends_copied"), 1)

                steps(e, [(0, act_indices(e, n)), (4, mask), (4, weights), (6, ends), (6, act_ohf(e, n))])
            elif kind == "B":
                def gates(g):
                    gate(e, "act", sem("pre_ready"), grp(PREP[n], g))
                    gate(e, "act", sem("msg_ready"), grp(GATP[n], g, a=-2))
                    e.activation(SG[:, g.par(2), :, :], PR[:, g.par(2), :, :], ACT.Sigmoid).then_inc(sem("gate_ready"), 1)

                steps(e, [(0, act_indices(e, n)), (3, gates)])
            else:
                def hidden(g):
                    gate(e, "act", sem("pre_ready"), grp(2, g))
                    gate(e, "act", sem("hT_on_pe"), grp(0, g, a=-2))
                    e.activation(SG[:, g.par(2), :, :], PR[:, g.par(2), :, :], ACT.Relu).then_inc(sem("hidden_ready"), 1)

                def hT(g):
                    gate(e, "act", sem("hT_on_pe"), grp(0, g))
                    gate(e, "act", sem("mlp_on_pe"), grp(0, g, a=-2))
                    gate(e, "act", sem("scanned"), grp(m, g, a=-2))
                    e.activation(MS[0:D, g.par(2), :], B[2][0:D, :], ACT.Copy).then_inc(sem("mask_copied"), 1)
                    e.activation(HT[:, g.par(2), :], B[3][0:D, :], ACT.Copy).then_inc(sem("hT_copied"), 1)

                def ends(g):
                    gate(e, "act", sem("back_on_pe"), grp(m, g))
                    gate(e, "act", sem("picked"), grp(n, g, a=-2))
                    e.activation(XS[:, g.par(2), :, 0:D], B[5][:, 0:Q * D].rearrange("p (a w) -> p a w", a=Q), ACT.Copy)\
                        .then_inc(sem("ends_copied"), 1)

                steps(e, [(0, act_indices(e, n)), (3, hidden), (3, hT), (5, ends), (5, act_ohf(e, n))])

        def dve_add(e, n, w, m):
            def fn(g):
                gate(e, "dve", sem("picked"), grp(n, g))
                for q in range(Q):
                    t = tile_of(e, g, q)
                    gate(e, "dve", sem("sums_added"), g.times(Q, n * NG * Q + q))
                    e.tensor_tensor(ACC[:, bass.ds(t, 1), 0:w], ACC[:, bass.ds(t, 1), 0:w],
                                    B[6][:, q * w:q * w + w].unsqueeze(1), ALU.add).then_inc(sem("sums_added"), 1)
            return fn

        def dve_pass(e, n):
            kind, m = KINDS[n], ENDP[n]
            if kind == "A":
                slope = [0.2, 0.2, 0.01][n]

                def score(g):
                    gate(e, "dve", sem(f"rows_in{g.slot}"), ring(n, g, 64))
                    gate(e, "dve", sem("ohT_used"), grp(n, g))
                    e.tensor_copy(G[:, g.slot, :, 65:67],
                                  FLD[:, F_A0:F_A1 + 1, bass.ds(g.times(Q), Q)].rearrange("p f v -> p v f"))
                    e.tensor_tensor(SCT[:, 0, :], B[0][:, 0:Q], G[:, g.slot, :, 67:68].rearrange("p q o -> p (q o)"),
                                    ALU.add).then_inc(sem("spread_read"), 1)
                    gate(e, "dve", sem("spread_read"), grp(NA_BEFORE[n], g))
                    e.tensor_tensor(SCT[:, 1, :], SCT[:, 0, :], FLD[:, F_XW, bass.ds(g.times(Q), Q)], ALU.add)\
                        .then_inc(sem("raw_score"), 1)
                    gate(e, "dve", sem("raw_score"), grp(NA_BEFORE[n], g))
                    gate(e, "dve", sem("rows_on_pe"), grp(NA_BEFORE[n], g, a=-2))
                    e.scalar_tensor_tensor(out=SC[:, g.par(2), :], in0=SCT[:, 1, :], scalar=slope, in1=SCT[:, 1, :],
                                           op0=ALU.mult, op1=ALU.max).then_inc(sem("score_ready"), 1)

                def running_max(g):
                    p, o = g.par(2), 1 - g.par(2)
                    gate(e, "dve", sem("rows_on_pe"), grp(NA_BEFORE[n], g))
                    gate(e, "dve", sem("mask_copied"), grp(m, g))
                    gate(e, "dve", sem("back_on_pe"), grp(m, g, a=-2))
                    if g.i is None and g.c == 0:
                        init = -BIG
                        e.memset(R[:, 0, 0:1], -BIG).then_inc(sem("scan_carry"), 1)
                    else:
                        init = R[:, o, Q * P:Q * P + 1]
                        gate(e, "dve", sem("scan_max_done"), grp(m, g, a=-1))
                        e.tensor_copy(R[:, p, 0:1], R[:, o, Q * P:Q * P + 1]).then_inc(sem("scan_carry"), 1)
                    e.tensor_tensor_scan(R[:, p, 1:Q * P + 1], MS[:, p, :], B[1][0:67, :], init, ALU.add, ALU.max)\
                        .then_inc(sem("scan_max_done"), 1)
                    gate(e, "dve", sem("scan_max_done"), grp(m, g))
                    gate(e, "dve", sem("scan_carry"), grp(NA_BEFORE[n], g))
                    e.tensor_tensor(QT[:, :], B[2][0:67, :], R[:, p, 0:Q * P], ALU.add).then_inc(sem("q_done"), 1)
                    gate(e, "dve", sem("q_done"), grp(NA_BEFORE[n], g))
                    gate(e, "dve", sem("weighted"), grp(NA_BEFORE[n], g, a=-2))
                    e.tensor_tensor(UT[:, p, :], QT[:, :], B[1][0:67, :], ALU.subtract).then_inc(sem("u_done"), 1)
                    gate(e, "dve", sem("u_done"), grp(NA_BEFORE[n], g))
                    e.tensor_scalar(NT[:, p, :], UT[:, p, :], 0.0, None, ALU.min).then_inc(sem("min_done"), 1)

                def running_sum(g):
                    p, o = g.par(2), 1 - g.par(2)
                    gate(e, "dve", sem("weighted"), grp(NA_BEFORE[n], g))
                    e.tensor_tensor(WH[:, :], FW[:, p, 1, :], B[3 + p][0:67, :], ALU.mult).then_inc(sem("wh_done"), 1)
                    gate(e, "dve", sem("wh_done"), grp(NA_BEFORE[n], g))
                    gate(e, "dve", sem("back_on_pe"), grp(m, g, a=-2))
                    if g.i is None and g.c == 0:
                        init = 0.0
                    else:
                        init = SO[:, o, Q * P - 1:Q * P]
                        gate(e, "dve", sem("scanned"), grp(m, g, a=-1))
                    e.tensor_tensor_scan(SO[:, p, :], FW[:, p, 0, :], WH[:, :], init, ALU.mult, ALU.add)\
                        .then_inc(sem("scanned"), 1)

                steps(e, [(2, running_sum), (1, running_max), (4, dve_add(e, n, WA, m)), (0, score)])
            else:
                def pre(g):
                    gate(e, "dve", sem(f"rows_in{g.slot}"), ring(n, g, 64))
                    gate(e, "dve", sem("ohT_used"), grp(n, g))
                    if kind == "B":
                        gate(e, "dve", sem("gate_ready"), grp(GATP[n], g, a=-2))
                    else:
                        gate(e, "dve", sem("hidden_ready"), grp(0, g, a=-2))
                    e.tensor_tensor(PR[:, g.par(2), :, :], B[0][:, 0:Q * D].rearrange("p (q d) -> p q d", q=Q),
                                    G[:, g.slot, :, 0:D], ALU.add).then_inc(sem("pre_ready"), 1)

                if kind == "B":
                    def msg(g):
                        gate(e, "dve", sem("picked"), grp(n, g, a=-2))
                        for q in range(Q):
                            oh = e.tensor_scalar(OEF[:, g.par(2), q * P:(q + 1) * P], iotab[:, :],
                                                 FLD[:, F_DREL, bass.ds(g.times(Q, q), 1)], None, ALU.is_equal)
                        oh.then_inc(sem("ohF_ready"), 1)
                        gate(e, "dve", sem("gate_ready"), grp(GATP[n], g))
                        e.tensor_tensor(MSG[:, g.par(2), :, :], SG[:, g.par(2), :, :], G[:, g.slot, :, D:2 * D],
                                        ALU.mult).then_inc(sem("msg_ready"), 1)
                    steps(e, [(0, pre), (1, msg), (2, dve_add(e, n, D, None))])
                else:
                    def scan(g):
                        p, o = g.par(2), 1 - g.par(2)
                        gate(e, "dve", sem("mlp_on_pe"), grp(0, g))
                        gate(e, "dve", sem("mask_copied"), grp(m, g))
                        gate(e, "dve", sem("back_on_pe"), grp(m, g, a=-2))
                        if g.i is None and g.c == 0:
                            init = -BIG
                        else:
                            init = SO[0:D, o, Q * P - 1:Q * P]
                            gate(e, "dve", sem("scanned"), grp(m, g, a=-1))
                        e.tensor_tensor_scan(SO[0:D, p, :], MS[0:D, p, :], B[1][0:D, :], init, ALU.add, ALU.max)\
                            .then_inc(sem("scanned"), 1)

                    steps(e, [(2, scan), (4, dve_add(e, n, D, m)), (0, pre)])

        def dve_index(e):
            def build_oh(g):
                gate(e, "dve", sem("idx_on_pe"), g.times(1, 1 - 2))
                gate(e, "dve", sem(f"ohE_out{g.slot}"), g.rounds(16))
                for q in range(Q):
                    v = bass.ds(g.times(Q, q), 1)
                    e.tensor_scalar(OHD[:, g.par(2), q, :], iotab[:, :], FLD[:, F_DREL, v], None, ALU.is_equal)
                    e.tensor_scalar(OHS[:, g.par(2), q, :], iotab[:, :], FLD[:, F_SLO, v], None, ALU.is_equal)
                    e.tensor_scalar(HI[:, g.par(2), 0, q, :], iotab[:, 0:32], FLD[:, F_SHI, v], None, ALU.is_equal)
                    e.tensor_scalar(HI[:, g.par(2), 1, q, :], iotab[:, 0:32], FLD[:, F_DHI, v], None, ALU.is_equal)
                    oh = e.tensor_scalar(OE[:, g.slot, q * P:(q + 1) * P], iotab[:, :], FLD[:, F_EREL, v], None, ALU.is_equal)
                oh.then_inc(sem("oh_built"), 1)

            steps(e, [(0, build_oh)])
            e.wait_ge(sem("idx_on_pe"), NG)
            e.tensor_copy(CNT[:, 0, :], B[0][:, 0:TILES])
            e.tensor_copy(CNT[:, 1, :], B[1][:, 0:TILES]).then_inc(sem("degrees_done"), 1)

        def pe_index(e):
            def count(g):
                gate(e, "pe", sem("oh_built"), g.times(1, 1))
                gate(e, "pe", sem("ohT_copied"), g.times(1, 0))
                first, last = g.i is None and g.c == 0, g.i is None and g.c == NG - 1
                for q in range(Q):
                    e.transpose(BT[:, q * P:(q + 1) * P], OHD[:, g.par(2), q, :], identb[:, :])
                for q in range(Q):
                    e.matmul(B[0][:, 0:32], OHS[:, g.par(2), q, :], HI[:, g.par(2), 0, q, :],
                             start=(first and q == 0), stop=(last and q == Q - 1))
                    mm = e.matmul(B[1][:, 0:32], OHD[:, g.par(2), q, :], HI[:, g.par(2), 1, q, :],
                                  start=(first and q == 0), stop=(last and q == Q - 1))
                mm.then_inc(sem("idx_on_pe"), 1)

            steps(e, [(1, count)])

        def act_index(e):
            def evac(g):
                gate(e, "act", sem("idx_on_pe"), g.times(1, 1))
                gate(e, "act", sem(f"ohT_out{g.slot}"), g.rounds(16))
                e.activation(OT[:, g.slot, :], BT[:, 0:Q * P], ACT.Copy).then_inc(sem("ohT_copied"), 1)

            steps(e, [(0, evac)])

        def sp_index(e):
            def store(g):
                gate(e, "sp", sem("oh_built"), g.times(1, 1))
                e.dma_start(ohE_d[bass.ds(g.times(1), 1), :, :].rearrange("g p f -> p g f"),
                            OE[:, g.slot, :].unsqueeze(1)).then_inc(sem(f"ohE_out{g.slot}"), 16)
                gate(e, "sp", sem("ohT_copied"), g.times(1, 1))
                e.dma_start(ohT_d[bass.ds(g.times(1), 1), :, :].rearrange("g p f -> p g f"),
                            OT[:, g.slot, :].unsqueeze(1)).then_inc(sem(f"ohT_out{g.slot}"), 16)

            steps(e, [(0, store)])
            for k in range(U):
                e.wait_ge(sem(f"ohE_out{k}"), 16 * ROUNDS)
                e.wait_ge(sem(f"ohT_out{k}"), 16 * ROUNDS)

        FULL = CHUNKS - 1

        def sp_prep(e):
            dst = A["dst"]
            x_in = sem("x_in")
            e.dma_start(DST_I[:, :], dst.rearrange("(p i) -> p i", p=125)).then_inc(sem("dst_in"), 16)
            e.wait_ge(sem("cleared"), 1)
            e.dma_start(X[:, 0:TILES - 1, :], x_t[0:(TILES - 1) * P, :].rearrange("(t p) w -> p t w", p=P)).then_inc(x_in, 16)
            e.dma_start(X[0:LASTN, TILES - 1, :], x_t[(TILES - 1) * P:N, :]).then_inc(x_in, 16)
            w_in = sem("weights_in")
            n = [0]

            def load(o, i):
                e.dma_start(o, i).then_inc(w_in, 16)
                n[0] += 16

            for c, nm in enumerate(["L0_gnn_W1", "L0_gnn_W2", "L1_gnn_W_fc", "L1_gnn_W_m1", "L1_gnn_W_m2"]):
                load(WIN[:, c, :], A[nm])
            load(WIN[:, 5:7, :].rearrange("o c d -> o (c d)"), A["L3_gnn_W1"])
            load(WIN[:, 7, :], A["L3_gnn_W2"])
            for c, nm in enumerate(["L0_gnn_a_src1", "L0_gnn_a_dst1", "L0_gnn_a_src2", "L0_gnn_a_dst2"]):
                load(AV[:, c:c + 1], A[nm].unsqueeze(1))
            wat = A["L1_gnn_W_attn"]
            for c in range(6):
                load(AV[:, 4 + c:5 + c], wat[0:1, c * D:(c + 1) * D].rearrange("a o -> o a"))
            load(WE[:, 0:2], A["L1_gnn_W_edge"])
            load(WE[:, 2:3], wat[0:1, 6 * D:6 * D + 2].rearrange("a o -> o a"))
            load(WE[:, 3:3 + D], A["L1_gnn_W_e2n"].rearrange("o j -> j o"))
            for l in range(2):
                for c, nm in enumerate("qvks"):
                    load(WAUG[3 + l][0:D, c * D:(c + 1) * D], A["L2_gnn_W" + nm][l, :, :])
                    load(WAUG[3 + l][D:D + 1, c * D:(c + 1) * D], A["L2_gnn_b" + nm][l:l + 1, :])
                load(BIASR[D:D + 1, l, :], A["L2_gnn_bias"][l:l + 1, :])
            load(WAUG[5][D:D + 1, D:2 * D], A["L3_gnn_b1"].unsqueeze(0))
            for c, ap in enumerate([A["L0_gnn_b1"].unsqueeze(0), A["L0_gnn_b2"].unsqueeze(0), A["L2_gnn_gamma"][0:1, :],
                                    A["L2_gnn_gamma"][1:2, :], A["L2_gnn_beta"][0:1, :], A["L2_gnn_beta"][1:2, :],
                                    A["L3_gnn_b2"].unsqueeze(0)]):
                load(ROW[:, c, :], ap.to_broadcast([P, D]))
            assert n[0] == 16 * WEIGHT_LOADS, n[0] // 16

        WEIGHT_LOADS = 5 + 2 + 4 + 6 + 3 + 2 * 9 + 1 + 7

        def act_prep(e):
            src, dst, attr = A["src"], A["dst"], A["edge_attr_2"]
            done = sem("record_in")
            n = [0]

            def put(o, i):
                e.dma_start(o, i).then_inc(done, 16)
                n[0] += 16

            W0 = FULL * P
            dv = dst[0:W0].rearrange("(c k) -> c k", k=P)
            put(rec_d[0:FULL, 0:P], src[0:W0].rearrange("(c k) -> c k", k=P))
            put(rec_d[0:FULL, P:2 * P], dv)
            put(rec_d[0:FULL, 2 * P + 1:3 * P], dv[:, 0:P - 1])
            put(rec_d[1:FULL + 1, 2 * P:2 * P + 1], dv[:, P - 1:P])
            put(rec_d[0:FULL, 3 * P:4 * P - 1], dv[:, 1:P])
            put(rec_d[0:FULL - 1, 4 * P - 1:4 * P], dv[1:FULL, 0:1])
            put(rec_d[FULL - 1:FULL, 4 * P - 1:4 * P], dst[W0:W0 + 1].unsqueeze(0))
            put(rec_d[0:FULL, 4 * P:6 * P], attr[0:W0, :].bitcast(i32).rearrange("(c k) a -> c (k a)", k=P))
            put(rec_d[FULL:FULL + 1, 0:LASTE], src[W0:E].unsqueeze(0))
            put(rec_d[FULL:FULL + 1, P:P + LASTE], dst[W0:E].unsqueeze(0))
            put(rec_d[FULL:FULL + 1, 2 * P + 1:2 * P + LASTE], dst[W0:E - 1].unsqueeze(0))
            put(rec_d[FULL:FULL + 1, 3 * P:3 * P + LASTE - 1], dst[W0 + 1:E].unsqueeze(0))
            put(rec_d[FULL:FULL + 1, 4 * P:4 * P + 2 * LASTE], attr[W0:E, :].bitcast(i32).rearrange("k a -> (k a)").unsqueeze(0))
            e.wait_ge(sem("pad_set"), 1)
            put(rec_d[0:1, 2 * P:2 * P + 1], PADR[:, REC:REC + 1])
            put(rec_d[FULL:FULL + 1, LASTE:P], PADR[:, LASTE:P])
            put(rec_d[FULL:FULL + 1, P + LASTE:2 * P], PADR[:, P + LASTE:2 * P])
            put(rec_d[FULL:FULL + 1, 2 * P + LASTE:3 * P], PADR[:, 2 * P + LASTE:3 * P])
            put(rec_d[FULL:FULL + 1, 3 * P + LASTE - 1:4 * P], PADR[:, 3 * P + LASTE - 1:4 * P])
            put(rec_d[FULL:FULL + 1, 4 * P + 2 * LASTE:6 * P], PADR[:, 4 * P + 2 * LASTE:6 * P])
            put(rec_d[FULL + 1:FULL + 2, :], PADR[:, 0:REC])
            assert n[0] == 16 * RECORD_PUTS, n[0] // 16
            e.wait_ge(sem("walk_done"), 1)
            e.dma_start(tv_d[:, :].rearrange("k p -> p k"), TVPI[:, :]).then_inc(sem("walk_out"), 16)
            e.wait_ge(sem("walk_out"), 16)
            e.dma_start(TVR[:, :].rearrange("o (k p) -> o k p", p=P), tv_d[:, :].unsqueeze(0)).then_inc(sem("walk_in"), 16)

        RECORD_PUTS = 20

        def pool_prep(e):
            e.memset(PADR[:, 0:P], 0)
            e.memset(PADR[:, P:4 * P], 9999)
            e.memset(PADR[:, 4 * P:6 * P], 0)
            e.memset(PADR[:, REC:REC + 1], -1).then_inc(sem("pad_set"), 1)
            e.iota(ioi[:, :], [[1, P]], base=0, channel_multiplier=0)
            e.iota(iop[:, :], [[0, 1]], base=0, channel_multiplier=1)
            e.iota(VIO_I[:, :], [[P, VB]], base=0, channel_multiplier=1).then_inc(sem("iota_done"), 1)
            e.wait_ge(sem("record_in"), 16 * RECORD_PUTS)
            e.wait_ge(sem("walk_done"), 1)
            for k in range(VB):
                e.indirect_dma_start(out=REC_S[:, k, :], out_offset=None, in_=rec_d[:, :],
                                     in_offset=bass.IndirectOffsetOnAxis(ap=CVI[:, k:k + 1], axis=0)).then_inc(sem("records_in"), 16)

        def dve_prep(e, v):
            v(e.memset(X[:, TILES - 1, :], 0.0))
            e.memset(XT[D:D + 1, :], 1.0)
            e.memset(ones[:, :], 1.0)
            e.memset(FLD[:, F_XW, :], 0.0)
            for k in range(3):
                e.memset(WAUG[k][:, 64:69], 0.0)
                e.memset(WAUG[k][D:D + 1, 0:D], 0.0)
            e.memset(WAUG[5][D:D + 1, 0:D], 0.0)
            e.memset(START[:, 0:32], 0.0).then_inc(sem("cleared"), 1)
            e.wait_ge(sem("cleared"), 1)
            for k in range(3):
                e.memset(WAUG[k][D:D + 1, 64:65], 1.0)
            e.wait_ge(sem("iota_done"), 1)
            e.tensor_copy(iotab[:, :], ioi[:, :])
            e.tensor_copy(iotaf[:, :], ioi[:, :])
            e.tensor_copy(VIO[:, :], VIO_I[:, :])
            v(e.tensor_copy(iopf[:, :], iop[:, :]))
            e.tensor_scalar(identb[:, :], iotab[:, :], iopf[:, :], None, ALU.is_equal)
            v(e.tensor_scalar(ident[:, :], iotaf[:, :], iopf[:, :], None, ALU.is_equal))
            v(e.tensor_scalar(lastones[:, :], ones[:, :], iopf[:, :], float(LASTN), ALU.mult, ALU.mult))
            v(e.tensor_scalar(lastones[:, :], lastones[:, :], float(LASTN * LASTN), None, ALU.is_lt))
            e.sem_inc(sem("constants_done"), 1)
            e.wait_ge(sem("dst_in"), 16)
            v(e.tensor_copy(DST_F[:, :], DST_I[:, :]))
            for t in range(1, TILES):
                v(e.tensor_scalar(DST_J[:, :], DST_F[:, :], float(t * P), 0.0, ALU.is_lt, ALU.add,
                                  accum_out=START[0:125, t:t + 1]))
            e.sem_inc(sem("starts_counted"), 1)
            e.wait_ge(sem("starts_summed"), 1)
            v(e.tensor_scalar(VT_I[:, :], B[0][:, 0:32], -(P / 2 - 0.5), 1.0 / P, ALU.add, ALU.mult))
            v(e.tensor_copy(VT_F[:, :], VT_I[:, :]))
            v(e.tensor_scalar(VT_F[:, :], VT_F[:, :], float(CHUNKS - 1), None, ALU.min))
            v(e.tensor_tensor(VT_F[:, :], VT_F[:, :], iotaf[:, 0:32], ALU.add))
            v(e.tensor_tensor(CMP[:, :, :], VIO[:, :].unsqueeze(2).to_broadcast([P, VB, TILES - 1]),
                              VT_F[:, 1:TILES].unsqueeze(1).to_broadcast([P, VB, TILES - 1]), ALU.is_ge))
            v(e.tensor_reduce(TVP[:, :], CMP[:, :, :], AX.X, ALU.add))
            v(e.tensor_tensor(CVF[:, :], VIO[:, :], TVP[:, :], ALU.subtract))
            v(e.tensor_scalar(CVF[:, :], CVF[:, :], float(CHUNKS), None, ALU.min))
            e.tensor_copy(TVPI[:, :], TVP[:, :])
            v(e.tensor_copy(CVI[:, :], CVF[:, :]))
            e.sem_inc(sem("walk_done"), 1)
            e.wait_ge(sem("records_in"), 16 * VB)
            f = lambda k: VF[:, k, :, :]
            rec = lambda k: REC_S[:, :, k * P:(k + 1) * P]
            tv = TVP[:, :].unsqueeze(2).to_broadcast([P, VB, P])
            HII = REC_S[:, :, 2 * P:3 * P]
            e.tensor_copy(f(F_SRC), rec(0))
            e.tensor_copy(f(F_DREL), rec(1))
            e.tensor_copy(f(F_RST), rec(2))
            e.tensor_copy(f(F_EREL), rec(3))
            e.tensor_copy(f(F_A0), REC_S[:, :, 4 * P:6 * P].bitcast(f32).rearrange("p v (k a) -> p v k a", a=2)[:, :, :, 0])
            v(e.tensor_copy(f(F_A1), REC_S[:, :, 4 * P:6 * P].bitcast(f32).rearrange("p v (k a) -> p v k a", a=2)[:, :, :, 1]))
            e.tensor_tensor(f(F_RST), f(F_DREL), f(F_RST), ALU.not_equal)
            e.tensor_tensor(f(F_EREL), f(F_DREL), f(F_EREL), ALU.is_equal)
            v(e.tensor_scalar(HII, f(F_SRC), -(P / 2 - 0.5), 1.0 / P, ALU.add, ALU.mult))
            v(e.tensor_copy(f(F_SHI), HII))
            v(e.tensor_scalar(f(F_SLO), f(F_SHI), -float(P), None, ALU.mult))
            v(e.tensor_tensor(f(F_SLO), f(F_SLO), f(F_SRC), ALU.add))
            v(e.tensor_scalar(f(F_DHI), tv, -float(P), None, ALU.mult))
            v(e.tensor_tensor(f(F_DREL), f(F_DREL), f(F_DHI), ALU.add))
            v(e.scalar_tensor_tensor(out=f(F_EREL), in0=f(F_EREL), scalar=20000.0, in1=f(F_DREL), op0=ALU.mult, op1=ALU.add))
            v(e.tensor_scalar(f(F_RST), f(F_RST), -BIG, None, ALU.mult))
            v(e.tensor_scalar(f(F_XW), f(F_DREL), 0.0, None, ALU.is_lt))
            v(e.tensor_scalar(f(F_DHI), f(F_DREL), float(P), None, ALU.is_ge))
            v(e.tensor_tensor(f(F_XW), f(F_XW), f(F_DHI), ALU.add))
            v(e.scalar_tensor_tensor(out=f(F_SHI), in0=f(F_XW), scalar=1000.0, in1=f(F_SHI), op0=ALU.mult, op1=ALU.add))
            v(e.scalar_tensor_tensor(out=f(F_DHI), in0=f(F_XW), scalar=1000.0, in1=tv, op0=ALU.mult, op1=ALU.add))
            e.sem_inc(sem("fields_done"), 1)
            r = 0
            for fl in FIELDS:
                for b0 in range(0, VB, 4):
                    e.wait_ge(sem("fields_on_pe"), r + 1)
                    w = min(4, VB - b0) * P
                    e.tensor_copy(FLD[:, fl, b0 * P:b0 * P + w], B[r % 2][:, 0:w]).then_inc(sem("fields_copied"), 1)
                    r += 1
            e.wait_ge(sem("weights_in"), 16 * WEIGHT_LOADS)
            for l in range(2):
                e.tensor_tensor(WAUG[3 + l][D:D + 1, 3 * D:4 * D], WAUG[3 + l][D:D + 1, 3 * D:4 * D], BIASR[D:D + 1, l, :], ALU.add)
                e.tensor_copy(WAUG[l][0:D, 0:D], WIN[:, l, :])
            e.wait_ge(sem("weights_turned"), 1)
            e.tensor_copy(WTT[:, :, :].rearrange("p c d -> p (c d)"), B[4][0:D, 0:6 * D]).then_inc(sem("turned_copied"), 1)
            e.wait_ge(sem("turned_copied"), 1)
            e.tensor_copy(WAUG[2][0:D, 0:D], WTT[:, 2, :])
            e.tensor_copy(WAUG[5][0:D, 0:D], WTT[:, 4, :])
            e.tensor_tensor(WAUG[5][0:D, D:2 * D], WTT[:, 3, :], WTT[:, 4, :], ALU.subtract)
            e.tensor_copy(W2T[:, :], WTT[:, 5, :])
            e.wait_ge(sem("weights_folded"), 1)
            for l in range(3):
                e.tensor_copy(WAUG[l][0:D, 67:69], B[5][0:D, 2 * l:2 * l + 2])
            e.tensor_copy(WES[:, :], B[6][:, 0:2 + 2 * D])
            v(e.tensor_copy(UV[:, :, :].rearrange("p c d -> p (c d)"), B[6][:, 256:512]))
            e.sem_inc(sem("weights_ready"), 1)

        FIELDS = [F_SRC, F_DREL, F_EREL, F_RST, F_A0, F_A1, F_SHI, F_DHI, F_SLO]

        def pe_prep(e):
            e.wait_ge(sem("starts_counted"), 1)
            e.matmul(B[0][:, 0:32], ones[0:125, :], START[0:125, :], start=True, stop=True).then_inc(sem("starts_summed"), 1)
            e.wait_ge(sem("fields_done"), 1)
            r = 0
            for fl in FIELDS:
                for b0 in range(0, VB, 4):
                    if r >= 2:
                        e.wait_ge(sem("fields_copied"), r - 1)
                    for b in range(b0, min(b0 + 4, VB)):
                        mm = e.transpose(B[r % 2][:, (b - b0) * P:(b - b0 + 1) * P], VF[:, fl, b, :], ident[:, :])
                    mm.then_inc(sem("fields_on_pe"), 1)
                    r += 1
            e.wait_ge(sem("weights_in"), 16 * WEIGHT_LOADS)
            for k, c in enumerate([0, 1, 2, 5, 6, 7]):
                mm = e.transpose(B[4][0:D, k * D:(k + 1) * D], WIN[:, c, :], ident[0:D, 0:D])
            mm.then_inc(sem("weights_turned"), 1)
            e.wait_ge(sem("turned_copied"), 1)
            e.matmul(B[5][0:D, 0:2], WTT[:, 0, :], AV[:, 0:2], start=True, stop=True)
            e.matmul(B[5][0:D, 2:4], WTT[:, 1, :], AV[:, 2:4], start=True, stop=True)
            e.matmul(B[5][0:D, 4:6], WIN[:, 2, :], AV[:, 4:8:3], start=True, stop=True)
            e.matmul(B[6][:, 0:2], WE[:, 2:3].to_broadcast([2, P]), WE[:, 0:2], start=True, stop=True)
            for i in range(2):
                e.matmul(B[6][:, 2 + i * D:2 + (i + 1) * D], WE[:, i:i + 1].to_broadcast([2, P]), WE[:, 3:3 + D], start=True, stop=True)
            for k, (blk, wm) in enumerate([(1, 3), (2, 4), (4, 3), (5, 4)]):
                mm = e.matmul(B[6][:, 256 + k * D:256 + (k + 1) * D], AV[:, 4 + blk:5 + blk].to_broadcast([D, P]), WIN[:, wm, :],
                              start=True, stop=True)
            mm.then_inc(sem("weights_folded"), 1)

        WIDE = [69, 69, 69, 256, 256, 128]
        PER = [512 // w for w in WIDE]
        PROJ = [-(-TILES // k) for k in PER]
        PBASE = [sum(PROJ[:k]) for k in range(7)]
        TURNS = -(-TILES // 4)
        XIN = [X, X1, X, X, X1, X]

        def pe_project(e, n):
            e.wait_ge(sem("x_ready"), n + 1)
            for k in range(TURNS):
                if k >= 2:
                    e.wait_ge(sem("xT_copied"), n * TURNS + k - 1)
                for t in range(4 * k, min(4 * k + 4, TILES)):
                    mm = e.transpose(B[k % 2][0:D, (t % 4) * P:(t % 4 + 1) * P], XIN[n][:, t, :], ident[:, :])
                mm.then_inc(sem("xT_on_pe"), 1)
            if n == 0:
                e.wait_ge(sem("weights_ready"), 1)
            for k in range(PROJ[n]):
                last = min((k + 1) * PER[n], TILES) - 1
                e.wait_ge(sem("xT_copied"), n * TURNS + last // 4 + 1)
                if k >= 2:
                    e.wait_ge(sem("proj_copied"), PBASE[n] + k - 1)
                for t in range(k * PER[n], last + 1):
                    o = (t - k * PER[n]) * WIDE[n]
                    mm = e.matmul(B[2 + k % 2][:, o:o + WIDE[n]], XT[:, t * P:(t + 1) * P], WAUG[n][:, :], start=True, stop=True)
                mm.then_inc(sem("proj_on_pe"), 1)

        def act_project(e, n):
            for k in range(TURNS):
                e.wait_ge(sem("xT_on_pe"), n * TURNS + k + 1)
                w = (min(4 * k + 4, TILES) - 4 * k) * P
                e.activation(XT[0:D, k * 4 * P:k * 4 * P + w], B[k % 2][0:D, 0:w], ACT.Copy).then_inc(sem("xT_copied"), 1)

        def dve_project(e, v, n):
            for k in range(PROJ[n]):
                e.wait_ge(sem("proj_on_pe"), PBASE[n] + k + 1)
                t0, t1 = k * PER[n], min((k + 1) * PER[n], TILES)
                bank = B[2 + k % 2][:, 0:(t1 - t0) * WIDE[n]].rearrange("p (t w) -> p t w", w=WIDE[n])
                if KINDS[n] == "A":
                    e.tensor_copy(TB[:, t0:t1, 0:WA], bank[:, :, 0:WA])
                    e.tensor_copy(KF[:, t0:t1, 0:1], bank[:, :, WA:WA + 1]).then_inc(sem("proj_copied"), 1)
                elif KINDS[n] == "B":
                    e.tensor_copy(TB[:, t0:t1, :], bank[:, :, 0:2 * D])
                    e.tensor_copy(KF[:, t0:t1, :], bank[:, :, 2 * D:3 * D])
                    e.tensor_copy(ROOT[:, t0:t1, :], bank[:, :, 3 * D:4 * D]).then_inc(sem("proj_copied"), 1)
                else:
                    e.tensor_copy(TB[:, t0:t1, 0:D], bank[:, :, 0:D])
                    e.tensor_copy(KF[:, t0:t1, :], bank[:, :, D:2 * D]).then_inc(sem("proj_copied"), 1)
            e.wait_ge(sem("proj_copied"), PBASE[n + 1])
            if n == 2:
                moments(e, v)
            w = 1 if KINDS[n] == "A" else D
            r = T1[:, :, 0:w]
            kf = KF[:, :, 0:w]
            v(e.tensor_copy(KS[:, :, 0, 0:w], kf))
            v(e.tensor_tensor(r, kf, KS[:, :, 0, 0:w], ALU.subtract))
            v(e.tensor_copy(KS[:, :, 1, 0:w], r))
            v(e.tensor_tensor(r, r, KS[:, :, 1, 0:w], ALU.subtract))
            e.tensor_copy(KS[:, :, 2, 0:w], r)
            e.memset(ACC[:, :, :], 0.0)
            if n == 2:
                e.tensor_scalar(FLD[:, F_XW, :], FLD[:, F_A0, :], WES[:, 0:1], None, ALU.mult).then_inc(sem("edge_term"), 1)
                e.wait_ge(sem("edge_term"), 1)
                e.scalar_tensor_tensor(out=FLD[:, F_XW, :], in0=FLD[:, F_A1, :], scalar=WES[:, 1:2], in1=FLD[:, F_XW, :],
                                       op0=ALU.mult, op1=ALU.add)
            e.memset(CONST[:, :], 0.0).then_inc(sem("parts_ready"), 1)
            e.wait_ge(sem("parts_ready"), n + 1)

        def sp_table(e, n):
            w = [WA, WA, WA, 128, 128, 64][n]
            e.wait_ge(sem("proj_copied"), PBASE[n + 1])
            e.dma_start(tiled(tabs[n][:, :]), TB[:, :, 0:w]).then_inc(sem("table_written"), 16)
            e.wait_ge(sem("table_written"), 16 * (n + 1))

        def sums_pe(e, src, bank, o, masked):
            for t in range(TILES):
                lhs = lastones if masked and t == TILES - 1 else ones
                mm = e.matmul(bank[:, o:o + D], lhs[:, :], src[:, t, :], start=(t == 0), stop=(t == TILES - 1))
            mm.then_inc(sem("summed"), 1)

        def per_node(ap):
            return ap.unsqueeze(2).to_broadcast([P, TILES, D])

        def per_feat(ap):
            return ap.unsqueeze(1).to_broadcast([P, TILES, D])

        Z = TB[:, :, 0:D]

        def pe_moments(e):
            for s in range(2):
                e.wait_ge(sem("weighted_z"), s + 1)
                sums_pe(e, T1, B[4], s * D, False)
            for s in range(2):
                e.wait_ge(sem("powers_z"), s + 1)
                sums_pe(e, T2, B[5], (2 * s) * D, False)
                sums_pe(e, T1, B[5], (2 * s + 1) * D, False)

        def moments(e, v):
            for s in range(2):
                v(e.tensor_tensor(T1[:, :, :], Z, per_node(CNT[:, s, :]), ALU.mult))
                e.sem_inc(sem("weighted_z"), 1)
                e.wait_ge(sem("summed"), s + 1)
            v(e.tensor_scalar(MU[:, :, :].rearrange("p s d -> p (s d)"), B[4][:, 0:2 * D], 1.0 / E, None, ALU.mult))
            for s in range(2):
                v(e.tensor_tensor(T1[:, :, :], Z, per_feat(MU[:, s, :]), ALU.subtract))
                v(e.tensor_tensor(T2[:, :, :], T1[:, :, :], T1[:, :, :], ALU.mult))
                v(e.tensor_tensor(T2[:, :, :], T2[:, :, :], per_node(CNT[:, s, :]), ALU.mult))
                v(e.tensor_tensor(T1[:, :, :], T1[:, :, :], T2[:, :, :], ALU.mult))
                e.sem_inc(sem("powers_z"), 1)
                e.wait_ge(sem("summed"), 2 + 2 * s + 2)
            mk = MK[:, :, :].rearrange("p s d -> p (s d)")
            a = MK2[:, :, :].rearrange("p s d -> p (s d)")
            b = MK3[:, :, :].rearrange("p s d -> p (s d)")
            v(e.tensor_scalar(mk, B[5][:, 0:4 * D], 1.0 / E, None, ALU.mult))
            v(e.tensor_scalar(a, mk, -1.0, None, ALU.mult))
            v(e.tensor_tensor(a, a, mk, ALU.max))
            v(e.tensor_scalar(a, a, 1e-18, None, ALU.max))
            e.sem_inc(sem("moments_in"), 1)
            v(e.tensor_scalar(b, mk, 0.0, None, ALU.is_gt))
            v(e.tensor_scalar(mk, mk, 0.0, None, ALU.is_lt))
            v(e.tensor_tensor(b, b, mk, ALU.subtract))
            e.wait_ge(sem("roots_done"), 1)
            v(e.tensor_tensor(b, b, a, ALU.mult))
            v(e.tensor_tensor(b, b, UV[:, :, :].rearrange("p s d -> p (s d)"), ALU.mult))
            v(e.tensor_reduce(CONST[:, :], b, AX.X, ALU.add))
            v(e.tensor_scalar(KF[:, :, 0], KF[:, :, 0], CONST[:, :], None, ALU.add))

        def act_moments(e):
            e.wait_ge(sem("moments_in"), 1)
            a = MK2[:, :, :].rearrange("p (s k) d -> p s k d", k=2)
            e.activation(a[:, :, 0, :], a[:, :, 0, :], ACT.Sqrt)
            e.activation(a[:, :, 1, :], a[:, :, 1, :], ACT.Ln).then_inc(sem("log_done"), 1)
            e.wait_ge(sem("log_done"), 1)
            e.activation(a[:, :, 1, :], a[:, :, 1, :], ACT.Exp, scale=1.0 / 3).then_inc(sem("roots_done"), 1)

        def layernorm(e, v, last_n):
            v(e.tensor_tensor(T1[:, :, :], T1[:, :, :], X[:, :, :], ALU.add))
            v(e.tensor_reduce(NV[:, 0, :], T1[:, :, :], AX.X, ALU.add))
            v(e.tensor_scalar(NV[:, 0, :], NV[:, 0, :], 1.0 / D, None, ALU.mult))
            v(e.tensor_tensor(T1[:, :, :], T1[:, :, :], per_node(NV[:, 0, :]), ALU.subtract))
            v(e.tensor_tensor(T2[:, :, :], T1[:, :, :], T1[:, :, :], ALU.mult))
            v(e.tensor_reduce(NV[:, 1, :], T2[:, :, :], AX.X, ALU.add))
            v(e.tensor_scalar(NV[:, 1, :], NV[:, 1, :], 1.0 / D, LN_EPS, ALU.mult, ALU.add))
            e.sem_inc(sem("ln_var"), 1)
            e.wait_ge(sem("ln_root"), last_n + 1)
            v(e.reciprocal(NV[:, 3, :], NV[:, 2, :]))
            v(e.tensor_tensor(X[:, :, :], T1[:, :, :], per_node(NV[:, 3, :]), ALU.mult))

        def act_layernorm(e, k):
            e.wait_ge(sem("ln_var"), k + 1)
            e.activation(NV[:, 2, :], NV[:, 1, :], ACT.Sqrt).then_inc(sem("ln_root"), 1)

        def dve_finish(e, v, n):
            e.wait_ge(sem("sums_added"), (n + 1) * NG * Q)
            nv = lambda k: NV[:, k, :]
            if n < 2:
                z, r = ACC[:, :, D], ACC[:, :, WA - 1]
                v(e.tensor_tensor(nv(0), TB[:, :, WA - 1], KF[:, :, 0], ALU.add))
                v(e.scalar_tensor_tensor(out=nv(0), in0=nv(0), scalar=0.2, in1=nv(0), op0=ALU.mult, op1=ALU.max))
                v(e.tensor_scalar(nv(1), z, 0.0, None, ALU.is_gt))
                v(e.tensor_scalar(nv(2), nv(1), BIG, -BIG, ALU.mult, ALU.add))
                v(e.tensor_tensor(nv(2), nv(2), r, ALU.add))
                v(e.tensor_tensor(nv(3), nv(2), nv(0), ALU.max))
                v(e.tensor_tensor(nv(4), nv(2), nv(3), ALU.subtract))
                v(e.tensor_tensor(nv(5), nv(0), nv(3), ALU.subtract))
                e.sem_inc(sem("self_in"), 1)
                e.wait_ge(sem("self_out"), n + 1)
                v(e.tensor_tensor(nv(1), z, nv(6), ALU.mult))
                v(e.tensor_tensor(nv(1), nv(1), nv(7), ALU.add))
                v(e.tensor_scalar(nv(1), nv(1), 1e-16, None, ALU.add))
                v(e.reciprocal(nv(2), nv(1)))
                v(e.tensor_tensor(T1[:, :, :], ACC[:, :, 0:D], per_node(nv(6)), ALU.mult))
                v(e.tensor_tensor(T2[:, :, :], TB[:, :, 0:D], per_node(nv(7)), ALU.mult))
                v(e.tensor_tensor(T1[:, :, :], T1[:, :, :], T2[:, :, :], ALU.add))
                v(e.tensor_tensor(T1[:, :, :], T1[:, :, :], per_node(nv(2)), ALU.mult))
                v(e.tensor_tensor(T1[:, :, :], T1[:, :, :], per_feat(ROW[:, n, :]), ALU.add))
                if n == 0:
                    v(e.tensor_scalar(X1[:, :, :], T1[:, :, :], 0.0, None, ALU.max))
                else:
                    layernorm(e, v, 0)
            elif n == 2:
                z = ACC[:, :, D]
                v(e.tensor_scalar(nv(0), z, 0.0, None, ALU.is_le))
                v(e.tensor_tensor(nv(0), nv(0), z, ALU.add))
                v(e.reciprocal(nv(1), nv(0)))
                v(e.tensor_copy(T1[:, :, :], ACC[:, :, 0:D]))
                for i in range(2):
                    v(e.tensor_tensor(T2[:, :, :], per_node(ACC[:, :, D + 1 + i]), per_feat(WES[:, 2 + i * D:2 + (i + 1) * D]), ALU.mult))
                    v(e.tensor_tensor(T1[:, :, :], T1[:, :, :], T2[:, :, :], ALU.add))
                v(e.tensor_tensor(T1[:, :, :], T1[:, :, :], per_node(nv(1)), ALU.mult))
                layernorm(e, v, 1)
            elif n < 5:
                l = n - 3
                v(e.tensor_tensor(T1[:, :, :], ACC[:, :, 0:D], ROOT[:, :, :], ALU.add))
                v(e.tensor_scalar(T1[:, :, :], T1[:, :, :], 0.0, None, ALU.max))
                e.sem_inc(sem("bn_in"), 1)
                e.wait_ge(sem("summed"), 6 + 2 * l + 1)
                v(e.tensor_scalar(BN[:, 0, :], B[4][:, 0:D], 1.0 / N, None, ALU.mult))
                v(e.tensor_tensor(T1[:, :, :], T1[:, :, :], per_feat(BN[:, 0, :]), ALU.subtract))
                v(e.tensor_tensor(T2[:, :, :], T1[:, :, :], T1[:, :, :], ALU.mult))
                e.sem_inc(sem("bn_sq"), 1)
                e.wait_ge(sem("summed"), 6 + 2 * l + 2)
                v(e.tensor_scalar(BN[:, 1, :], B[5][:, 0:D], 1.0 / N, BN_EPS, ALU.mult, ALU.add))
                e.sem_inc(sem("bn_var"), 1)
                e.wait_ge(sem("bn_root"), l + 1)
                v(e.reciprocal(BN[:, 3, :], BN[:, 2, :]))
                v(e.tensor_tensor(BN[:, 3, :], BN[:, 3, :], ROW[:, 2 + l, :], ALU.mult))
                v(e.tensor_tensor(T1[:, :, :], T1[:, :, :], per_feat(BN[:, 3, :]), ALU.mult))
                dst = X1 if l == 0 else T1
                v(e.tensor_tensor(dst[:, :, :], T1[:, :, :], per_feat(ROW[:, 4 + l, :]), ALU.add))
                if l == 1:
                    layernorm(e, v, 2)
            else:
                v(e.tensor_scalar(nv(0), CNT[:, 1, :], 0.0, None, ALU.is_gt))
                v(e.tensor_tensor(T1[:, :, :], ACC[:, :, 0:D], per_feat(ROW[:, 6, :]), ALU.add))
                v(e.tensor_tensor(T1[:, :, :], T1[:, :, :], per_node(nv(0)), ALU.mult))
                layernorm(e, v, 3)
            e.sem_inc(sem("x_ready"), 1)

        def pe_finish(e, n):
            if n in (3, 4):
                e.wait_ge(sem("bn_in"), n - 2)
                sums_pe(e, T1, B[4], 0, True)
                e.wait_ge(sem("bn_sq"), n - 2)
                sums_pe(e, T2, B[5], 0, True)

        def act_finish(e, n):
            if n < 2:
                e.wait_ge(sem("self_in"), n + 1)
                e.activation(NV[:, 6, :], NV[:, 4, :], ACT.Exp)
                e.activation(NV[:, 7, :], NV[:, 5, :], ACT.Exp).then_inc(sem("self_out"), 1)
            if n in (3, 4):
                e.wait_ge(sem("bn_var"), n - 2)
                e.activation(BN[:, 2, :], BN[:, 1, :], ACT.Sqrt).then_inc(sem("bn_root"), 1)
            if n in (1, 2, 4, 5):
                act_layernorm(e, {1: 0, 2: 1, 4: 2, 5: 3}[n])

        @block.gpsimd
        def _(e):
            pool_prep(e)
            for n in range(6):
                pool_pass(e, n)

        @block.sync
        def _(e):
            sp_prep(e)
            sp_index(e)
            for n in range(6):
                sp_table(e, n)
                sp_pass(e, n)
            e.wait_ge(sem("x_ready"), 7)
            e.dma_start(out[0:(TILES - 1) * P, :].rearrange("(t p) w -> p t w", p=P), X[:, 0:TILES - 1, :]).then_inc(sem("result_out"), 16)
            e.dma_start(out[(TILES - 1) * P:N, :], X[0:LASTN, TILES - 1, :]).then_inc(sem("result_out"), 16)
            e.wait_ge(sem("result_out"), 32)

        @block.tensor
        def _(e):
            pe_prep(e)
            pe_index(e)
            e.wait_ge(sem("walk_in"), 16)
            for n in range(6):
                pe_project(e, n)
                if n == 2:
                    pe_moments(e)
                pe_pass(e, n)
                pe_finish(e, n)

        @block.scalar
        def _(e):
            act_prep(e)
            act_index(e)
            for n in range(6):
                act_project(e, n)
                if n == 2:
                    act_moments(e)
                act_pass(e, n)
                act_finish(e, n)

        @block.vector
        def _(e):
            v = Own(e, "dve_done")
            dve_prep(e, v)
            dve_index(e)
            e.wait_ge(sem("degrees_done"), 1)
            e.wait_ge(sem("x_in"), 32)
            e.wait_ge(sem("walk_in"), 16)
            e.sem_inc(sem("x_ready"), 1)
            for n in range(6):
                dve_project(e, v, n)
                dve_pass(e, n)
                dve_finish(e, v, n)


_INS = ["x", "src", "dst", "edge_attr_2", "L0_gnn_W1", "L0_gnn_a_src1", "L0_gnn_a_dst1", "L0_gnn_b1", "L0_gnn_W2",
        "L0_gnn_a_src2", "L0_gnn_a_dst2", "L0_gnn_b2", "L1_gnn_W_fc", "L1_gnn_W_attn", "L1_gnn_W_edge", "L1_gnn_W_e2n",
        "L1_gnn_W_m1", "L1_gnn_W_m2", "L2_gnn_Wk", "L2_gnn_bk", "L2_gnn_Wq", "L2_gnn_bq", "L2_gnn_Wv", "L2_gnn_bv",
        "L2_gnn_Ws", "L2_gnn_bs", "L2_gnn_bias", "L2_gnn_gamma", "L2_gnn_beta", "L3_gnn_W1", "L3_gnn_b1", "L3_gnn_W2",
        "L3_gnn_b2"]


def kernel(**inputs):
    import numpy as _np
    import concourse.bacc as _bacc
    from concourse import mybir as _mybir
    from concourse.bass_utils import run_bass_kernel_spmd as _run

    nc = _bacc.Bacc("TRN2", target_bir_lowering=False, num_devices=1)
    arrays, args = {}, {}
    for name in _INS:
        a = _np.ascontiguousarray(inputs[name])
        arrays[f"in_{name}"] = a
        args[name] = nc.dram_tensor(f"in_{name}", a.shape, _mybir.dt.from_np(a.dtype), kind="ExternalInput").ap()
    result = nc.dram_tensor("out_0", (N, D), _mybir.dt.float32, kind="ExternalOutput").ap()
    build(nc, args, result)
    r = _run(nc, [arrays], core_ids=[0])
    return r.results[0]["out_0"]
```

```python
import concourse.bass as bass
from concourse import mybir
from contextlib import ExitStack

f32 = mybir.dt.float32
i32 = mybir.dt.int32
u32 = mybir.dt.uint32
bf16 = mybir.dt.bfloat16
ALU = mybir.AluOpType
ACT = mybir.ActivationFunctionType
AX = mybir.AxisListType

P = 128
N, E, D = 3125, 100000, 64
TILES = -(-N // P)
LASTN = N - (TILES - 1) * P
CHUNKS = -(-E // P)
LASTE = E - (CHUNKS - 1) * P
Q = 4
SPANS = -(-CHUNKS // Q)
U = 4
NG = -(-(SPANS + TILES - 1) // U) * U
VB = -(-NG * Q // P)
VP = VB * P
REC = 6 * P
NF = 11
F_SRC, F_DREL, F_EREL, F_RST, F_A0, F_A1, F_M, F_XW, F_SHI, F_DHI, F_SLO = range(NF)
F_D, F_W, F_S = F_DHI, F_DHI, F_SLO
WT = D + 1
WA = WT + 3
TW = [WT, WT, WT, 2 * D, 2 * D, D]
BIG = 1e30
LN_EPS = 1e-5
BN_EPS = 1e-5


class At:

    def __init__(self, c, i=None):
        self.c, self.i = c, i

    def times(self, m, a=0):
        return self.c * m + a if self.i is None else self.i * (m * U) + (self.c * m + a)

    def rounds(self, m, a=0):
        return (self.c // U) * m + a if self.i is None else self.i * m + ((self.c // U) * m + a)

    @property
    def slot(self):
        return self.c % U

    def par(self, n):
        return self.c % n


def steps(e, stages):
    top = max(lag for lag, _ in stages)
    first = -(-(top + U) // U) * U

    def one(c, i=None):
        for lag, fn in stages:
            if i is not None or 0 <= c - lag < NG:
                fn(At(c - lag, i))

    for s in range(first):
        one(s)
    with e.Fori(0, (NG - first) // U) as i:
        for k in range(U):
            one(first + k, i)
    for s in range(NG, NG + top):
        one(s)


def build(nc, A, out):
    ctx = ExitStack()
    with ctx, nc.allow_non_contiguous_dma(reason="small columns and transposed weights"):
        def sb(name, shape, dt=f32):
            return ctx.enter_context(nc.sbuf_tensor(name, shape, dt))

        def pb(name, shape, dt=f32):
            return ctx.enter_context(nc.psum_tensor(name, shape, dt))

        made = {}

        def sem(name):
            if name not in made:
                made[name] = ctx.enter_context(nc.semaphore(name))
            return made[name]

        class Own:

            def __init__(self, e, name):
                self.e, self.sem, self.n = e, sem(name), 0

            def done(self, ins):
                self.n += 1
                ins.then_inc(self.sem, 1)

            def wait(self):
                if self.n:
                    self.e.wait_ge(self.sem, self.n)

            def __call__(self, ins):
                self.done(ins)
                self.wait()

        def gate(e, who, s, val):
            if isinstance(val, int):
                if val > 0:
                    e.wait_ge(s, val)
            else:
                e.wait_ge(s, val)
                e.sem_inc(sem("passed_" + who), 1)

        def hold(e, s, val):
            if not isinstance(val, int) or val > 0:
                e.wait_ge(s, val)

        rec_d = nc.dram_tensor("rec_d", [CHUNKS + 1, REC], i32)
        ohT_d = nc.dram_tensor("ohT_d", [NG, P, 2 * Q * P], bf16)
        tv_d = nc.dram_tensor("tv_d", [VB, P], i32)
        tabs = [nc.dram_tensor(f"tab{k}_d", [TILES * P, w], f32) for k, w in enumerate(TW)]

        X = sb("X", [P, TILES, D])
        X1 = sb("X1", [P, TILES, D])
        TB = sb("TB", [P, TILES, 128])
        KF = sb("KF", [P, TILES, D])
        KS = sb("KS", [P, TILES, 3, D], bf16)
        ROOT = sb("ROOT", [P, TILES, D])
        ACC = sb("ACC", [P, TILES, WA])
        T1 = sb("T1", [P, TILES, D])
        T2 = sb("T2", [P, TILES, D])
        NV = sb("NV", [P, 8, TILES])
        XT = sb("XT", [D + 1, TILES * P])
        WAUG = [sb(f"WAUG{k}", [D + 1, w]) for k, w in enumerate([WT + 2] * 3 + [4 * D] * 2 + [2 * D])]
        WIN = sb("WIN", [D, 8, D])
        WTT = sb("WTT", [D, 6, D])
        W2T = sb("W2T", [D, D])
        AV = sb("AV", [D, 10])
        WE = sb("WE", [2, 2 + 1 + D])
        WES = sb("WES", [P, 2 + 2 * D])
        BIASR = sb("BIASR", [D + 1, 2, D])
        ROW = sb("ROW", [P, 7, D])
        UV = sb("UV", [P, 4, D])
        MU = sb("MU", [P, 2, D])
        MK = sb("MK", [P, 4, D])
        MK2 = sb("MK2", [P, 4, D])
        MK3 = sb("MK3", [P, 4, D])
        CONST = sb("CONST", [P, 1])
        BN = sb("BN", [P, 4, D])
        ident = sb("ident", [P, P])
        identb = sb("identb", [P, P], bf16)
        ones = sb("ones", [P, P])
        lastones = sb("lastones", [P, P])
        iotab = sb("iotab", [P, P], bf16)
        iotaf = sb("iotaf", [P, P])
        iopf = sb("iopf", [P, 1])
        FLD = sb("FLD", [P, NF, VP])
        TVR = sb("TVR", [1, VP], i32)
        AS = sb("AS", [P, TILES])
        ATB = sb("ATB", [P, 3, TILES], bf16)
        zeros = sb("zeros", [P, P])
        RSTV = sb("RSTV", [P, VB, P])
        ENDV = sb("ENDV", [P, VB, P])
        PM = sb("PM", [P, VB, P])
        SMK = sb("SMK", [P, VB, P])
        HASR = sb("HASR", [1, VP])
        HASE = sb("HASE", [1, VP])
        CINS = sb("CINS", [P, 2, VB])
        CNT = sb("CNT", [P, 2, TILES])

        prep = ExitStack()

        def tmp(name, shape, dt=f32):
            return prep.enter_context(nc.sbuf_tensor(name, shape, dt))

        ioi = tmp("ioi", [P, P], i32)
        iop = tmp("iop", [P, 1], i32)
        flat = lambda T: T[:, :, :].rearrange("p t d -> p (t d)")
        DST_I = flat(ROOT)[0:125, 0:E // 125].bitcast(i32)
        DST_F = flat(T1)[0:125, 0:E // 125]
        DST_J = flat(T2)[0:125, 0:E // 125]
        START = tmp("START", [P, 32])
        VT_F = tmp("VT_F", [P, 32])
        VT_I = tmp("VT_I", [P, 32], i32)
        VIO_I = tmp("VIO_I", [P, VB], i32)
        VIO = tmp("VIO", [P, VB])
        CMP = tmp("CMP", [P, VB, TILES - 1])
        TVP = tmp("TVP", [P, VB])
        TVPI = tmp("TVPI", [P, VB], i32)
        CVF = tmp("CVF", [P, VB])
        CVI = tmp("CVI", [P, VB], u32)
        PADR = tmp("PADR", [1, REC + 1], i32)
        REC_S = flat(FLD)[:, 0:VB * REC].bitcast(i32).rearrange("p (v r) -> p v r", r=REC)
        VF = tmp("VF", [P, NF, VB, P])
        prep.close()

        IDX = sb("IDX", [P, U, Q], u32)
        RS4 = sb("RS4", [P, U, Q])
        G = sb("G", [P, U, Q, 128])
        OT = sb("OT", [P, U, 2 * Q * P], bf16)
        OHD = sb("OHD", [P, 2, Q, P], bf16)
        OHS = sb("OHS", [P, 2, Q, P], bf16)
        HID = sb("HID", [P, 2, Q, 32], bf16)
        HIS = sb("HIS", [P, 2, Q, TILES], bf16)
        PRD = sb("PRD", [P, Q, 3, TILES])
        OEF = sb("OEF", [P, 2, Q * P])
        MS = sb("MS", [D, 2, Q * P])
        SO = sb("SO", [D, 2, Q * P])
        PR = sb("PR", [P, 2, Q, D])
        SG = sb("SG", [P, 2, Q, D])
        MSG = sb("MSG", [P, 2, Q, D])
        XS = MSG
        HT = sb("HT", [D, 2, Q * P])

        B = [pb(f"bank{k}", [P, 512]) for k in range(7)]
        BT = pb("bankT", [P, 1024], bf16)

        block = ctx.enter_context(nc.Block())
        AP_ATT = ["L0a", "L0b", "L1"]
        x_t = A["x"]

        def tiled(ap):
            return ap.rearrange("(t p) w -> p t w", p=P)

        KINDS = ["A", "A", "A", "B", "B", "C"]
        NA_BEFORE = [0, 1, 2, 3, 3, 3]
        ROUNDS = NG // U

        def grp(n, g, per=1, a=0):
            return g.times(per, n * NG * per + per + a * per)

        def ring(n, g, per):
            return g.rounds(per, n * ROUNDS * per + per)

        MASKP = 0
        GATP = [None, None, None, 0, 1, None]
        PREP = [None, None, None, 0, 1, 2]

        def rows_free(n, g, a):
            return {"A": ("picked", grp(n, g, a=a)), "B": ("msg_ready", grp(GATP[n] or 0, g, a=a)),
                    "C": ("hT_on_pe", grp(0, g, a=a))}[KINDS[n]]

        def pool_pass(e, n):
            w = TW[n]
            e.wait_ge(sem("table_written"), 16 * (n + 1))

            def gather(g):
                gate(e, "pool", sem("idx_ready"), grp(n, g))
                for q in range(Q):
                    e.indirect_dma_start(
                        out=G[:, g.slot, q, 0:w], out_offset=None, in_=tabs[n][:, :],
                        in_offset=bass.IndirectOffsetOnAxis(ap=IDX[:, g.slot, q:q + 1], axis=0),
                    ).then_inc(sem(f"rows_in{g.slot}"), 16)

            steps(e, [(0, gather)])

        def sp_stream(e, n):
            w = 2 * Q * P if KINDS[n] == "A" else Q * P

            def load(g):
                if KINDS[n] == "A":
                    gate(e, "sp", sem("scores_on_pe"), grp(n, g, a=-U))
                else:
                    gate(e, "sp", sem("spread_on_pe"), grp(PREP[n], g, a=-U))
                e.dma_start(OT[:, g.slot, 0:w].unsqueeze(1),
                            ohT_d[bass.ds(g.times(1), 1), :, 0:w].rearrange("g p f -> p g f")).then_inc(sem(f"ohT_in{g.slot}"), 16)

            steps(e, [(0, load)])

        def tile_of(e, g):
            return e.value_load(TVR[0:1, bass.ds(g.times(Q), 1)], min_val=0, max_val=TILES - 1)

        def pe_scores(e, n):
            e.wait_ge(sem("parts_ready"), n + 1)

            def fn(g):
                bank = B[g.par(2)]
                t = tile_of(e, g)
                gate(e, "pe", sem(f"ohT_in{g.slot}"), ring(n, g, 16))
                gate(e, "pe", sem("score_read"), grp(n, g, a=-2))
                for q in range(Q):
                    e.matmul(bank[:, 3 * q:3 * q + 3], OT[:, g.slot, q * P:(q + 1) * P],
                             KS[:, bass.ds(t, 1), :, 0:1].rearrange("p a k o -> p (a k o)"), start=True, stop=True)
                    mm = e.matmul(bank[:, 16 + 3 * TILES * q:16 + 3 * TILES * (q + 1)], OT[:, g.slot, (Q + q) * P:(Q + q + 1) * P],
                                  ATB[:, :, :].rearrange("p k t -> p (k t)"), start=True, stop=True)
                mm.then_inc(sem("scores_on_pe"), 1)

            steps(e, [(0, fn)])

        def dve_scores(e, n):
            def fn(g):
                bank = B[g.par(2)]
                vs = bass.ds(g.times(Q), Q)
                e.tensor_tensor(HIS[:, 0, :, :], FLD[:, F_SHI, vs].unsqueeze(2).to_broadcast([P, Q, TILES]),
                                iotaf[:, 0:TILES].unsqueeze(1).to_broadcast([P, Q, TILES]), ALU.is_equal).then_inc(sem("tile_hot"), 1)
                gate(e, "dve", sem("scores_on_pe"), grp(n, g))
                hold(e, sem("tile_hot"), grp(n, g))
                e.tensor_tensor(PRD[:, :, :, :], bank[:, 16:16 + 3 * TILES * Q].rearrange("p (q k t) -> p q k t", q=Q, k=3),
                                HIS[:, 0, :, :].unsqueeze(2).to_broadcast([P, Q, 3, TILES]), ALU.mult).then_inc(sem("own_tile"), 1)
                e.tensor_reduce(FLD[:, F_D, vs], bank[:, 0:3 * Q].rearrange("p (q k) -> p q k", k=3), AX.X, ALU.add)
                hold(e, sem("own_tile"), grp(n, g))
                e.tensor_reduce(FLD[:, F_S, vs], PRD[:, :, :, :].rearrange("p q k t -> p q (k t)"), AX.X, ALU.add)\
                    .then_inc(sem("score_read"), 1)

            steps(e, [(0, fn)])
            e.wait_ge(sem("score_read"), (n + 1) * NG)

        SV = ROOT[:, :, :].rearrange("p t d -> p (t d)")[:, 0:VP].rearrange("p (k i) -> p k i", k=VB)
        FV = T1[:, :, :].rearrange("p t d -> p (t d)")[:, 0:VP].rearrange("p (k i) -> p k i", k=VB)
        MV = T2[:, :, :].rearrange("p t d -> p (t d)")[:, 0:VP].rearrange("p (k i) -> p k i", k=VB)
        LASTR = XT[0:1, 0:VP]
        CARRY = XT[0:1, VP:2 * VP + 1]
        HALVES = [(0, 4), (4, VB)]

        def turn_blocks(e, src, b0, name):
            for h, (k0, k1) in enumerate(HALVES):
                for k in range(k0, k1):
                    mm = e.transpose(B[b0 + h][:, (k - k0) * P:(k - k0 + 1) * P], src(k), ident[:, :])
            mm.then_inc(sem(name), 1)

        def row_out(e, src, name):
            for h, (k0, k1) in enumerate(HALVES):
                for k in range(k0, k1):
                    mm = e.transpose(B[4 + h][0:1, (k - k0) * P:(k - k0 + 1) * P], src(k), ident[:, :])
            mm.then_inc(sem(name), 1)

        def row_in(e, src, name):
            for k in range(VB):
                mm = e.transpose(B[6][:, k:k + 1], src(k), ident[0:1, 0:1])
            mm.then_inc(sem(name), 1)

        def pe_segments(e, n):
            e.wait_ge(sem("scores_ready"), n + 1)
            turn_blocks(e, lambda k: FLD[:, F_S, k * P:(k + 1) * P], 2, "scores_turned")
            e.wait_ge(sem("prefix_done"), n + 1)
            row_out(e, lambda k: FV[:, k, P - 1:P], "prefix_row")
            e.wait_ge(sem("prefix_carry"), n + 1)
            row_in(e, lambda k: CARRY[:, k * P:(k + 1) * P], "prefix_cols")
            e.wait_ge(sem("suffix_done"), n + 1)
            row_out(e, lambda k: MV[:, k, 0:1], "suffix_row")
            e.wait_ge(sem("suffix_carry"), n + 1)
            row_in(e, lambda k: CARRY[:, 1 + k * P:1 + (k + 1) * P], "suffix_cols")
            e.wait_ge(sem("maxima_done"), n + 1)
            turn_blocks(e, lambda k: MV[:, k, :], 0, "maxima_turned")
            e.wait_ge(sem("weights_done"), n + 1)
            turn_blocks(e, lambda k: SV[:, k, :], 2, "weights_back")

        def act_segments(e, n):
            e.wait_ge(sem("scores_turned"), n + 1)
            for h, (k0, k1) in enumerate(HALVES):
                mm = e.activation(SV[:, k0:k1, :].rearrange("p k i -> p (k i)"), B[2 + h][:, 0:(k1 - k0) * P], ACT.Copy)
            mm.then_inc(sem("scores_in_rows"), 1)
            e.wait_ge(sem("exponents_done"), n + 1)
            e.activation(SV, FV, ACT.Exp).then_inc(sem("weights_done"), 1)
            e.wait_ge(sem("maxima_turned"), n + 1)
            for h, (k0, k1) in enumerate(HALVES):
                e.activation(FLD[:, F_M, k0 * P:k1 * P], B[h][:, 0:(k1 - k0) * P], ACT.Copy)
            e.wait_ge(sem("weights_back"), n + 1)
            for h, (k0, k1) in enumerate(HALVES):
                mm = e.activation(FLD[:, F_W, k0 * P:k1 * P], B[2 + h][:, 0:(k1 - k0) * P], ACT.Copy)
            mm.then_inc(sem("attention_ready"), 1)

        def dve_segments(e, v, n):
            slope = [0.2, 0.2, 0.01][n]
            s = FLD[:, F_S, :]
            v(e.tensor_tensor(s, s, FLD[:, F_D, :], ALU.add))
            v(e.tensor_tensor(s, s, FLD[:, F_XW, :], ALU.add))
            v(e.scalar_tensor_tensor(out=s, in0=s, scalar=slope, in1=s, op0=ALU.mult, op1=ALU.max))
            e.sem_inc(sem("scores_ready"), 1)
            e.wait_ge(sem("scores_in_rows"), n + 1)
            for k in range(VB):
                sc = e.tensor_tensor_scan(FV[:, k, :], RSTV[:, k, :], SV[:, k, :], -BIG, ALU.add, ALU.max)
            sc.then_inc(sem("prefix_done"), 1)
            e.wait_ge(sem("prefix_row"), n + 1)
            e.memset(CARRY[:, 0:1], -BIG)
            e.tensor_copy(LASTR[:, 0:4 * P], B[4][0:1, :])
            v(e.tensor_copy(LASTR[:, 4 * P:VP], B[5][0:1, 0:VP - 4 * P]))
            e.tensor_tensor_scan(CARRY[:, 1:VP + 1], HASR[:, :], LASTR, -BIG, ALU.add, ALU.max).then_inc(sem("prefix_carry"), 1)
            e.wait_ge(sem("prefix_cols"), n + 1)
            v(e.tensor_copy(CINS[:, 0, :], B[6][:, 0:VB]))
            v(e.tensor_tensor(MV, PM[:, :, :], CINS[:, 0, :].unsqueeze(2).to_broadcast([P, VB, P]), ALU.add))
            v(e.tensor_tensor(FV, MV, FV, ALU.max))
            for k in range(VB):
                sc = e.tensor_tensor_scan(MV[:, k, ::-1], ENDV[:, k, ::-1], FV[:, k, ::-1], -BIG, ALU.add, ALU.max)
            sc.then_inc(sem("suffix_done"), 1)
            e.wait_ge(sem("suffix_row"), n + 1)
            e.memset(CARRY[:, VP:VP + 1], -BIG)
            e.tensor_copy(LASTR[:, 0:4 * P], B[4][0:1, :])
            v(e.tensor_copy(LASTR[:, 4 * P:VP], B[5][0:1, 0:VP - 4 * P]))
            e.tensor_tensor_scan(XT[0:1, 2 * VP - 1:VP - 1:-1], HASE[:, ::-1], XT[0:1, VP - 1::-1], -BIG, ALU.add, ALU.max)\
                .then_inc(sem("suffix_carry"), 1)
            e.wait_ge(sem("suffix_cols"), n + 1)
            v(e.tensor_copy(CINS[:, 1, :], B[6][:, 0:VB]))
            v(e.tensor_tensor(FV, SMK[:, :, :], CINS[:, 1, :].unsqueeze(2).to_broadcast([P, VB, P]), ALU.add))
            v(e.tensor_tensor(MV, MV, FV, ALU.max))
            e.sem_inc(sem("maxima_done"), 1)
            v(e.tensor_tensor(FV, SV, MV, ALU.subtract))
            e.sem_inc(sem("exponents_done"), 1)
            e.wait_ge(sem("attention_ready"), n + 1)

        def pe_spread(e, n, bank):
            def fn(g):
                t = tile_of(e, g)
                gate(e, "pe", sem(f"ohT_in{g.slot}"), ring(n, g, 16))
                gate(e, "pe", sem("pre_ready"), grp(PREP[n], g, a=-1))
                for q in range(Q):
                    for k in range(3):
                        mm = e.matmul(bank[:, q * D:(q + 1) * D], OT[:, g.slot, q * P:(q + 1) * P],
                                      KS[:, bass.ds(t, 1), k, :].rearrange("p a w -> p (a w)"),
                                      start=(k == 0), stop=(k == 2))
                mm.then_inc(sem("spread_on_pe"), 1)
            return fn

        def pe_pick(e, n, w, src, ready):
            def fn(g):
                gate(e, "pe", sem(ready[0]), grp(ready[1], g))
                gate(e, "pe", sem("ohF_ready"), grp(n, g))
                gate(e, "pe", sem("sums_added"), grp(n, g, a=-2))
                for q in range(Q):
                    mm = e.matmul(B[5 + g.par(2)][:, 0:w], OEF[:, g.par(2), q * P:(q + 1) * P], src(g, q),
                                  start=(q == 0), stop=(q == Q - 1))
                mm.then_inc(sem("picked"), 1)
            return fn

        def pe_pass(e, n):
            kind = KINDS[n]
            if kind == "A":
                steps(e, [(0, pe_pick(e, n, WA, lambda g, q: G[:, g.slot, q, 0:WA], ("rows_whole", n)))])
                return
            e.wait_ge(sem("parts_ready"), n + 1)
            if kind == "B":
                steps(e, [(0, pe_spread(e, n, B[0])),
                          (1, pe_pick(e, n, D, lambda g, q: MSG[:, g.par(2), q, :], ("msg_ready", GATP[n])))])
            else:
                def turn(g):
                    gate(e, "pe", sem("hidden_ready"), grp(0, g))
                    gate(e, "pe", sem("masks_ready"), grp(0, g))
                    gate(e, "pe", sem("hT_copied"), grp(0, g, a=-1))
                    for q in range(Q):
                        e.matmul(B[2][0:D, q * P:(q + 1) * P], RS4[:, g.slot, q:q + 1].to_broadcast([P, D]),
                                 ident[:, :], start=True, stop=True)
                    for q in range(Q):
                        mm = e.transpose(B[3][0:D, q * P:(q + 1) * P], SG[:, g.par(2), q, :], ident[:, :])
                    mm.then_inc(sem("hT_on_pe"), 1)

                def mlp(g):
                    gate(e, "pe", sem("hT_copied"), grp(0, g))
                    gate(e, "pe", sem("scanned"), grp(0, g, a=-1))
                    e.matmul(B[1][0:D, :], W2T[:, :], HT[:, g.par(2), :], start=True, stop=True).then_inc(sem("mlp_on_pe"), 1)

                def back(g):
                    gate(e, "pe", sem("scanned"), grp(0, g))
                    gate(e, "pe", sem("ends_copied"), grp(0, g, a=-1))
                    for q in range(Q):
                        mm = e.transpose(B[4][:, q * D:(q + 1) * D], SO[:, g.par(2), q * P:(q + 1) * P], ident[0:D, 0:D])
                    mm.then_inc(sem("back_on_pe"), 1)

                steps(e, [(2, mlp), (1, turn), (0, pe_spread(e, n, B[0])), (3, back),
                          (4, pe_pick(e, n, D, lambda g, q: XS[:, g.par(2), q, :], ("ends_copied", 0)))])

        def act_indices(e, n):
            def fn(g):
                free, val = rows_free(n, g, -U)
                gate(e, "act", sem(free), val)
                e.activation(IDX[:, g.slot, :], FLD[:, F_SRC, bass.ds(g.times(Q), Q)], ACT.Copy).then_inc(sem("idx_ready"), 1)
                if KINDS[n] == "C":
                    e.activation(RS4[:, g.slot, :], FLD[:, F_RST, bass.ds(g.times(Q), Q)], ACT.Copy).then_inc(sem("masks_ready"), 1)
            return fn

        def act_pass(e, n):
            kind = KINDS[n]
            if kind == "A":
                steps(e, [(0, act_indices(e, n))])
            elif kind == "B":
                def gates(g):
                    gate(e, "act", sem("pre_ready"), grp(PREP[n], g))
                    gate(e, "act", sem("msg_ready"), grp(GATP[n], g, a=-2))
                    e.activation(SG[:, g.par(2), :, :], PR[:, g.par(2), :, :], ACT.Sigmoid).then_inc(sem("gate_ready"), 1)

                steps(e, [(0, act_indices(e, n)), (3, gates)])
            else:
                def hidden(g):
                    gate(e, "act", sem("pre_ready"), grp(2, g))
                    gate(e, "act", sem("hT_on_pe"), grp(0, g, a=-2))
                    e.activation(SG[:, g.par(2), :, :], PR[:, g.par(2), :, :], ACT.Relu).then_inc(sem("hidden_ready"), 1)

                def hT(g):
                    gate(e, "act", sem("hT_on_pe"), grp(0, g))
                    gate(e, "act", sem("mlp_on_pe"), grp(0, g, a=-2))
                    gate(e, "act", sem("scanned"), grp(0, g, a=-2))
                    e.activation(MS[:, g.par(2), :], B[2][0:D, :], ACT.Copy)
                    e.activation(HT[:, g.par(2), :], B[3][0:D, :], ACT.Copy).then_inc(sem("hT_copied"), 1)

                def ends(g):
                    gate(e, "act", sem("back_on_pe"), grp(0, g))
                    gate(e, "act", sem("picked"), grp(n, g, a=-2))
                    e.activation(XS[:, g.par(2), :, :], B[4][:, 0:Q * D].rearrange("p (a w) -> p a w", a=Q), ACT.Copy)\
                        .then_inc(sem("ends_copied"), 1)

                steps(e, [(0, act_indices(e, n)), (3, hidden), (3, hT), (5, ends)])

        def dve_add(e, n, w):
            def fn(g):
                t = tile_of(e, g)
                gate(e, "dve", sem("picked"), grp(n, g))
                hold(e, sem("sums_added"), grp(n, g, a=-1))
                e.tensor_tensor(ACC[:, bass.ds(t, 1), 0:w], ACC[:, bass.ds(t, 1), 0:w],
                                B[5 + g.par(2)][:, 0:w].unsqueeze(1), ALU.add).then_inc(sem("sums_added"), 1)
            return fn

        def one_hots(e, g, field, weight=None):
            for q in range(Q):
                vq = bass.ds(g.times(Q, q), 1)
                oh = e.tensor_scalar(OEF[:, g.par(2), q * P:(q + 1) * P], iotab[:, :], FLD[:, field, vq],
                                     None if weight is None else FLD[:, weight, vq], ALU.is_equal,
                                     *([] if weight is None else [ALU.mult]))
            oh.then_inc(sem("ohF_ready"), 1)

        def dve_pass(e, n):
            kind = KINDS[n]
            if kind == "A":
                def weigh(g):
                    gate(e, "dve", sem("picked"), grp(n, g, a=-2))
                    one_hots(e, g, F_DREL, F_W)

                def join(g):
                    gate(e, "dve", sem(f"rows_in{g.slot}"), ring(n, g, 64))
                    e.tensor_copy(G[:, g.slot, :, WT:WA],
                                  FLD[:, F_A0:F_M + 1, bass.ds(g.times(Q), Q)].rearrange("p f v -> p v f")).then_inc(sem("rows_whole"), 1)

                steps(e, [(0, weigh), (0, join), (1, dve_add(e, n, WA))])
                return

            def pre(g):
                gate(e, "dve", sem(f"rows_in{g.slot}"), ring(n, g, 64))
                if kind == "B":
                    gate(e, "dve", sem("gate_ready"), grp(GATP[n], g, a=-2))
                else:
                    gate(e, "dve", sem("hidden_ready"), grp(0, g, a=-2))
                hold(e, sem("spread_on_pe"), grp(PREP[n], g))
                e.tensor_tensor(PR[:, g.par(2), :, :], B[0][:, 0:Q * D].rearrange("p (q d) -> p q d", q=Q),
                                G[:, g.slot, :, 0:D], ALU.add).then_inc(sem("pre_ready"), 1)

            if kind == "B":
                def msg(g):
                    gate(e, "dve", sem("picked"), grp(n, g, a=-2))
                    one_hots(e, g, F_DREL)
                    hold(e, sem("gate_ready"), grp(GATP[n], g))
                    e.tensor_tensor(MSG[:, g.par(2), :, :], SG[:, g.par(2), :, :], G[:, g.slot, :, D:2 * D],
                                    ALU.mult).then_inc(sem("msg_ready"), 1)

                steps(e, [(1, msg), (0, pre), (2, dve_add(e, n, D))])
            else:
                def scan(g):
                    p, o = g.par(2), 1 - g.par(2)
                    gate(e, "dve", sem("picked"), grp(n, g, a=-2))
                    one_hots(e, g, F_EREL)
                    gate(e, "dve", sem("mlp_on_pe"), grp(0, g))
                    gate(e, "dve", sem("back_on_pe"), grp(0, g, a=-2))
                    if g.i is None and g.c == 0:
                        init = -BIG
                    else:
                        init = SO[:, o, Q * P - 1:Q * P]
                        hold(e, sem("scanned"), grp(0, g, a=-1))
                    e.tensor_tensor_scan(SO[:, p, :], MS[:, p, :], B[1][0:D, :], init, ALU.add, ALU.max)\
                        .then_inc(sem("scanned"), 1)

                steps(e, [(2, scan), (0, pre), (4, dve_add(e, n, D))])

        def dve_index(e):
            def build_oh(g):
                gate(e, "dve", sem("idx_on_pe"), g.times(1, 1 - 2))
                for q in range(Q):
                    v = bass.ds(g.times(Q, q), 1)
                    e.tensor_scalar(OHD[:, g.par(2), q, :], iotab[:, :], FLD[:, F_DREL, v], None, ALU.is_equal)
                    e.tensor_scalar(OHS[:, g.par(2), q, :], iotab[:, :], FLD[:, F_SLO, v], None, ALU.is_equal)
                    e.tensor_scalar(HIS[:, g.par(2), q, :], iotab[:, 0:TILES], FLD[:, F_SHI, v], None, ALU.is_equal)
                    oh = e.tensor_scalar(HID[:, g.par(2), q, :], iotab[:, 0:32], FLD[:, F_DHI, v], None, ALU.is_equal)
                oh.then_inc(sem("oh_built"), 1)

            steps(e, [(0, build_oh)])
            e.wait_ge(sem("idx_on_pe"), NG)
            e.tensor_copy(CNT[:, 0, :], B[0][:, 0:TILES])
            e.tensor_copy(CNT[:, 1, :], B[1][:, 0:TILES]).then_inc(sem("degrees_done"), 1)

        def pe_index(e):
            def count(g):
                gate(e, "pe", sem("oh_built"), g.times(1, 1))
                gate(e, "pe", sem("ohT_copied"), g.times(1, 0))
                first, last = g.i is None and g.c == 0, g.i is None and g.c == NG - 1
                for q in range(Q):
                    e.transpose(BT[:, q * P:(q + 1) * P], OHD[:, g.par(2), q, :], identb[:, :])
                    e.transpose(BT[:, (Q + q) * P:(Q + q + 1) * P], OHS[:, g.par(2), q, :], identb[:, :])
                for q in range(Q):
                    e.matmul(B[0][:, 0:TILES], OHS[:, g.par(2), q, :],
                             HIS[:, g.par(2), q, :],
                             start=(first and q == 0), stop=(last and q == Q - 1))
                    mm = e.matmul(B[1][:, 0:32], OHD[:, g.par(2), q, :], HID[:, g.par(2), q, :],
                                  start=(first and q == 0), stop=(last and q == Q - 1))
                mm.then_inc(sem("idx_on_pe"), 1)

            steps(e, [(1, count)])

        def act_index(e):
            def evac(g):
                gate(e, "act", sem("idx_on_pe"), g.times(1, 1))
                gate(e, "act", sem(f"ohT_out{g.slot}"), g.rounds(16))
                e.activation(OT[:, g.slot, :], BT[:, :], ACT.Copy).then_inc(sem("ohT_copied"), 1)

            steps(e, [(0, evac)])

        def sp_index(e):
            def store(g):
                gate(e, "sp", sem("ohT_copied"), g.times(1, 1))
                e.dma_start(ohT_d[bass.ds(g.times(1), 1), :, :].rearrange("g p f -> p g f"),
                            OT[:, g.slot, :].unsqueeze(1)).then_inc(sem(f"ohT_out{g.slot}"), 16)

            steps(e, [(0, store)])
            for k in range(U):
                e.wait_ge(sem(f"ohT_out{k}"), 16 * ROUNDS)

        FULL = CHUNKS - 1

        def sp_prep(e):
            dst = A["dst"]
            x_in = sem("x_in")
            e.dma_start(DST_I, dst.rearrange("(p i) -> p i", p=125)).then_inc(sem("dst_in"), 16)
            e.wait_ge(sem("cleared"), 1)
            e.dma_start(X[:, 0:TILES - 1, :], x_t[0:(TILES - 1) * P, :].rearrange("(t p) w -> p t w", p=P)).then_inc(x_in, 16)
            e.dma_start(X[0:LASTN, TILES - 1, :], x_t[(TILES - 1) * P:N, :]).then_inc(x_in, 16)
            w_in = sem("weights_in")
            n = [0]

            def load(o, i):
                e.dma_start(o, i).then_inc(w_in, 16)
                n[0] += 16

            for c, nm in enumerate(["L0_gnn_W1", "L0_gnn_W2", "L1_gnn_W_fc", "L1_gnn_W_m1", "L1_gnn_W_m2"]):
                load(WIN[:, c, :], A[nm])
            load(WIN[:, 5:7, :].rearrange("o c d -> o (c d)"), A["L3_gnn_W1"])
            load(WIN[:, 7, :], A["L3_gnn_W2"])
            for c, nm in enumerate(["L0_gnn_a_src1", "L0_gnn_a_dst1", "L0_gnn_a_src2", "L0_gnn_a_dst2"]):
                load(AV[:, c:c + 1], A[nm].unsqueeze(1))
            wat = A["L1_gnn_W_attn"]
            for c in range(6):
                load(AV[:, 4 + c:5 + c], wat[0:1, c * D:(c + 1) * D].rearrange("a o -> o a"))
            load(WE[:, 0:2], A["L1_gnn_W_edge"])
            load(WE[:, 2:3], wat[0:1, 6 * D:6 * D + 2].rearrange("a o -> o a"))
            load(WE[:, 3:3 + D], A["L1_gnn_W_e2n"].rearrange("o j -> j o"))
            for l in range(2):
                for c, nm in enumerate("qvks"):
                    load(WAUG[3 + l][0:D, c * D:(c + 1) * D], A["L2_gnn_W" + nm][l, :, :])
                    load(WAUG[3 + l][D:D + 1, c * D:(c + 1) * D], A["L2_gnn_b" + nm][l:l + 1, :])
                load(BIASR[D:D + 1, l, :], A["L2_gnn_bias"][l:l + 1, :])
            load(WAUG[5][D:D + 1, D:2 * D], A["L3_gnn_b1"].unsqueeze(0))
            for c, ap in enumerate([A["L0_gnn_b1"].unsqueeze(0), A["L0_gnn_b2"].unsqueeze(0), A["L2_gnn_gamma"][0:1, :],
                                    A["L2_gnn_gamma"][1:2, :], A["L2_gnn_beta"][0:1, :], A["L2_gnn_beta"][1:2, :],
                                    A["L3_gnn_b2"].unsqueeze(0)]):
                load(ROW[:, c, :], ap.to_broadcast([P, D]))
            assert n[0] == 16 * WEIGHT_LOADS, n[0] // 16

        WEIGHT_LOADS = 5 + 2 + 4 + 6 + 3 + 2 * 9 + 1 + 7

        def act_prep(e):
            src, dst, attr = A["src"], A["dst"], A["edge_attr_2"]
            done = sem("record_in")
            n = [0]

            def put(o, i):
                e.dma_start(o, i).then_inc(done, 16)
                n[0] += 16

            W0 = FULL * P
            dv = dst[0:W0].rearrange("(c k) -> c k", k=P)
            put(rec_d[0:FULL, 0:P], src[0:W0].rearrange("(c k) -> c k", k=P))
            put(rec_d[0:FULL, P:2 * P], dv)
            put(rec_d[0:FULL, 2 * P + 1:3 * P], dv[:, 0:P - 1])
            put(rec_d[1:FULL + 1, 2 * P:2 * P + 1], dv[:, P - 1:P])
            put(rec_d[0:FULL, 3 * P:4 * P - 1], dv[:, 1:P])
            put(rec_d[0:FULL - 1, 4 * P - 1:4 * P], dv[1:FULL, 0:1])
            put(rec_d[FULL - 1:FULL, 4 * P - 1:4 * P], dst[W0:W0 + 1].unsqueeze(0))
            put(rec_d[0:FULL, 4 * P:6 * P], attr[0:W0, :].bitcast(i32).rearrange("(c k) a -> c (k a)", k=P))
            put(rec_d[FULL:FULL + 1, 0:LASTE], src[W0:E].unsqueeze(0))
            put(rec_d[FULL:FULL + 1, P:P + LASTE], dst[W0:E].unsqueeze(0))
            put(rec_d[FULL:FULL + 1, 2 * P + 1:2 * P + LASTE], dst[W0:E - 1].unsqueeze(0))
            put(rec_d[FULL:FULL + 1, 3 * P:3 * P + LASTE - 1], dst[W0 + 1:E].unsqueeze(0))
            put(rec_d[FULL:FULL + 1, 4 * P:4 * P + 2 * LASTE], attr[W0:E, :].bitcast(i32).rearrange("k a -> (k a)").unsqueeze(0))
            e.wait_ge(sem("pad_set"), 1)
            put(rec_d[0:1, 2 * P:2 * P + 1], PADR[:, REC:REC + 1])
            put(rec_d[FULL:FULL + 1, LASTE:P], PADR[:, LASTE:P])
            put(rec_d[FULL:FULL + 1, P + LASTE:2 * P], PADR[:, P + LASTE:2 * P])
            put(rec_d[FULL:FULL + 1, 2 * P + LASTE:3 * P], PADR[:, 2 * P + LASTE:3 * P])
            put(rec_d[FULL:FULL + 1, 3 * P + LASTE - 1:4 * P], PADR[:, 3 * P + LASTE - 1:4 * P])
            put(rec_d[FULL:FULL + 1, 4 * P + 2 * LASTE:6 * P], PADR[:, 4 * P + 2 * LASTE:6 * P])
            put(rec_d[FULL + 1:FULL + 2, :], PADR[:, 0:REC])
            assert n[0] == 16 * RECORD_PUTS, n[0] // 16
            e.wait_ge(sem("walk_done"), 1)
            e.dma_start(tv_d[:, :].rearrange("k p -> p k"), TVPI[:, :]).then_inc(sem("walk_out"), 16)
            e.wait_ge(sem("walk_out"), 16)
            e.dma_start(TVR[:, :].rearrange("o (k p) -> o k p", p=P), tv_d[:, :].unsqueeze(0)).then_inc(sem("walk_in"), 16)

        RECORD_PUTS = 20

        def pool_prep(e):
            e.memset(PADR[:, 0:P], 0)
            e.memset(PADR[:, P:4 * P], 9999)
            e.memset(PADR[:, 4 * P:6 * P], 0)
            e.memset(PADR[:, REC:REC + 1], -1).then_inc(sem("pad_set"), 1)
            e.iota(ioi[:, :], [[1, P]], base=0, channel_multiplier=0)
            e.iota(iop[:, :], [[0, 1]], base=0, channel_multiplier=1)
            e.iota(VIO_I[:, :], [[P, VB]], base=0, channel_multiplier=1).then_inc(sem("iota_done"), 1)
            e.wait_ge(sem("record_in"), 16 * RECORD_PUTS)
            e.wait_ge(sem("walk_done"), 1)
            for k in range(VB):
                e.indirect_dma_start(out=REC_S[:, k, :], out_offset=None, in_=rec_d[:, :],
                                     in_offset=bass.IndirectOffsetOnAxis(ap=CVI[:, k:k + 1], axis=0)).then_inc(sem("records_in"), 16)

        def dve_prep(e, v):
            v(e.memset(X[:, TILES - 1, :], 0.0))
            e.memset(XT[D:D + 1, :], 1.0)
            e.memset(ones[:, :], 1.0)
            e.memset(zeros[:, :], 0.0)
            e.memset(FLD[:, F_XW, :], 0.0)
            for k in range(3):
                e.memset(WAUG[k][:, D:WT], 0.0)
                e.memset(WAUG[k][D:D + 1, WT:WT + 2], 0.0)
                e.memset(WAUG[k][D:D + 1, 0:D], 0.0)
            e.memset(WAUG[5][D:D + 1, 0:D], 0.0)
            e.memset(START[:, 0:32], 0.0).then_inc(sem("cleared"), 1)
            e.wait_ge(sem("cleared"), 1)
            for k in range(3):
                e.memset(WAUG[k][D:D + 1, D:WT], 1.0)
            e.wait_ge(sem("iota_done"), 1)
            e.tensor_copy(iotab[:, :], ioi[:, :])
            e.tensor_copy(iotaf[:, :], ioi[:, :])
            e.tensor_copy(VIO[:, :], VIO_I[:, :])
            v(e.tensor_copy(iopf[:, :], iop[:, :]))
            e.tensor_scalar(identb[:, :], iotab[:, :], iopf[:, :], None, ALU.is_equal)
            v(e.tensor_scalar(ident[:, :], iotaf[:, :], iopf[:, :], None, ALU.is_equal))
            v(e.tensor_scalar(lastones[:, :], ones[:, :], iopf[:, :], float(LASTN), ALU.mult, ALU.mult))
            v(e.tensor_scalar(lastones[:, :], lastones[:, :], float(LASTN * LASTN), None, ALU.is_lt))
            e.sem_inc(sem("constants_done"), 1)
            e.wait_ge(sem("dst_in"), 16)
            v(e.tensor_copy(DST_F, DST_I))
            for t in range(1, TILES):
                v(e.tensor_scalar(DST_J, DST_F, float(t * P), 0.0, ALU.is_lt, ALU.add,
                                  accum_out=START[0:125, t:t + 1]))
            e.sem_inc(sem("starts_counted"), 1)
            e.wait_ge(sem("starts_summed"), 1)
            v(e.tensor_scalar(VT_I[:, :], B[0][:, 0:32], -(P * Q / 2 - 0.5), 1.0 / (P * Q), ALU.add, ALU.mult))
            v(e.tensor_copy(VT_F[:, :], VT_I[:, :]))
            v(e.tensor_scalar(VT_F[:, :], VT_F[:, :], float(SPANS - 1), None, ALU.min))
            v(e.tensor_tensor(VT_F[:, :], VT_F[:, :], iotaf[:, 0:32], ALU.add))
            v(e.tensor_scalar(VT_F[:, :], VT_F[:, :], float(Q), None, ALU.mult))
            v(e.tensor_tensor(CMP[:, :, :], VIO[:, :].unsqueeze(2).to_broadcast([P, VB, TILES - 1]),
                              VT_F[:, 1:TILES].unsqueeze(1).to_broadcast([P, VB, TILES - 1]), ALU.is_ge))
            v(e.tensor_reduce(TVP[:, :], CMP[:, :, :], AX.X, ALU.add))
            v(e.scalar_tensor_tensor(out=CVF[:, :], in0=TVP[:, :], scalar=-float(Q), in1=VIO[:, :], op0=ALU.mult, op1=ALU.add))
            v(e.tensor_scalar(CVF[:, :], CVF[:, :], float(CHUNKS), None, ALU.min))
            e.tensor_copy(TVPI[:, :], TVP[:, :])
            v(e.tensor_copy(CVI[:, :], CVF[:, :]))
            e.sem_inc(sem("walk_done"), 1)
            e.wait_ge(sem("records_in"), 16 * VB)
            f = lambda k: VF[:, k, :, :]
            rec = lambda k: REC_S[:, :, k * P:(k + 1) * P]
            tv = TVP[:, :].unsqueeze(2).to_broadcast([P, VB, P])
            HII = REC_S[:, :, 2 * P:3 * P]
            e.tensor_copy(f(F_SRC), rec(0))
            e.tensor_copy(f(F_DREL), rec(1))
            e.tensor_copy(f(F_RST), rec(2))
            e.tensor_copy(f(F_EREL), rec(3))
            e.tensor_copy(f(F_A0), REC_S[:, :, 4 * P:6 * P].bitcast(f32).rearrange("p v (k a) -> p v k a", a=2)[:, :, :, 0])
            v(e.tensor_copy(f(F_A1), REC_S[:, :, 4 * P:6 * P].bitcast(f32).rearrange("p v (k a) -> p v k a", a=2)[:, :, :, 1]))
            e.tensor_tensor(f(F_RST), f(F_DREL), f(F_RST), ALU.not_equal)
            e.tensor_tensor(f(F_EREL), f(F_DREL), f(F_EREL), ALU.is_equal)
            v(e.tensor_scalar(HII, f(F_SRC), -(P / 2 - 0.5), 1.0 / P, ALU.add, ALU.mult))
            v(e.tensor_copy(f(F_SHI), HII))
            v(e.tensor_scalar(f(F_SLO), f(F_SHI), -float(P), None, ALU.mult))
            v(e.tensor_tensor(f(F_SLO), f(F_SLO), f(F_SRC), ALU.add))
            v(e.tensor_scalar(f(F_DHI), tv, -float(P), None, ALU.mult))
            v(e.tensor_tensor(f(F_DREL), f(F_DREL), f(F_DHI), ALU.add))
            e.tensor_scalar(ENDV[:, :, :], f(F_EREL), 0.0, -BIG, ALU.is_equal, ALU.mult)
            v(e.scalar_tensor_tensor(out=f(F_EREL), in0=f(F_EREL), scalar=20000.0, in1=f(F_DREL), op0=ALU.mult, op1=ALU.add))
            e.tensor_scalar(RSTV[:, :, :], f(F_RST), -BIG, None, ALU.mult)
            v(e.tensor_scalar(f(F_RST), f(F_RST), -BIG, None, ALU.mult))
            for k in range(VB):
                e.tensor_tensor_scan(PM[:, k, :], zeros[:, :], RSTV[:, k, :], 0.0, ALU.add, ALU.min)
                v(e.tensor_tensor_scan(SMK[:, k, ::-1], zeros[:, :], ENDV[:, k, ::-1], 0.0, ALU.add, ALU.min))
            v(e.tensor_scalar(f(F_XW), f(F_DREL), 0.0, None, ALU.is_lt))
            v(e.tensor_scalar(f(F_DHI), f(F_DREL), float(P), None, ALU.is_ge))
            v(e.tensor_tensor(f(F_XW), f(F_XW), f(F_DHI), ALU.add))
            v(e.scalar_tensor_tensor(out=f(F_SHI), in0=f(F_XW), scalar=1000.0, in1=f(F_SHI), op0=ALU.mult, op1=ALU.add))
            v(e.scalar_tensor_tensor(out=f(F_DHI), in0=f(F_XW), scalar=1000.0, in1=tv, op0=ALU.mult, op1=ALU.add))
            e.sem_inc(sem("fields_done"), 1)
            r = 0
            for fl in FIELDS:
                for b0 in range(0, VB, 4):
                    e.wait_ge(sem("fields_on_pe"), r + 1)
                    w = min(4, VB - b0) * P
                    e.tensor_copy(FLD[:, fl, b0 * P:b0 * P + w], B[r % 2][:, 0:w]).then_inc(sem("fields_copied"), 1)
                    r += 1
            for k, row in enumerate([HASR, HASE]):
                e.wait_ge(sem("flags_row"), k + 1)
                e.tensor_copy(row[:, 0:4 * P], B[4][0:1, :])
                e.tensor_copy(row[:, 4 * P:VP], B[5][0:1, 0:VP - 4 * P]).then_inc(sem("flags_copied"), 1)
            e.wait_ge(sem("weights_in"), 16 * WEIGHT_LOADS)
            for l in range(2):
                e.tensor_tensor(WAUG[3 + l][D:D + 1, 3 * D:4 * D], WAUG[3 + l][D:D + 1, 3 * D:4 * D], BIASR[D:D + 1, l, :], ALU.add)
                e.tensor_copy(WAUG[l][0:D, 0:D], WIN[:, l, :])
            e.wait_ge(sem("weights_turned"), 1)
            e.tensor_copy(WTT[:, :, :].rearrange("p c d -> p (c d)"), B[4][0:D, 0:6 * D]).then_inc(sem("turned_copied"), 1)
            e.wait_ge(sem("turned_copied"), 1)
            e.tensor_copy(WAUG[2][0:D, 0:D], WTT[:, 2, :])
            e.tensor_copy(WAUG[5][0:D, 0:D], WTT[:, 4, :])
            e.tensor_tensor(WAUG[5][0:D, D:2 * D], WTT[:, 3, :], WTT[:, 4, :], ALU.subtract)
            e.tensor_copy(W2T[:, :], WTT[:, 5, :])
            e.wait_ge(sem("weights_folded"), 1)
            for l in range(3):
                e.tensor_copy(WAUG[l][0:D, WT:WT + 2], B[5][0:D, 2 * l:2 * l + 2])
            e.tensor_copy(WES[:, :], B[6][:, 0:2 + 2 * D])
            v(e.tensor_copy(UV[:, :, :].rearrange("p c d -> p (c d)"), B[6][:, 256:512]))
            e.sem_inc(sem("weights_ready"), 1)

        FIELDS = [F_SRC, F_DREL, F_EREL, F_RST, F_A0, F_A1, F_SHI, F_DHI, F_SLO]

        def pe_prep(e):
            e.wait_ge(sem("starts_counted"), 1)
            e.matmul(B[0][:, 0:32], ones[0:125, :], START[0:125, :], start=True, stop=True).then_inc(sem("starts_summed"), 1)
            e.wait_ge(sem("fields_done"), 1)
            r = 0
            for fl in FIELDS:
                for b0 in range(0, VB, 4):
                    if r >= 2:
                        e.wait_ge(sem("fields_copied"), r - 1)
                    for b in range(b0, min(b0 + 4, VB)):
                        mm = e.transpose(B[r % 2][:, (b - b0) * P:(b - b0 + 1) * P], VF[:, fl, b, :], ident[:, :])
                    mm.then_inc(sem("fields_on_pe"), 1)
                    r += 1
            row_out(e, lambda k: PM[:, k, P - 1:P], "flags_row")
            e.wait_ge(sem("flags_copied"), 1)
            row_out(e, lambda k: SMK[:, k, 0:1], "flags_row")
            e.wait_ge(sem("flags_copied"), 2)
            e.wait_ge(sem("weights_in"), 16 * WEIGHT_LOADS)
            for k, c in enumerate([0, 1, 2, 5, 6, 7]):
                mm = e.transpose(B[4][0:D, k * D:(k + 1) * D], WIN[:, c, :], ident[0:D, 0:D])
            mm.then_inc(sem("weights_turned"), 1)
            e.wait_ge(sem("turned_copied"), 1)
            e.matmul(B[5][0:D, 0:2], WTT[:, 0, :], AV[:, 0:2], start=True, stop=True)
            e.matmul(B[5][0:D, 2:4], WTT[:, 1, :], AV[:, 2:4], start=True, stop=True)
            e.matmul(B[5][0:D, 4:6], WIN[:, 2, :], AV[:, 4:8:3], start=True, stop=True)
            e.matmul(B[6][:, 0:2], WE[:, 2:3].to_broadcast([2, P]), WE[:, 0:2], start=True, stop=True)
            for i in range(2):
                e.matmul(B[6][:, 2 + i * D:2 + (i + 1) * D], WE[:, i:i + 1].to_broadcast([2, P]), WE[:, 3:3 + D], start=True, stop=True)
            for k, (blk, wm) in enumerate([(1, 3), (2, 4), (4, 3), (5, 4)]):
                mm = e.matmul(B[6][:, 256 + k * D:256 + (k + 1) * D], AV[:, 4 + blk:5 + blk].to_broadcast([D, P]), WIN[:, wm, :],
                              start=True, stop=True)
            mm.then_inc(sem("weights_folded"), 1)

        WIDE = [WT + 2] * 3 + [4 * D] * 2 + [2 * D]
        PER = [512 // w for w in WIDE]
        PROJ = [-(-TILES // k) for k in PER]
        PBASE = [sum(PROJ[:k]) for k in range(7)]
        TURNS = -(-TILES // 4)
        XIN = [X, X1, X, X, X1, X]

        def pe_project(e, n):
            e.wait_ge(sem("x_ready"), n + 1)
            for k in range(TURNS):
                if k >= 2:
                    e.wait_ge(sem("xT_copied"), n * TURNS + k - 1)
                for t in range(4 * k, min(4 * k + 4, TILES)):
                    mm = e.transpose(B[k % 2][0:D, (t % 4) * P:(t % 4 + 1) * P], XIN[n][:, t, :], ident[:, :])
                mm.then_inc(sem("xT_on_pe"), 1)
            if n == 0:
                e.wait_ge(sem("weights_ready"), 1)
            for k in range(PROJ[n]):
                last = min((k + 1) * PER[n], TILES) - 1
                e.wait_ge(sem("xT_copied"), n * TURNS + last // 4 + 1)
                if k >= 2:
                    e.wait_ge(sem("proj_copied"), PBASE[n] + k - 1)
                for t in range(k * PER[n], last + 1):
                    o = (t - k * PER[n]) * WIDE[n]
                    mm = e.matmul(B[2 + k % 2][:, o:o + WIDE[n]], XT[:, t * P:(t + 1) * P], WAUG[n][:, :], start=True, stop=True)
                mm.then_inc(sem("proj_on_pe"), 1)

        def act_project(e, n):
            for k in range(TURNS):
                e.wait_ge(sem("xT_on_pe"), n * TURNS + k + 1)
                w = (min(4 * k + 4, TILES) - 4 * k) * P
                e.activation(XT[0:D, k * 4 * P:k * 4 * P + w], B[k % 2][0:D, 0:w], ACT.Copy).then_inc(sem("xT_copied"), 1)

        def dve_project(e, v, n):
            for k in range(PROJ[n]):
                e.wait_ge(sem("proj_on_pe"), PBASE[n] + k + 1)
                t0, t1 = k * PER[n], min((k + 1) * PER[n], TILES)
                bank = B[2 + k % 2][:, 0:(t1 - t0) * WIDE[n]].rearrange("p (t w) -> p t w", w=WIDE[n])
                if KINDS[n] == "A":
                    e.tensor_copy(TB[:, t0:t1, 0:WT], bank[:, :, 0:WT])
                    e.tensor_copy(AS[:, t0:t1], bank[:, :, WT])
                    e.tensor_copy(KF[:, t0:t1, 0:1], bank[:, :, WT + 1:WT + 2]).then_inc(sem("proj_copied"), 1)
                elif KINDS[n] == "B":
                    e.tensor_copy(TB[:, t0:t1, :], bank[:, :, 0:2 * D])
                    e.tensor_copy(KF[:, t0:t1, :], bank[:, :, 2 * D:3 * D])
                    e.tensor_copy(ROOT[:, t0:t1, :], bank[:, :, 3 * D:4 * D]).then_inc(sem("proj_copied"), 1)
                else:
                    e.tensor_copy(TB[:, t0:t1, 0:D], bank[:, :, 0:D])
                    e.tensor_copy(KF[:, t0:t1, :], bank[:, :, D:2 * D]).then_inc(sem("proj_copied"), 1)
            e.wait_ge(sem("proj_copied"), PBASE[n + 1])
            if n == 2:
                moments(e, v)
            w = 1 if KINDS[n] == "A" else D
            r = T1[:, :, 0:w]
            kf = KF[:, :, 0:w]
            v(e.tensor_copy(KS[:, :, 0, 0:w], kf))
            v(e.tensor_tensor(r, kf, KS[:, :, 0, 0:w], ALU.subtract))
            v(e.tensor_copy(KS[:, :, 1, 0:w], r))
            v(e.tensor_tensor(r, r, KS[:, :, 1, 0:w], ALU.subtract))
            v(e.tensor_copy(KS[:, :, 2, 0:w], r))
            if KINDS[n] == "A":
                rs = NV[:, 0, :]
                v(e.tensor_copy(ATB[:, 0, :], AS[:, :]))
                v(e.tensor_tensor(rs, AS[:, :], ATB[:, 0, :], ALU.subtract))
                v(e.tensor_copy(ATB[:, 1, :], rs))
                v(e.tensor_tensor(rs, rs, ATB[:, 1, :], ALU.subtract))
                e.tensor_copy(ATB[:, 2, :], rs)
            e.memset(ACC[:, :, :], 0.0)
            if n == 2:
                e.tensor_scalar(FLD[:, F_XW, :], FLD[:, F_A0, :], WES[:, 0:1], None, ALU.mult).then_inc(sem("edge_term"), 1)
                e.wait_ge(sem("edge_term"), 1)
                e.scalar_tensor_tensor(out=FLD[:, F_XW, :], in0=FLD[:, F_A1, :], scalar=WES[:, 1:2], in1=FLD[:, F_XW, :],
                                       op0=ALU.mult, op1=ALU.add)
            e.memset(CONST[:, :], 0.0).then_inc(sem("parts_ready"), 1)
            e.wait_ge(sem("parts_ready"), n + 1)

        def sp_table(e, n):
            w = TW[n]
            e.wait_ge(sem("proj_copied"), PBASE[n + 1])
            e.dma_start(tiled(tabs[n][:, :]), TB[:, :, 0:w]).then_inc(sem("table_written"), 16)
            e.wait_ge(sem("table_written"), 16 * (n + 1))

        def sums_pe(e, src, bank, o, masked):
            for t in range(TILES):
                lhs = lastones if masked and t == TILES - 1 else ones
                mm = e.matmul(bank[:, o:o + D], lhs[:, :], src[:, t, :], start=(t == 0), stop=(t == TILES - 1))
            mm.then_inc(sem("summed"), 1)

        def per_node(ap):
            return ap.unsqueeze(2).to_broadcast([P, TILES, D])

        def per_feat(ap):
            return ap.unsqueeze(1).to_broadcast([P, TILES, D])

        Z = TB[:, :, 0:D]

        def pe_moments(e):
            for s in range(2):
                e.wait_ge(sem("weighted_z"), s + 1)
                sums_pe(e, T1, B[4], s * D, False)
            for s in range(2):
                e.wait_ge(sem("powers_z"), s + 1)
                sums_pe(e, T2, B[5], (2 * s) * D, False)
                sums_pe(e, T1, B[5], (2 * s + 1) * D, False)

        def moments(e, v):
            for s in range(2):
                v(e.tensor_tensor(T1[:, :, :], Z, per_node(CNT[:, s, :]), ALU.mult))
                e.sem_inc(sem("weighted_z"), 1)
                e.wait_ge(sem("summed"), s + 1)
            v(e.tensor_scalar(MU[:, :, :].rearrange("p s d -> p (s d)"), B[4][:, 0:2 * D], 1.0 / E, None, ALU.mult))
            for s in range(2):
                v(e.tensor_tensor(T1[:, :, :], Z, per_feat(MU[:, s, :]), ALU.subtract))
                v(e.tensor_tensor(T2[:, :, :], T1[:, :, :], T1[:, :, :], ALU.mult))
                v(e.tensor_tensor(T2[:, :, :], T2[:, :, :], per_node(CNT[:, s, :]), ALU.mult))
                v(e.tensor_tensor(T1[:, :, :], T1[:, :, :], T2[:, :, :], ALU.mult))
                e.sem_inc(sem("powers_z"), 1)
                e.wait_ge(sem("summed"), 2 + 2 * s + 2)
            mk = MK[:, :, :].rearrange("p s d -> p (s d)")
            a = MK2[:, :, :].rearrange("p s d -> p (s d)")
            b = MK3[:, :, :].rearrange("p s d -> p (s d)")
            v(e.tensor_scalar(mk, B[5][:, 0:4 * D], 1.0 / E, None, ALU.mult))
            v(e.tensor_scalar(a, mk, -1.0, None, ALU.mult))
            v(e.tensor_tensor(a, a, mk, ALU.max))
            v(e.tensor_scalar(a, a, 1e-18, None, ALU.max))
            e.sem_inc(sem("moments_in"), 1)
            v(e.tensor_scalar(b, mk, 0.0, None, ALU.is_gt))
            v(e.tensor_scalar(mk, mk, 0.0, None, ALU.is_lt))
            v(e.tensor_tensor(b, b, mk, ALU.subtract))
            e.wait_ge(sem("roots_done"), 1)
            v(e.tensor_tensor(b, b, a, ALU.mult))
            v(e.tensor_tensor(b, b, UV[:, :, :].rearrange("p s d -> p (s d)"), ALU.mult))
            v(e.tensor_reduce(CONST[:, :], b, AX.X, ALU.add))
            v(e.tensor_scalar(KF[:, :, 0], KF[:, :, 0], CONST[:, :], None, ALU.add))

        def act_moments(e):
            e.wait_ge(sem("moments_in"), 1)
            a = MK2[:, :, :].rearrange("p (s k) d -> p s k d", k=2)
            e.activation(a[:, :, 0, :], a[:, :, 0, :], ACT.Sqrt)
            e.activation(a[:, :, 1, :], a[:, :, 1, :], ACT.Ln).then_inc(sem("log_done"), 1)
            e.wait_ge(sem("log_done"), 1)
            e.activation(a[:, :, 1, :], a[:, :, 1, :], ACT.Exp, scale=1.0 / 3).then_inc(sem("roots_done"), 1)

        def layernorm(e, v, last_n):
            v(e.tensor_tensor(T1[:, :, :], T1[:, :, :], X[:, :, :], ALU.add))
            v(e.tensor_reduce(NV[:, 0, :], T1[:, :, :], AX.X, ALU.add))
            v(e.tensor_scalar(NV[:, 0, :], NV[:, 0, :], 1.0 / D, None, ALU.mult))
            v(e.tensor_tensor(T1[:, :, :], T1[:, :, :], per_node(NV[:, 0, :]), ALU.subtract))
            v(e.tensor_tensor(T2[:, :, :], T1[:, :, :], T1[:, :, :], ALU.mult))
            v(e.tensor_reduce(NV[:, 1, :], T2[:, :, :], AX.X, ALU.add))
            v(e.tensor_scalar(NV[:, 1, :], NV[:, 1, :], 1.0 / D, LN_EPS, ALU.mult, ALU.add))
            e.sem_inc(sem("ln_var"), 1)
            e.wait_ge(sem("ln_root"), last_n + 1)
            v(e.reciprocal(NV[:, 3, :], NV[:, 2, :]))
            v(e.tensor_tensor(X[:, :, :], T1[:, :, :], per_node(NV[:, 3, :]), ALU.mult))

        def act_layernorm(e, k):
            e.wait_ge(sem("ln_var"), k + 1)
            e.activation(NV[:, 2, :], NV[:, 1, :], ACT.Sqrt).then_inc(sem("ln_root"), 1)

        def dve_finish(e, v, n):
            e.wait_ge(sem("sums_added"), (n + 1) * NG)
            nv = lambda k: NV[:, k, :]
            if n < 2:
                z, r = ACC[:, :, D], NV[:, 1, :]
                v(e.tensor_tensor(nv(0), AS[:, :], KF[:, :, 0], ALU.add))
                v(e.scalar_tensor_tensor(out=nv(0), in0=nv(0), scalar=0.2, in1=nv(0), op0=ALU.mult, op1=ALU.max))
                v(e.tensor_scalar(nv(2), z, 0.0, None, ALU.is_le))
                v(e.tensor_tensor(nv(1), z, nv(2), ALU.add))
                v(e.reciprocal(nv(3), nv(1)))
                v(e.tensor_tensor(nv(1), ACC[:, :, WA - 1], nv(3), ALU.mult))
                v(e.scalar_tensor_tensor(out=nv(2), in0=nv(2), scalar=-BIG, in1=r, op0=ALU.mult, op1=ALU.add))
                v(e.tensor_tensor(nv(3), nv(2), nv(0), ALU.max))
                v(e.tensor_tensor(nv(4), nv(2), nv(3), ALU.subtract))
                v(e.tensor_tensor(nv(5), nv(0), nv(3), ALU.subtract))
                e.sem_inc(sem("self_in"), 1)
                e.wait_ge(sem("self_out"), n + 1)
                v(e.tensor_tensor(nv(1), z, nv(6), ALU.mult))
                v(e.tensor_tensor(nv(1), nv(1), nv(7), ALU.add))
                v(e.tensor_scalar(nv(1), nv(1), 1e-16, None, ALU.add))
                v(e.reciprocal(nv(2), nv(1)))
                v(e.tensor_tensor(T1[:, :, :], ACC[:, :, 0:D], per_node(nv(6)), ALU.mult))
                v(e.tensor_tensor(T2[:, :, :], TB[:, :, 0:D], per_node(nv(7)), ALU.mult))
                v(e.tensor_tensor(T1[:, :, :], T1[:, :, :], T2[:, :, :], ALU.add))
                v(e.tensor_tensor(T1[:, :, :], T1[:, :, :], per_node(nv(2)), ALU.mult))
                v(e.tensor_tensor(T1[:, :, :], T1[:, :, :], per_feat(ROW[:, n, :]), ALU.add))
                if n == 0:
                    v(e.tensor_scalar(X1[:, :, :], T1[:, :, :], 0.0, None, ALU.max))
                else:
                    layernorm(e, v, 0)
            elif n == 2:
                z = ACC[:, :, D]
                v(e.tensor_scalar(nv(0), z, 0.0, None, ALU.is_le))
                v(e.tensor_tensor(nv(0), nv(0), z, ALU.add))
                v(e.reciprocal(nv(1), nv(0)))
                v(e.tensor_copy(T1[:, :, :], ACC[:, :, 0:D]))
                for i in range(2):
                    v(e.tensor_tensor(T2[:, :, :], per_node(ACC[:, :, D + 1 + i]), per_feat(WES[:, 2 + i * D:2 + (i + 1) * D]), ALU.mult))
                    v(e.tensor_tensor(T1[:, :, :], T1[:, :, :], T2[:, :, :], ALU.add))
                v(e.tensor_tensor(T1[:, :, :], T1[:, :, :], per_node(nv(1)), ALU.mult))
                layernorm(e, v, 1)
            elif n < 5:
                l = n - 3
                v(e.tensor_tensor(T1[:, :, :], ACC[:, :, 0:D], ROOT[:, :, :], ALU.add))
                v(e.tensor_scalar(T1[:, :, :], T1[:, :, :], 0.0, None, ALU.max))
                e.sem_inc(sem("bn_in"), 1)
                e.wait_ge(sem("summed"), 6 + 2 * l + 1)
                v(e.tensor_scalar(BN[:, 0, :], B[4][:, 0:D], 1.0 / N, None, ALU.mult))
                v(e.tensor_tensor(T1[:, :, :], T1[:, :, :], per_feat(BN[:, 0, :]), ALU.subtract))
                v(e.tensor_tensor(T2[:, :, :], T1[:, :, :], T1[:, :, :], ALU.mult))
                e.sem_inc(sem("bn_sq"), 1)
                e.wait_ge(sem("summed"), 6 + 2 * l + 2)
                v(e.tensor_scalar(BN[:, 1, :], B[5][:, 0:D], 1.0 / N, BN_EPS, ALU.mult, ALU.add))
                e.sem_inc(sem("bn_var"), 1)
                e.wait_ge(sem("bn_root"), l + 1)
                v(e.reciprocal(BN[:, 3, :], BN[:, 2, :]))
                v(e.tensor_tensor(BN[:, 3, :], BN[:, 3, :], ROW[:, 2 + l, :], ALU.mult))
                v(e.tensor_tensor(T1[:, :, :], T1[:, :, :], per_feat(BN[:, 3, :]), ALU.mult))
                dst = X1 if l == 0 else T1
                v(e.tensor_tensor(dst[:, :, :], T1[:, :, :], per_feat(ROW[:, 4 + l, :]), ALU.add))
                if l == 1:
                    layernorm(e, v, 2)
            else:
                v(e.tensor_scalar(nv(0), CNT[:, 1, :], 0.0, None, ALU.is_gt))
                v(e.tensor_tensor(T1[:, :, :], ACC[:, :, 0:D], per_feat(ROW[:, 6, :]), ALU.add))
                v(e.tensor_tensor(T1[:, :, :], T1[:, :, :], per_node(nv(0)), ALU.mult))
                layernorm(e, v, 3)
            e.sem_inc(sem("x_ready"), 1)

        def pe_finish(e, n):
            if n in (3, 4):
                e.wait_ge(sem("bn_in"), n - 2)
                sums_pe(e, T1, B[4], 0, True)
                e.wait_ge(sem("bn_sq"), n - 2)
                sums_pe(e, T2, B[5], 0, True)

        def act_finish(e, n):
            if n < 2:
                e.wait_ge(sem("self_in"), n + 1)
                e.activation(NV[:, 6, :], NV[:, 4, :], ACT.Exp)
                e.activation(NV[:, 7, :], NV[:, 5, :], ACT.Exp).then_inc(sem("self_out"), 1)
            if n in (3, 4):
                e.wait_ge(sem("bn_var"), n - 2)
                e.activation(BN[:, 2, :], BN[:, 1, :], ACT.Sqrt).then_inc(sem("bn_root"), 1)
            if n in (1, 2, 4, 5):
                act_layernorm(e, {1: 0, 2: 1, 4: 2, 5: 3}[n])

        @block.gpsimd
        def _(e):
            pool_prep(e)
            for n in range(6):
                pool_pass(e, n)

        @block.sync
        def _(e):
            sp_prep(e)
            sp_index(e)
            for n in range(6):
                sp_table(e, n)
                sp_stream(e, n)
            e.wait_ge(sem("x_ready"), 7)
            e.dma_start(out[0:(TILES - 1) * P, :].rearrange("(t p) w -> p t w", p=P), X[:, 0:TILES - 1, :]).then_inc(sem("result_out"), 16)
            e.dma_start(out[(TILES - 1) * P:N, :], X[0:LASTN, TILES - 1, :]).then_inc(sem("result_out"), 16)
            e.wait_ge(sem("result_out"), 32)

        @block.tensor
        def _(e):
            pe_prep(e)
            pe_index(e)
            e.wait_ge(sem("walk_in"), 16)
            for n in range(6):
                pe_project(e, n)
                if n == 2:
                    pe_moments(e)
                if KINDS[n] == "A":
                    pe_scores(e, n)
                    pe_segments(e, n)
                pe_pass(e, n)
                pe_finish(e, n)

        @block.scalar
        def _(e):
            act_prep(e)
            act_index(e)
            for n in range(6):
                act_project(e, n)
                if n == 2:
                    act_moments(e)
                if KINDS[n] == "A":
                    act_segments(e, n)
                act_pass(e, n)
                act_finish(e, n)

        @block.vector
        def _(e):
            v = Own(e, "dve_done")
            dve_prep(e, v)
            dve_index(e)
            e.wait_ge(sem("degrees_done"), 1)
            e.wait_ge(sem("x_in"), 32)
            e.wait_ge(sem("walk_in"), 16)
            e.sem_inc(sem("x_ready"), 1)
            for n in range(6):
                dve_project(e, v, n)
                if KINDS[n] == "A":
                    dve_scores(e, n)
                    dve_segments(e, v, n)
                dve_pass(e, n)
                dve_finish(e, v, n)


_INS = ["x", "src", "dst", "edge_attr_2", "L0_gnn_W1", "L0_gnn_a_src1", "L0_gnn_a_dst1", "L0_gnn_b1", "L0_gnn_W2",
        "L0_gnn_a_src2", "L0_gnn_a_dst2", "L0_gnn_b2", "L1_gnn_W_fc", "L1_gnn_W_attn", "L1_gnn_W_edge", "L1_gnn_W_e2n",
        "L1_gnn_W_m1", "L1_gnn_W_m2", "L2_gnn_Wk", "L2_gnn_bk", "L2_gnn_Wq", "L2_gnn_bq", "L2_gnn_Wv", "L2_gnn_bv",
        "L2_gnn_Ws", "L2_gnn_bs", "L2_gnn_bias", "L2_gnn_gamma", "L2_gnn_beta", "L3_gnn_W1", "L3_gnn_b1", "L3_gnn_W2",
        "L3_gnn_b2"]


def kernel(**inputs):
    import numpy as _np
    import concourse.bacc as _bacc
    from concourse import mybir as _mybir
    from concourse.bass_utils import run_bass_kernel_spmd as _run

    nc = _bacc.Bacc("TRN2", target_bir_lowering=False, num_devices=1)
    arrays, args = {}, {}
    for name in _INS:
        a = _np.ascontiguousarray(inputs[name])
        arrays[f"in_{name}"] = a
        args[name] = nc.dram_tensor(f"in_{name}", a.shape, _mybir.dt.from_np(a.dtype), kind="ExternalInput").ap()
    result = nc.dram_tensor("out_0", (N, D), _mybir.dt.float32, kind="ExternalOutput").ap()
    build(nc, args, result)
    r = _run(nc, [arrays], core_ids=[0])
    return r.results[0]["out_0"]
```

```python
import concourse.bass as bass
from concourse import mybir
from contextlib import ExitStack

f32 = mybir.dt.float32
i32 = mybir.dt.int32
u32 = mybir.dt.uint32
bf16 = mybir.dt.bfloat16
ALU = mybir.AluOpType
ACT = mybir.ActivationFunctionType
AX = mybir.AxisListType

P = 128
N, E, D = 3125, 100000, 64
TILES = -(-N // P)
assert TILES % 8 == 1
LASTN = N - (TILES - 1) * P
CHUNKS = -(-E // P)
LASTE = E - (CHUNKS - 1) * P
Q = 4
SPANS = -(-CHUNKS // Q)
U = 4
NG = -(-(SPANS + TILES - 1) // U) * U
KEPT = NG // 2
VB = -(-NG * Q // P)
VP = VB * P
REC = 6 * P
NF = 11
F_SRC, F_DREL, F_EREL, F_A0, F_A1, F_M, F_XW, F_SHI, F_W, F_SLO, F_S = range(NF)
WT = D + 1
WA = WT + 3
TW = [WT, WT, WT, 2 * D, 2 * D, D]
BIG = 1e30
LN_EPS = 1e-5
BN_EPS = 1e-5


class At:

    def __init__(self, c, i=None):
        self.c, self.i = c, i

    def times(self, m, a=0):
        return self.c * m + a if self.i is None else self.i * (m * U) + (self.c * m + a)

    def rounds(self, m, a=0):
        return (self.c // U) * m + a if self.i is None else self.i * m + ((self.c // U) * m + a)

    @property
    def slot(self):
        return self.c % U

    def par(self, n):
        return self.c % n


def steps(e, stages, count=NG, after_head=None):
    top = max(lag for lag, _ in stages)
    first = -(-(top + U) // U) * U

    def one(c, i=None):
        for lag, fn in stages:
            if i is not None or 0 <= c - lag < count:
                fn(At(c - lag, i))

    for s in range(first):
        one(s)
    if after_head is not None:
        after_head()
    rounds = (count - first) // U
    with e.Fori(0, rounds) as i:
        for k in range(U):
            one(first + k, i)
    for s in range(first + rounds * U, count + top):
        one(s)


def build(nc, A, out):
    ctx = ExitStack()
    with ctx, nc.allow_non_contiguous_dma(reason="small columns and transposed weights"):
        def sb(name, shape, dt=f32):
            return ctx.enter_context(nc.sbuf_tensor(name, shape, dt))

        def pb(name, shape, dt=f32):
            return ctx.enter_context(nc.psum_tensor(name, shape, dt))

        made = {}

        def sem(name):
            if name not in made:
                made[name] = ctx.enter_context(nc.semaphore(name))
            return made[name]

        class Own:

            def __init__(self, e, name):
                self.e, self.sem, self.n = e, sem(name), 0

            def done(self, ins):
                self.n += 1
                ins.then_inc(self.sem, 1)

            def wait(self):
                if self.n:
                    self.e.wait_ge(self.sem, self.n)

            def __call__(self, ins):
                self.done(ins)
                self.wait()

        def gate(e, who, s, val):
            if isinstance(val, int):
                if val > 0:
                    e.wait_ge(s, val)
            else:
                e.wait_ge(s, val)
                e.sem_inc(sem("passed_" + who), 1)

        def hold(e, s, val):
            if not isinstance(val, int) or val > 0:
                e.wait_ge(s, val)

        rec_d = nc.dram_tensor("rec_d", [CHUNKS + 1, REC], i32)
        rows_d = nc.dram_tensor("rows_d", [3, VP * P], bf16)
        tv_d = nc.dram_tensor("tv_d", [VB, P], i32)
        kept_d = nc.dram_tensor("kept_d", [KEPT, P, Q * WT], f32)
        tabs = [nc.dram_tensor(f"tab{k}_d", [TILES * P, w], f32) for k, w in enumerate(TW)]

        X = sb("X", [P, TILES, D])
        X1 = sb("X1", [P, TILES, D])
        TB = sb("TB", [P, TILES, 128])
        KF = sb("KF", [P, TILES, D])
        KS = sb("KS", [P, TILES, 3, D], bf16)
        ROOT = sb("ROOT", [P, TILES, D])
        ACC = sb("ACC", [P, TILES, WA])
        T1 = sb("T1", [P, TILES, D])
        T2 = sb("T2", [P, TILES, D])
        NV = sb("NV", [P, 8, TILES])
        XT = sb("XT", [D + 1, TILES * P])
        WAUG = [sb(f"WAUG{k}", [D + 1, w]) for k, w in enumerate([WT + 2] * 3 + [4 * D] * 2 + [2 * D])]
        WIN = sb("WIN", [D, 8, D])
        WTT = sb("WTT", [D, 6, D])
        W2T = sb("W2T", [D, D])
        AV = sb("AV", [D, 10])
        WE = sb("WE", [2, 2 + 1 + D])
        WES = sb("WES", [P, 2 + 2 * D])
        BIASR = sb("BIASR", [D + 1, 2, D])
        ROW = sb("ROW", [P, 7, D])
        UV = sb("UV", [P, 4, D])
        MU = sb("MU", [P, 2, D])
        MK = sb("MK", [P, 4, D])
        MK2 = sb("MK2", [P, 4, D])
        MK3 = sb("MK3", [P, 4, D])
        CONST = sb("CONST", [P, 1])
        BN = sb("BN", [P, 4, D])
        ident = sb("ident", [P, P])
        ones = sb("ones", [P, P])
        lastones = sb("lastones", [P, P])
        iotab = sb("iotab", [P, P], bf16)
        iotaf = sb("iotaf", [P, P])
        iopf = sb("iopf", [P, 1])
        FLD = sb("FLD", [P, NF, VP])
        TVR = sb("TVR", [1, VP], i32)
        AS = sb("AS", [P, TILES])
        ATB = sb("ATB", [P, 3, TILES], bf16)
        zeros = sb("zeros", [P, P])
        RSTV = sb("RSTV", [P, VB, P])
        ENDV = sb("ENDV", [P, VB, P])
        PM = sb("PM", [P, VB, P])
        SMK = sb("SMK", [P, VB, P])
        HASR = sb("HASR", [1, VP])
        HASE = sb("HASE", [1, VP])
        CINS = sb("CINS", [P, 2, VB])
        CNT = sb("CNT", [P, 2, TILES])

        prep = ExitStack()

        def tmp(name, shape, dt=f32):
            return prep.enter_context(nc.sbuf_tensor(name, shape, dt))

        ioi = tmp("ioi", [P, P], i32)
        iop = tmp("iop", [P, 1], i32)
        flat = lambda T: T[:, :, :].rearrange("p t d -> p (t d)")
        DST_I = flat(ROOT)[0:125, 0:E // 125].bitcast(i32)
        DST_F = flat(T1)[0:125, 0:E // 125]
        DST_J = flat(T2)[0:125, 0:E // 125]
        START = tmp("START", [P, 32])
        VT_F = tmp("VT_F", [P, 32])
        VT_I = tmp("VT_I", [P, 32], i32)
        VIO_I = tmp("VIO_I", [P, VB], i32)
        VIO = tmp("VIO", [P, VB])
        CMP = tmp("CMP", [P, VB, TILES - 1])
        TVP = tmp("TVP", [P, VB])
        TVPI = tmp("TVPI", [P, VB], i32)
        CVF = tmp("CVF", [P, VB])
        CVI = tmp("CVI", [P, VB], u32)
        RB = tmp("RB", [P, 3, VB, P], bf16)
        PADR = tmp("PADR", [1, REC + 1], i32)
        REC_S = flat(FLD)[:, 0:VB * REC].bitcast(i32).rearrange("p (v r) -> p v r", r=REC)
        VF = tmp("VF", [P, NF - 1, VB, P])
        prep.close()

        IDX = sb("IDX", [P, U, Q], u32)
        G = sb("G", [P, U, Q, 128])
        ROWB = sb("ROWB", [P, U, 2 * Q * P], bf16)
        OT = sb("OT", [P, 2, 2 * Q * P], bf16)
        OHC = sb("OHC", [P, 4, Q * P], bf16)
        OHN = OHC[:, 0:2, :].rearrange("p a (q i) -> p a q i", q=Q)
        RSTB = OHC[0:D, :, :]
        HIS = sb("HIS", [P, Q, TILES], bf16)
        THOT = sb("THOT", [P, 2, Q, TILES], bf16)
        PRD = sb("PRD", [P, Q, TILES])
        GF = sb("GF", [P, 2, 2, Q])
        OEF = sb("OEF", [P, 2, Q * P])
        OEB = OEF[:, :, :].rearrange("p a w -> p (a w)")[:, 0:Q * P].bitcast(bf16).rearrange("p (a w) -> p a w", a=2)
        SO = sb("SO", [D, 2, Q * P])
        PR = sb("PR", [P, 2, Q, D])
        SG = sb("SG", [P, 2, Q, D])
        MSG = sb("MSG", [P, 2, Q, D])
        XR = [MSG[:, k, :, :].rearrange("p q d -> p (q d)") for k in range(2)]
        HT = sb("HT", [D, 2, Q * P])

        B = [pb(f"bank{k}", [P, 512]) for k in range(8)]

        block = ctx.enter_context(nc.Block())
        x_t = A["x"]

        def tiled(ap):
            return ap.rearrange("(t p) w -> p t w", p=P)

        KINDS = ["A", "A", "A", "B", "B", "C"]
        NA_BEFORE = [0, 1, 2, 3, 3, 3]
        ROUNDS = NG // U
        TABLE_PARTS = 3
        SPREAD = B[0]

        def grp(n, g, per=1, a=0):
            return g.times(per, n * NG * per + per + a * per)

        def ring(n, g, per):
            return g.rounds(per, n * ROUNDS * per + per)

        GATP = [None, None, None, 0, 1, None]
        PREP = [None, None, None, 0, 1, 2]

        def rows_free(n, g, a):
            return {"A": ("picked", grp(n, g, a=a)), "B": ("msg_ready", grp(GATP[n] or 0, g, a=a)),
                    "C": ("pre_ready", grp(2, g, a=a))}[KINDS[n]]

        def direct(n, g):
            return KINDS[n] != "A" or g.c % 2 == 0

        def rows_in(n, g):
            if not direct(n, g):
                return f"kept_in{g.slot}", ring(n, g, 16)
            return f"rows_in{g.slot}", ring(n - 3 * (g.c % 2), g, 64)

        def idx_ready(n, g):
            return f"idx_ready{g.slot}", ring(n - 3 * (g.c % 2), g, 1)

        FILLS = [-(-(KEPT - s) // U) for s in range(U)]

        def ahead(n, g, per, a=0):
            return g.rounds(per, n * FILLS[g.slot] * per + per + a * per)

        def kept_all(e, n):
            for s in range(U):
                e.wait_ge(sem(f"kept_out{s}"), 16 * (n + 1) * FILLS[s])

        def pool_pass(e, n):
            w = TW[n]
            e.wait_ge(sem("table_written"), 16 * TABLE_PARTS * (n + 1))

            def fetch(g, done):
                for q in range(Q):
                    e.indirect_dma_start(
                        out=G[:, g.slot, q, 0:w], out_offset=None, in_=tabs[n][:, :],
                        in_offset=bass.IndirectOffsetOnAxis(ap=IDX[:, g.slot, q:q + 1], axis=0),
                    ).then_inc(sem(done), 16)

            def fetch_ahead(g):
                gate(e, "pool", sem("ahead_idx_ready"), g.times(1, n * KEPT + 1))
                gate(e, "pool", sem(f"kept_out{g.slot}"), ahead(n, g, 16, a=-1))
                fetch(g, f"ahead_in{g.slot}")

            def gather(g):
                if direct(n, g):
                    ready, val = idx_ready(n, g)
                    gate(e, "pool", sem(ready), val)
                    free, val = rows_free(n, g, -U)
                    gate(e, "pool", sem(free), val)
                    fetch(g, f"rows_in{g.slot}")

            if KINDS[n] == "A":
                steps(e, [(0, fetch_ahead)], KEPT)
                kept_all(e, n)
            steps(e, [(0, gather)])

        def act_ahead(e, n):
            def indices(g):
                gate(e, "act", sem(f"ahead_in{g.slot}"), ahead(n, g, 64, a=-1))
                e.activation(IDX[:, g.slot, :], FLD[:, F_SRC, bass.ds(g.times(2 * Q, Q), Q)], ACT.Copy)\
                    .then_inc(sem("ahead_idx_ready"), 1)

            def keep(g):
                gate(e, "act", sem(f"ahead_in{g.slot}"), ahead(n, g, 64))
                e.dma_start(kept_d[bass.ds(g.times(1), 1), :, :].rearrange("o p (q w) -> p (o q) w", q=Q),
                            G[:, g.slot, :, 0:WT]).then_inc(sem(f"kept_out{g.slot}"), 16)

            steps(e, [(3, keep), (0, indices)], KEPT, after_head=(lambda: act_moments(e)) if n == 2 else None)
            for s in range(U):
                e.wait_ge(sem(f"ahead_in{s}"), 64 * (n + 1) * FILLS[s])
            for c in range(U):
                indices_of(e, n, At(c))

        def sp_kept(e, n):
            kept_all(e, n)

            def load(g):
                if not direct(n, g):
                    gate(e, "sp", sem("picked"), grp(n, g, a=-U))
                    e.dma_start(G[:, g.slot, :, 0:WT],
                                kept_d[bass.ds(half(g), 1), :, :].rearrange("o p (q w) -> p (o q) w", q=Q))\
                        .then_inc(sem(f"kept_in{g.slot}"), 16)

            steps(e, [(0, load)])

        def sp_stream(e, n):
            w = 2 if KINDS[n] == "A" else 1

            def load(g):
                gate(e, "sp", sem("ohT_ready"), grp(n, g, a=-U))
                at = bass.ds(g.times(Q * P), Q * P)
                e.dma_start(ROWB[:, g.slot, 0:w * Q * P].rearrange("p (r i) -> p r i", r=w),
                            rows_d[0:w, at].unsqueeze(0).to_broadcast([P, w, Q * P])).then_inc(sem(f"row_in{g.slot}"), 16)

            def load_resets(g):
                gate(e, "sp", sem("scanned"), grp(0, g, a=-U))
                at = bass.ds(g.times(Q * P), Q * P)
                e.dma_start(RSTB[:, g.slot, :].unsqueeze(1),
                            rows_d[2:3, at].unsqueeze(0).to_broadcast([D, 1, Q * P])).then_inc(sem(f"reset_in{g.slot}"), 16)

            steps(e, [(0, load), (4, load_resets)] if KINDS[n] == "C" else [(0, load)])

        def dve_hot(e, n):
            w = 2 * Q * P if KINDS[n] == "A" else Q * P
            used = ("scores_on_pe", n) if KINDS[n] == "A" else ("spread_on_pe", PREP[n])

            def hot(g):
                gate(e, "dve", sem(used[0]), grp(used[1], g, a=-2))
                hold(e, sem(f"row_in{g.slot}"), ring(n, g, 16))
                e.tensor_scalar(OT[:, g.par(2), 0:w], ROWB[:, g.slot, 0:w], iopf[:, :], None, ALU.is_equal)\
                    .then_inc(sem("ohT_ready"), 1)
            return hot

        def half(g):
            return g.c // 2 if g.i is None else g.i * (U // 2) + g.c // 2

        def tile_of(e, g):
            return e.value_load(TVR[0:1, bass.ds(g.times(Q), 1)], min_val=0, max_val=TILES - 1)

        def pe_scores(e, n):
            e.wait_ge(sem("parts_ready"), n + 1)

            def fn(g):
                bank = B[g.par(2)]
                t = tile_of(e, g)
                gate(e, "pe", sem("ohT_ready"), grp(n, g))
                gate(e, "pe", sem("score_read"), grp(n, g, a=-2))
                for q in range(Q):
                    cand = bank[:, TILES * q:TILES * (q + 1)]
                    for k in range(3):
                        e.matmul(cand, OT[:, g.par(2), (Q + q) * P:(Q + q + 1) * P], ATB[:, k, :], start=(k == 0), stop=False)
                    for k in range(3):
                        mm = e.matmul(cand, OT[:, g.par(2), q * P:(q + 1) * P],
                                      KS[:, bass.ds(t, 1), k, 0:1].rearrange("p a o -> p (a o)").to_broadcast([P, TILES]),
                                      start=False, stop=(k == 2))
                mm.then_inc(sem("scores_on_pe"), 1)

            def count(g):
                gate(e, "pe", sem("counts_hot"), grp(n, g))
                first, last = g.i is None and g.c == 0, g.i is None and g.c == NG - 1
                for q in range(Q):
                    mm = e.matmul(B[2][:, 0:TILES], OHN[:, g.par(2), q, :], THOT[:, g.par(2), q, :],
                                  start=(first and q == 0), stop=(last and q == Q - 1))
                mm.then_inc(sem("counted"), 1)

            steps(e, [(0, fn), (2, count)] if n < 2 else [(0, fn)])

        def dve_scores(e, v, n):
            if n == 1:
                e.wait_ge(sem("tiles_in"), 16)
                v(e.tensor_copy(FLD[:, F_M, :], FLD[:, F_W, :].bitcast(i32)))

            def hot_counts(g):
                place, tile = [(F_SLO, F_SHI), (F_DREL, F_M)][n]
                vs = bass.ds(g.times(Q), Q)
                gate(e, "dve", sem("counted"), grp(n, g, a=-2))
                e.tensor_tensor(OHN[:, g.par(2), :, :], FLD[:, place, vs].unsqueeze(2).to_broadcast([P, Q, P]),
                                iotaf[:, :].unsqueeze(1).to_broadcast([P, Q, P]), ALU.is_equal)
                e.tensor_tensor(THOT[:, g.par(2), :, :], FLD[:, tile, vs].unsqueeze(2).to_broadcast([P, Q, TILES]),
                                iotaf[:, 0:TILES].unsqueeze(1).to_broadcast([P, Q, TILES]), ALU.is_equal)\
                    .then_inc(sem("counts_hot"), 1)

            def own_tile(g):
                vs = bass.ds(g.times(Q), Q)
                e.tensor_tensor(HIS[:, :, :], FLD[:, F_SHI, vs].unsqueeze(2).to_broadcast([P, Q, TILES]),
                                iotaf[:, 0:TILES].unsqueeze(1).to_broadcast([P, Q, TILES]), ALU.is_equal).then_inc(sem("tile_hot"), 1)
                gate(e, "dve", sem("scores_on_pe"), grp(n, g))
                hold(e, sem("tile_hot"), grp(n, g))
                e.tensor_tensor(PRD[:, :, :], B[g.par(2)][:, 0:TILES * Q].rearrange("p (q t) -> p q t", q=Q),
                                HIS[:, :, :], ALU.mult).then_inc(sem("score_read"), 1)
                hold(e, sem("score_read"), grp(n, g))
                e.tensor_reduce(FLD[:, F_S, vs], PRD[:, :, :], AX.X, ALU.add)

            steps(e, [(0, dve_hot(e, n)), (1, own_tile), (1, hot_counts)] if n < 2 else [(0, dve_hot(e, n)), (1, own_tile)])
            if n < 2:
                e.wait_ge(sem("counted"), (n + 1) * NG)
                v(e.tensor_copy(CNT[:, n, :], B[2][:, 0:TILES]))
            e.memset(CONST[:, :], 0.0).then_inc(sem("scores_made"), 1)
            e.wait_ge(sem("scores_made"), n + 1)

        SV = ROOT[:, :, :].rearrange("p t d -> p (t d)")[:, 0:VP].rearrange("p (k i) -> p k i", k=VB)
        FV = T1[:, :, :].rearrange("p t d -> p (t d)")[:, 0:VP].rearrange("p (k i) -> p k i", k=VB)
        MV = T2[:, :, :].rearrange("p t d -> p (t d)")[:, 0:VP].rearrange("p (k i) -> p k i", k=VB)
        LASTR = XT[0:1, 0:VP]
        CARRY = XT[0:1, VP:2 * VP + 1]
        HALVES = [(0, 4), (4, VB)]

        def turn_blocks(e, src, b0, name):
            for h, (k0, k1) in enumerate(HALVES):
                for k in range(k0, k1):
                    mm = e.transpose(B[b0 + h][:, (k - k0) * P:(k - k0 + 1) * P], src(k), ident[:, :])
            mm.then_inc(sem(name), 1)

        def row_out(e, src, name):
            for h, (k0, k1) in enumerate(HALVES):
                for k in range(k0, k1):
                    mm = e.transpose(B[4 + h][0:1, (k - k0) * P:(k - k0 + 1) * P], src(k), ident[:, :])
            mm.then_inc(sem(name), 1)

        def row_in(e, src, name):
            for k in range(VB):
                mm = e.transpose(B[6][:, k:k + 1], src(k), ident[0:1, 0:1])
            mm.then_inc(sem(name), 1)

        def pe_segments(e, n):
            e.wait_ge(sem("scores_ready"), n + 1)
            turn_blocks(e, lambda k: FLD[:, F_S, k * P:(k + 1) * P], 2, "scores_turned")
            e.wait_ge(sem("prefix_done"), n + 1)
            row_out(e, lambda k: FV[:, k, P - 1:P], "prefix_row")
            e.wait_ge(sem("prefix_carry"), n + 1)
            row_in(e, lambda k: CARRY[:, k * P:(k + 1) * P], "prefix_cols")
            e.wait_ge(sem("suffix_done"), n + 1)
            row_out(e, lambda k: MV[:, k, 0:1], "suffix_row")
            e.wait_ge(sem("suffix_carry"), n + 1)
            row_in(e, lambda k: CARRY[:, 1 + k * P:1 + (k + 1) * P], "suffix_cols")
            e.wait_ge(sem("maxima_done"), n + 1)
            turn_blocks(e, lambda k: MV[:, k, :], 0, "maxima_turned")
            e.wait_ge(sem("weights_done"), n + 1)
            turn_blocks(e, lambda k: SV[:, k, :], 2, "weights_back")

        def act_segments(e, n):
            e.wait_ge(sem("scores_turned"), n + 1)
            for h, (k0, k1) in enumerate(HALVES):
                mm = e.activation(SV[:, k0:k1, :].rearrange("p k i -> p (k i)"), B[2 + h][:, 0:(k1 - k0) * P], ACT.Copy)
            mm.then_inc(sem("scores_in_rows"), 1)
            e.wait_ge(sem("exponents_done"), n + 1)
            e.activation(SV, FV, ACT.Exp).then_inc(sem("weights_done"), 1)
            e.wait_ge(sem("maxima_turned"), n + 1)
            for h, (k0, k1) in enumerate(HALVES):
                e.activation(FLD[:, F_M, k0 * P:k1 * P], B[h][:, 0:(k1 - k0) * P], ACT.Copy)
            e.wait_ge(sem("weights_back"), n + 1)
            for h, (k0, k1) in enumerate(HALVES):
                mm = e.activation(FLD[:, F_W, k0 * P:k1 * P], B[2 + h][:, 0:(k1 - k0) * P], ACT.Copy)
            mm.then_inc(sem("attention_ready"), 1)
            e.wait_ge(sem("attention_ready"), n + 1)

        def dve_segments(e, v, n):
            slope = [0.2, 0.2, 0.01][n]
            s = FLD[:, F_S, :]
            v(e.tensor_tensor(s, s, FLD[:, F_XW, :], ALU.add))
            v(e.scalar_tensor_tensor(out=s, in0=s, scalar=slope, in1=s, op0=ALU.mult, op1=ALU.max))
            e.sem_inc(sem("scores_ready"), 1)
            e.wait_ge(sem("scores_in_rows"), n + 1)
            for k in range(VB):
                sc = e.tensor_tensor_scan(FV[:, k, :], RSTV[:, k, :], SV[:, k, :], -BIG, ALU.add, ALU.max)
            sc.then_inc(sem("prefix_done"), 1)
            e.wait_ge(sem("prefix_row"), n + 1)
            e.memset(CARRY[:, 0:1], -BIG)
            e.tensor_copy(LASTR[:, 0:4 * P], B[4][0:1, :])
            v(e.tensor_copy(LASTR[:, 4 * P:VP], B[5][0:1, 0:VP - 4 * P]))
            e.tensor_tensor_scan(CARRY[:, 1:VP + 1], HASR[:, :], LASTR, -BIG, ALU.add, ALU.max).then_inc(sem("prefix_carry"), 1)
            e.wait_ge(sem("prefix_cols"), n + 1)
            v(e.tensor_copy(CINS[:, 0, :], B[6][:, 0:VB]))
            v(e.tensor_tensor(MV, PM[:, :, :], CINS[:, 0, :].unsqueeze(2).to_broadcast([P, VB, P]), ALU.add))
            v(e.tensor_tensor(FV, MV, FV, ALU.max))
            for k in range(VB):
                sc = e.tensor_tensor_scan(MV[:, k, ::-1], ENDV[:, k, ::-1], FV[:, k, ::-1], -BIG, ALU.add, ALU.max)
            sc.then_inc(sem("suffix_done"), 1)
            e.wait_ge(sem("suffix_row"), n + 1)
            e.memset(CARRY[:, VP:VP + 1], -BIG)
            e.tensor_copy(LASTR[:, 0:4 * P], B[4][0:1, :])
            v(e.tensor_copy(LASTR[:, 4 * P:VP], B[5][0:1, 0:VP - 4 * P]))
            e.tensor_tensor_scan(XT[0:1, 2 * VP - 1:VP - 1:-1], HASE[:, ::-1], XT[0:1, VP - 1::-1], -BIG, ALU.add, ALU.max)\
                .then_inc(sem("suffix_carry"), 1)
            e.wait_ge(sem("suffix_cols"), n + 1)
            v(e.tensor_copy(CINS[:, 1, :], B[6][:, 0:VB]))
            v(e.tensor_tensor(FV, SMK[:, :, :], CINS[:, 1, :].unsqueeze(2).to_broadcast([P, VB, P]), ALU.add))
            v(e.tensor_tensor(MV, MV, FV, ALU.max))
            e.sem_inc(sem("maxima_done"), 1)
            v(e.tensor_tensor(FV, SV, MV, ALU.subtract))
            e.sem_inc(sem("exponents_done"), 1)
            e.wait_ge(sem("attention_ready"), n + 1)

        MLP = [B[1], B[7]]

        def XP(p, k):
            o = Q * P + (k % 2) * Q * D
            return ROWB[:, p + 2 * (k // 2), o:o + Q * D]

        def pe_spread(e, n):
            def fn(g):
                t = tile_of(e, g)
                gate(e, "pe", sem("ohT_ready"), grp(n, g))
                gate(e, "pe", sem("pre_ready"), grp(PREP[n], g, a=-1))
                for q in range(Q):
                    for k in range(3):
                        mm = e.matmul(SPREAD[:, q * D:(q + 1) * D], OT[:, g.par(2), q * P:(q + 1) * P],
                                      KS[:, bass.ds(t, 1), k, :].rearrange("p a w -> p (a w)"),
                                      start=(k == 0), stop=(k == 2))
                mm.then_inc(sem("spread_on_pe"), 1)
            return fn

        def pe_pick(e, n, w, src, ready, fetched=False):
            def fn(g):
                gate(e, "pe", sem(ready[0]), grp(ready[1], g))
                if fetched:
                    landed, val = rows_in(n, g)
                    gate(e, "pe", sem(landed), val)
                gate(e, "pe", sem("ohF_ready"), grp(n, g))
                gate(e, "pe", sem("sums_added"), grp(n, g, a=-2))
                for q in range(Q):
                    mm = e.matmul(B[5 + g.par(2)][:, 0:w], OEF[:, g.par(2), q * P:(q + 1) * P], src(g, q),
                                  start=(q == 0), stop=(q == Q - 1))
                mm.then_inc(sem("picked"), 1)
            return fn

        def pe_pass(e, n):
            kind = KINDS[n]
            if kind == "A":
                steps(e, [(0, pe_pick(e, n, WA, lambda g, q: G[:, g.slot, q, 0:WA], ("rows_joined", n), fetched=True))])
                return
            e.wait_ge(sem("parts_ready"), n + 1)
            if kind == "B":
                steps(e, [(0, pe_spread(e, n)),
                          (1, pe_pick(e, n, D, lambda g, q: MSG[:, g.par(2), q, :], ("msg_ready", GATP[n])))])
            else:
                def turn(g):
                    gate(e, "pe", sem("hidden_ready"), grp(0, g))
                    gate(e, "pe", sem("hT_copied"), grp(0, g, a=-2))
                    for q in range(Q):
                        mm = e.transpose(B[2 + g.par(2)][0:D, q * P:(q + 1) * P], SG[:, g.par(2), q, :], ident[:, :])
                    mm.then_inc(sem("hT_on_pe"), 1)

                def mlp(g):
                    gate(e, "pe", sem("hT_copied"), grp(0, g))
                    gate(e, "pe", sem("scanned"), grp(0, g, a=-2))
                    e.matmul(MLP[g.par(2)][0:D, :], W2T[:, :], HT[:, g.par(2), :], start=True, stop=True).then_inc(sem("mlp_on_pe"), 1)

                def back(g):
                    gate(e, "pe", sem("scanned"), grp(0, g))
                    gate(e, "pe", sem("rest_made"), grp(0, g, a=-1))
                    for q in range(Q):
                        mm = e.transpose(B[4][:, q * D:(q + 1) * D], SO[:, g.par(2), q * P:(q + 1) * P], ident[0:D, 0:D])
                    mm.then_inc(sem("back_on_pe"), 1)

                def pick(g):
                    gate(e, "pe", sem("ends_split"), grp(0, g))
                    gate(e, "pe", sem("sums_added"), grp(n, g, a=-2))
                    for q in range(Q):
                        for k in range(3):
                            mm = e.matmul(B[5 + g.par(2)][:, 0:D], OEB[:, g.par(2), q * P:(q + 1) * P],
                                          XP(g.par(2), k)[:, q * D:(q + 1) * D],
                                          start=(q == 0 and k == 0), stop=(q == Q - 1 and k == 2))
                    mm.then_inc(sem("picked"), 1)

                steps(e, [(3, mlp), (7, pick), (2, turn), (5, back), (0, pe_spread(e, n))])

        def indices_of(e, n, g):
            if direct(n, g):
                ready, val = rows_in(n, g)
                gate(e, "act", sem(ready), val - 64)
                e.activation(IDX[:, g.slot, :], FLD[:, F_SRC, bass.ds(g.times(Q), Q)], ACT.Copy)\
                    .then_inc(sem(idx_ready(n, g)[0]), 1)

        def act_indices(e, n):
            def fn(g):
                if KINDS[n] != "A" or g.i is not None or g.c >= U:
                    indices_of(e, n, g)
            return fn

        COPIED = [0, 1, 2, None, None, 3]

        def act_pass(e, n):
            kind = KINDS[n]

            def fields(g):
                gate(e, "act", sem("ohF_ready"), grp(n, g, a=-2))
                at = bass.ds(g.times(Q), Q)
                if kind == "A":
                    e.activation(GF[:, g.par(2), :, :], FLD[:, F_DREL:F_W + 1:F_W - F_DREL, at], ACT.Copy).then_inc(sem("group_fields"), 1)
                else:
                    e.activation(GF[:, g.par(2), 0, :], FLD[:, F_EREL, at], ACT.Copy).then_inc(sem("group_fields"), 1)

            if kind == "A":
                def join(g):
                    gate(e, "act", sem("picked"), grp(n, g, a=-U))
                    e.activation(G[:, g.slot, :, WT:WA],
                                 FLD[:, F_A0:F_M + 1, bass.ds(g.times(Q), Q)].rearrange("p f v -> p v f"), ACT.Copy)\
                        .then_inc(sem("rows_joined"), 1)

                steps(e, [(0, act_indices(e, n)), (1, join), (1, fields)])
            elif kind == "B":
                def gates(g):
                    gate(e, "act", sem("pre_ready"), grp(PREP[n], g))
                    gate(e, "act", sem("msg_ready"), grp(GATP[n], g, a=-2))
                    e.activation(SG[:, g.par(2), :, :], PR[:, g.par(2), :, :], ACT.Sigmoid).then_inc(sem("gate_ready"), 1)

                steps(e, [(0, act_indices(e, n)), (3, gates)])
            else:
                def hidden(g):
                    gate(e, "act", sem("pre_ready"), grp(2, g))
                    gate(e, "act", sem("hT_on_pe"), grp(0, g, a=-2))
                    e.activation(SG[:, g.par(2), :, :], PR[:, g.par(2), :, :], ACT.Relu).then_inc(sem("hidden_ready"), 1)

                def hT(g):
                    gate(e, "act", sem("hT_on_pe"), grp(0, g))
                    gate(e, "act", sem("mlp_on_pe"), grp(0, g, a=-2))
                    e.activation(HT[:, g.par(2), :], B[2 + g.par(2)][0:D, :], ACT.Copy).then_inc(sem("hT_copied"), 1)

                def ends(g):
                    gate(e, "act", sem("back_on_pe"), grp(0, g))
                    gate(e, "act", sem("picked"), grp(n, g, a=-2))
                    e.activation(XP(g.par(2), 0), B[4][:, 0:Q * D], ACT.Copy).then_inc(sem("ends_copied"), 1)

                steps(e, [(0, act_indices(e, n)), (4, hidden), (5, hT), (8, fields), (8, ends)])

        def dve_add(e, n, w):
            def fn(g):
                t = tile_of(e, g)
                gate(e, "dve", sem("picked"), grp(n, g))
                hold(e, sem("sums_added"), grp(n, g, a=-1))
                e.tensor_tensor(ACC[:, bass.ds(t, 1), 0:w], ACC[:, bass.ds(t, 1), 0:w],
                                B[5 + g.par(2)][:, 0:w].unsqueeze(1), ALU.add).then_inc(sem("sums_added"), 1)
            return fn

        def one_hots(e, g, at, out=OEF, weighted=False):
            for q in range(Q):
                oh = e.tensor_scalar(out[:, g.par(2), q * P:(q + 1) * P], iotab[:, :], at(q),
                                     GF[:, g.par(2), 1, q:q + 1] if weighted else None, ALU.is_equal,
                                     *([ALU.mult] if weighted else []))
            oh.then_inc(sem("ohF_ready"), 1)

        def dve_pass(e, n):
            kind = KINDS[n]
            if kind == "A":
                def weigh(g):
                    gate(e, "dve", sem("picked"), grp(n, g, a=-2))
                    gate(e, "dve", sem("group_fields"), grp(COPIED[n], g))
                    one_hots(e, g, lambda q: GF[:, g.par(2), 0, q:q + 1], weighted=True)

                steps(e, [(0, weigh), (1, dve_add(e, n, WA))])
                return

            def pre(g):
                ready, val = rows_in(n, g)
                gate(e, "dve", sem(ready), val)
                if kind == "B":
                    gate(e, "dve", sem("gate_ready"), grp(GATP[n], g, a=-2))
                else:
                    gate(e, "dve", sem("hidden_ready"), grp(0, g, a=-2))
                hold(e, sem("spread_on_pe"), grp(PREP[n], g))
                e.tensor_tensor(PR[:, g.par(2), :, :], SPREAD[:, 0:Q * D].rearrange("p (q d) -> p q d", q=Q),
                                G[:, g.slot, :, 0:D], ALU.add).then_inc(sem("pre_ready"), 1)

            if kind == "B":
                def msg(g):
                    gate(e, "dve", sem("picked"), grp(n, g, a=-2))
                    one_hots(e, g, lambda q: FLD[:, F_DREL, bass.ds(g.times(Q, q), 1)])
                    hold(e, sem("gate_ready"), grp(GATP[n], g))
                    e.tensor_tensor(MSG[:, g.par(2), :, :], SG[:, g.par(2), :, :], G[:, g.slot, :, D:2 * D],
                                    ALU.mult).then_inc(sem("msg_ready"), 1)

                steps(e, [(0, dve_hot(e, n)), (2, msg), (1, pre), (3, dve_add(e, n, D))])
            else:
                def scan(g):
                    p, o = g.par(2), 1 - g.par(2)
                    gate(e, "dve", sem(f"reset_in{g.slot}"), ring(0, g, 16))
                    gate(e, "dve", sem("mlp_on_pe"), grp(0, g))
                    gate(e, "dve", sem("back_on_pe"), grp(0, g, a=-2))
                    if g.i is None and g.c == 0:
                        init = -BIG
                    else:
                        init = SO[:, o, Q * P - 1:Q * P]
                        hold(e, sem("scanned"), grp(0, g, a=-1))
                    e.tensor_tensor_scan(SO[:, p, :], RSTB[:, g.slot, :], MLP[g.par(2)][0:D, :], init, ALU.add, ALU.max)\
                        .then_inc(sem("scanned"), 1)

                def split(g):
                    p = g.par(2)
                    gate(e, "dve", sem("picked"), grp(n, g, a=-2))
                    gate(e, "dve", sem("group_fields"), grp(COPIED[n], g))
                    one_hots(e, g, lambda q: GF[:, g.par(2), 0, q:q + 1], out=OEB)
                    hold(e, sem("ends_copied"), grp(0, g))
                    e.tensor_tensor(XR[p], B[4][:, 0:Q * D], XP(p, 0), ALU.subtract).then_inc(sem("rest_made"), 1)
                    gate(e, "dve", sem("rest_made"), grp(0, g))
                    e.tensor_copy(XP(p, 1), XR[p]).then_inc(sem("second_made"), 1)
                    hold(e, sem("second_made"), grp(0, g))
                    e.tensor_tensor(XP(p, 2), XR[p], XP(p, 1), ALU.subtract).then_inc(sem("ends_split"), 1)

                steps(e, [(6, split), (1, pre), (0, dve_hot(e, n)), (4, scan), (8, dve_add(e, n, D))])

        FULL = CHUNKS - 1

        def sp_prep(e):
            dst = A["dst"]
            x_in = sem("x_in")
            e.dma_start(DST_I, dst.rearrange("(p i) -> p i", p=125)).then_inc(sem("dst_in"), 16)
            e.wait_ge(sem("cleared"), 1)
            e.dma_start(X[:, 0:TILES - 1, :], x_t[0:(TILES - 1) * P, :].rearrange("(t p) w -> p t w", p=P)).then_inc(x_in, 16)
            e.dma_start(X[0:LASTN, TILES - 1, :], x_t[(TILES - 1) * P:N, :]).then_inc(x_in, 16)
            w_in = sem("weights_in")
            n = [0]

            def load(o, i):
                e.dma_start(o, i).then_inc(w_in, 16)
                n[0] += 16

            for c, nm in enumerate(["L0_gnn_W1", "L0_gnn_W2", "L1_gnn_W_fc", "L1_gnn_W_m1", "L1_gnn_W_m2"]):
                load(WIN[:, c, :], A[nm])
            load(WIN[:, 5:7, :].rearrange("o c d -> o (c d)"), A["L3_gnn_W1"])
            load(WIN[:, 7, :], A["L3_gnn_W2"])
            for c, nm in enumerate(["L0_gnn_a_src1", "L0_gnn_a_dst1", "L0_gnn_a_src2", "L0_gnn_a_dst2"]):
                load(AV[:, c:c + 1], A[nm].unsqueeze(1))
            wat = A["L1_gnn_W_attn"]
            for c in range(6):
                load(AV[:, 4 + c:5 + c], wat[0:1, c * D:(c + 1) * D].rearrange("a o -> o a"))
            load(WE[:, 0:2], A["L1_gnn_W_edge"])
            load(WE[:, 2:3], wat[0:1, 6 * D:6 * D + 2].rearrange("a o -> o a"))
            load(WE[:, 3:3 + D], A["L1_gnn_W_e2n"].rearrange("o j -> j o"))
            for l in range(2):
                for c, nm in enumerate("qvks"):
                    load(WAUG[3 + l][0:D, c * D:(c + 1) * D], A["L2_gnn_W" + nm][l, :, :])
                    load(WAUG[3 + l][D:D + 1, c * D:(c + 1) * D], A["L2_gnn_b" + nm][l:l + 1, :])
                load(BIASR[D:D + 1, l, :], A["L2_gnn_bias"][l:l + 1, :])
            load(WAUG[5][D:D + 1, D:2 * D], A["L3_gnn_b1"].unsqueeze(0))
            for c, ap in enumerate([A["L0_gnn_b1"].unsqueeze(0), A["L0_gnn_b2"].unsqueeze(0), A["L2_gnn_gamma"][0:1, :],
                                    A["L2_gnn_gamma"][1:2, :], A["L2_gnn_beta"][0:1, :], A["L2_gnn_beta"][1:2, :],
                                    A["L3_gnn_b2"].unsqueeze(0)]):
                load(ROW[:, c, :], ap.to_broadcast([P, D]))
            assert n[0] == 16 * WEIGHT_LOADS, n[0] // 16

        WEIGHT_LOADS = 5 + 2 + 4 + 6 + 3 + 2 * 9 + 1 + 7

        def act_prep(e):
            src, dst, attr = A["src"], A["dst"], A["edge_attr_2"]
            done = sem("record_in")
            n = [0]

            def put(o, i):
                e.dma_start(o, i).then_inc(done, 16)
                n[0] += 16

            W0 = FULL * P
            dv = dst[0:W0].rearrange("(c k) -> c k", k=P)
            put(rec_d[0:FULL, 0:P], src[0:W0].rearrange("(c k) -> c k", k=P))
            put(rec_d[0:FULL, P:2 * P], dv)
            put(rec_d[0:FULL, 2 * P + 1:3 * P], dv[:, 0:P - 1])
            put(rec_d[1:FULL + 1, 2 * P:2 * P + 1], dv[:, P - 1:P])
            put(rec_d[0:FULL, 3 * P:4 * P - 1], dv[:, 1:P])
            put(rec_d[0:FULL - 1, 4 * P - 1:4 * P], dv[1:FULL, 0:1])
            put(rec_d[FULL - 1:FULL, 4 * P - 1:4 * P], dst[W0:W0 + 1].unsqueeze(0))
            put(rec_d[0:FULL, 4 * P:6 * P], attr[0:W0, :].bitcast(i32).rearrange("(c k) a -> c (k a)", k=P))
            put(rec_d[FULL:FULL + 1, 0:LASTE], src[W0:E].unsqueeze(0))
            put(rec_d[FULL:FULL + 1, P:P + LASTE], dst[W0:E].unsqueeze(0))
            put(rec_d[FULL:FULL + 1, 2 * P + 1:2 * P + LASTE], dst[W0:E - 1].unsqueeze(0))
            put(rec_d[FULL:FULL + 1, 3 * P:3 * P + LASTE - 1], dst[W0 + 1:E].unsqueeze(0))
            put(rec_d[FULL:FULL + 1, 4 * P:4 * P + 2 * LASTE], attr[W0:E, :].bitcast(i32).rearrange("k a -> (k a)").unsqueeze(0))
            e.wait_ge(sem("pad_set"), 1)
            put(rec_d[0:1, 2 * P:2 * P + 1], PADR[:, REC:REC + 1])
            put(rec_d[FULL:FULL + 1, LASTE:P], PADR[:, LASTE:P])
            put(rec_d[FULL:FULL + 1, P + LASTE:2 * P], PADR[:, P + LASTE:2 * P])
            put(rec_d[FULL:FULL + 1, 2 * P + LASTE:3 * P], PADR[:, 2 * P + LASTE:3 * P])
            put(rec_d[FULL:FULL + 1, 3 * P + LASTE - 1:4 * P], PADR[:, 3 * P + LASTE - 1:4 * P])
            put(rec_d[FULL:FULL + 1, 4 * P + 2 * LASTE:6 * P], PADR[:, 4 * P + 2 * LASTE:6 * P])
            put(rec_d[FULL + 1:FULL + 2, :], PADR[:, 0:REC])
            assert n[0] == 16 * RECORD_PUTS, n[0] // 16
            e.wait_ge(sem("walk_done"), 1)
            e.dma_start(tv_d[:, :].rearrange("k p -> p k"), TVPI[:, :]).then_inc(sem("walk_out"), 16)
            e.wait_ge(sem("walk_out"), 16)
            e.dma_start(TVR[:, :].rearrange("o (k p) -> o k p", p=P), tv_d[:, :].unsqueeze(0)).then_inc(sem("walk_in"), 16)

        RECORD_PUTS = 20

        def pool_prep(e):
            e.memset(PADR[:, 0:P], 0)
            e.memset(PADR[:, P:4 * P], 9999)
            e.memset(PADR[:, 4 * P:6 * P], 0)
            e.memset(PADR[:, REC:REC + 1], -1).then_inc(sem("pad_set"), 1)
            e.iota(ioi[:, :], [[1, P]], base=0, channel_multiplier=0)
            e.iota(iop[:, :], [[0, 1]], base=0, channel_multiplier=1)
            e.iota(VIO_I[:, :], [[P, VB]], base=0, channel_multiplier=1).then_inc(sem("iota_done"), 1)
            e.wait_ge(sem("record_in"), 16 * RECORD_PUTS)
            e.wait_ge(sem("walk_done"), 1)
            for k in range(VB):
                e.indirect_dma_start(out=REC_S[:, k, :], out_offset=None, in_=rec_d[:, :],
                                     in_offset=bass.IndirectOffsetOnAxis(ap=CVI[:, k:k + 1], axis=0)).then_inc(sem("records_in"), 16)

        def dve_prep(e, v):
            v(e.memset(X[:, TILES - 1, :], 0.0))
            e.memset(XT[D:D + 1, :], 1.0)
            e.memset(ones[:, :], 1.0)
            e.memset(zeros[:, :], 0.0)
            e.memset(FLD[:, F_XW, :], 0.0)
            e.memset(FLD[:, F_S, :], 0.0)
            for k in range(3):
                e.memset(WAUG[k][:, D:WT], 0.0)
                e.memset(WAUG[k][D:D + 1, WT:WT + 2], 0.0)
                e.memset(WAUG[k][D:D + 1, 0:D], 0.0)
            e.memset(WAUG[5][D:D + 1, 0:D], 0.0)
            e.memset(START[:, 0:32], 0.0).then_inc(sem("cleared"), 1)
            e.wait_ge(sem("cleared"), 1)
            for k in range(3):
                e.memset(WAUG[k][D:D + 1, D:WT], 1.0)
            e.wait_ge(sem("iota_done"), 1)
            e.tensor_copy(iotab[:, :], ioi[:, :])
            e.tensor_copy(iotaf[:, :], ioi[:, :])
            e.tensor_copy(VIO[:, :], VIO_I[:, :])
            v(e.tensor_copy(iopf[:, :], iop[:, :]))
            v(e.tensor_scalar(ident[:, :], iotaf[:, :], iopf[:, :], None, ALU.is_equal))
            v(e.tensor_scalar(lastones[:, :], ones[:, :], iopf[:, :], float(LASTN), ALU.mult, ALU.mult))
            v(e.tensor_scalar(lastones[:, :], lastones[:, :], float(LASTN * LASTN), None, ALU.is_lt))
            e.sem_inc(sem("constants_done"), 1)
            e.wait_ge(sem("dst_in"), 16)
            v(e.tensor_copy(DST_F, DST_I))
            for t in range(1, TILES):
                v(e.tensor_scalar(DST_J, DST_F, float(t * P), 0.0, ALU.is_lt, ALU.add,
                                  accum_out=START[0:125, t:t + 1]))
            e.sem_inc(sem("starts_counted"), 1)
            e.wait_ge(sem("starts_summed"), 1)
            v(e.tensor_scalar(VT_I[:, :], B[0][:, 0:32], -(P * Q / 2 - 0.5), 1.0 / (P * Q), ALU.add, ALU.mult))
            v(e.tensor_copy(VT_F[:, :], VT_I[:, :]))
            v(e.tensor_scalar(VT_F[:, :], VT_F[:, :], float(SPANS - 1), None, ALU.min))
            v(e.tensor_tensor(VT_F[:, :], VT_F[:, :], iotaf[:, 0:32], ALU.add))
            v(e.tensor_scalar(VT_F[:, :], VT_F[:, :], float(Q), None, ALU.mult))
            v(e.tensor_tensor(CMP[:, :, :], VIO[:, :].unsqueeze(2).to_broadcast([P, VB, TILES - 1]),
                              VT_F[:, 1:TILES].unsqueeze(1).to_broadcast([P, VB, TILES - 1]), ALU.is_ge))
            v(e.tensor_reduce(TVP[:, :], CMP[:, :, :], AX.X, ALU.add))
            v(e.scalar_tensor_tensor(out=CVF[:, :], in0=TVP[:, :], scalar=-float(Q), in1=VIO[:, :], op0=ALU.mult, op1=ALU.add))
            v(e.tensor_scalar(CVF[:, :], CVF[:, :], float(CHUNKS), None, ALU.min))
            e.tensor_copy(TVPI[:, :], TVP[:, :])
            v(e.tensor_copy(CVI[:, :], CVF[:, :]))
            e.sem_inc(sem("walk_done"), 1)
            e.wait_ge(sem("records_in"), 16 * VB)
            f = lambda k: VF[:, k, :, :]
            rec = lambda k: REC_S[:, :, k * P:(k + 1) * P]
            tv = TVP[:, :].unsqueeze(2).to_broadcast([P, VB, P])
            HII = REC_S[:, :, 2 * P:3 * P]
            e.tensor_copy(f(F_SRC), rec(0))
            e.tensor_copy(f(F_DREL), rec(1))
            e.tensor_copy(f(F_M), rec(2))
            e.tensor_copy(f(F_EREL), rec(3))
            e.tensor_copy(f(F_A0), REC_S[:, :, 4 * P:6 * P].bitcast(f32).rearrange("p v (k a) -> p v k a", a=2)[:, :, :, 0])
            v(e.tensor_copy(f(F_A1), REC_S[:, :, 4 * P:6 * P].bitcast(f32).rearrange("p v (k a) -> p v k a", a=2)[:, :, :, 1]))
            e.tensor_tensor(f(F_M), f(F_DREL), f(F_M), ALU.not_equal)
            e.tensor_tensor(f(F_EREL), f(F_DREL), f(F_EREL), ALU.is_equal)
            v(e.tensor_scalar(HII, f(F_SRC), -(P / 2 - 0.5), 1.0 / P, ALU.add, ALU.mult))
            v(e.tensor_copy(f(F_SHI), HII))
            v(e.tensor_scalar(f(F_SLO), f(F_SHI), -float(P), None, ALU.mult))
            v(e.tensor_tensor(f(F_SLO), f(F_SLO), f(F_SRC), ALU.add))
            v(e.tensor_scalar(f(F_W), tv, -float(P), None, ALU.mult))
            v(e.tensor_tensor(f(F_DREL), f(F_DREL), f(F_W), ALU.add))
            e.tensor_scalar(ENDV[:, :, :], f(F_EREL), 0.0, -BIG, ALU.is_equal, ALU.mult)
            v(e.scalar_tensor_tensor(out=f(F_EREL), in0=f(F_EREL), scalar=20000.0, in1=f(F_DREL), op0=ALU.mult, op1=ALU.add))
            e.tensor_scalar(RSTV[:, :, :], f(F_M), -BIG, None, ALU.mult)
            v(e.tensor_scalar(f(F_M), f(F_M), -BIG, None, ALU.mult))
            for k in range(VB):
                e.tensor_tensor_scan(PM[:, k, :], zeros[:, :], RSTV[:, k, :], 0.0, ALU.add, ALU.min)
                v(e.tensor_tensor_scan(SMK[:, k, ::-1], zeros[:, :], ENDV[:, k, ::-1], 0.0, ALU.add, ALU.min))
            v(e.tensor_scalar(f(F_XW), f(F_DREL), 0.0, None, ALU.is_lt))
            v(e.tensor_scalar(f(F_W), f(F_DREL), float(P), None, ALU.is_ge))
            v(e.tensor_tensor(f(F_XW), f(F_XW), f(F_W), ALU.add))
            v(e.scalar_tensor_tensor(out=f(F_SHI), in0=f(F_XW), scalar=1000.0, in1=f(F_SHI), op0=ALU.mult, op1=ALU.add))
            e.tensor_copy(RB[:, 0, :, :], f(F_DREL))
            e.tensor_copy(RB[:, 1, :, :], f(F_SLO))
            v(e.tensor_copy(RB[:, 2, :, :], f(F_M)))
            e.sem_inc(sem("rows_built"), 1)
            e.sem_inc(sem("fields_done"), 1)
            r = 0
            for fl in FIELDS:
                for b0 in range(0, VB, 4):
                    e.wait_ge(sem("fields_on_pe"), r + 1)
                    w = min(4, VB - b0) * P
                    e.tensor_copy(FLD[:, fl, b0 * P:b0 * P + w], B[r % 2][:, 0:w]).then_inc(sem("fields_copied"), 1)
                    r += 1
            for k, row in enumerate([HASR, HASE]):
                e.wait_ge(sem("flags_row"), k + 1)
                e.tensor_copy(row[:, 0:4 * P], B[4][0:1, :])
                e.tensor_copy(row[:, 4 * P:VP], B[5][0:1, 0:VP - 4 * P]).then_inc(sem("flags_copied"), 1)
            e.wait_ge(sem("weights_in"), 16 * WEIGHT_LOADS)
            for l in range(2):
                e.tensor_tensor(WAUG[3 + l][D:D + 1, 3 * D:4 * D], WAUG[3 + l][D:D + 1, 3 * D:4 * D], BIASR[D:D + 1, l, :], ALU.add)
                e.tensor_copy(WAUG[l][0:D, 0:D], WIN[:, l, :])
            e.wait_ge(sem("weights_turned"), 1)
            e.tensor_copy(WTT[:, :, :].rearrange("p c d -> p (c d)"), B[4][0:D, 0:6 * D]).then_inc(sem("turned_copied"), 1)
            e.wait_ge(sem("turned_copied"), 1)
            e.tensor_copy(WAUG[2][0:D, 0:D], WTT[:, 2, :])
            e.tensor_copy(WAUG[5][0:D, 0:D], WTT[:, 4, :])
            e.tensor_tensor(WAUG[5][0:D, D:2 * D], WTT[:, 3, :], WTT[:, 4, :], ALU.subtract)
            e.tensor_copy(W2T[:, :], WTT[:, 5, :])
            e.wait_ge(sem("weights_folded"), 1)
            for l in range(3):
                e.tensor_copy(WAUG[l][0:D, WT:WT + 2], B[5][0:D, 2 * l:2 * l + 2])
            e.tensor_copy(WES[:, :], B[6][:, 0:2 + 2 * D])
            v(e.tensor_copy(UV[:, :, :].rearrange("p c d -> p (c d)"), B[6][:, 256:512]))
            e.sem_inc(sem("weights_ready"), 1)

        FIELDS = [F_SRC, F_DREL, F_EREL, F_A0, F_A1, F_SHI, F_SLO]

        def pe_prep(e):
            e.wait_ge(sem("starts_counted"), 1)
            e.matmul(B[0][:, 0:32], ones[0:125, :], START[0:125, :], start=True, stop=True).then_inc(sem("starts_summed"), 1)
            e.wait_ge(sem("fields_done"), 1)
            r = 0
            for fl in FIELDS:
                for b0 in range(0, VB, 4):
                    if r >= 2:
                        e.wait_ge(sem("fields_copied"), r - 1)
                    for b in range(b0, min(b0 + 4, VB)):
                        mm = e.transpose(B[r % 2][:, (b - b0) * P:(b - b0 + 1) * P], VF[:, fl, b, :], ident[:, :])
                    mm.then_inc(sem("fields_on_pe"), 1)
                    r += 1
            row_out(e, lambda k: PM[:, k, P - 1:P], "flags_row")
            e.wait_ge(sem("flags_copied"), 1)
            row_out(e, lambda k: SMK[:, k, 0:1], "flags_row")
            e.wait_ge(sem("flags_copied"), 2)
            e.wait_ge(sem("weights_in"), 16 * WEIGHT_LOADS)
            for k, c in enumerate([0, 1, 2, 5, 6, 7]):
                mm = e.transpose(B[4][0:D, k * D:(k + 1) * D], WIN[:, c, :], ident[0:D, 0:D])
            mm.then_inc(sem("weights_turned"), 1)
            e.wait_ge(sem("turned_copied"), 1)
            e.matmul(B[5][0:D, 0:2], WTT[:, 0, :], AV[:, 0:2], start=True, stop=True)
            e.matmul(B[5][0:D, 2:4], WTT[:, 1, :], AV[:, 2:4], start=True, stop=True)
            e.matmul(B[5][0:D, 4:6], WIN[:, 2, :], AV[:, 4:8:3], start=True, stop=True)
            e.matmul(B[6][:, 0:2], WE[:, 2:3].to_broadcast([2, P]), WE[:, 0:2], start=True, stop=True)
            for i in range(2):
                e.matmul(B[6][:, 2 + i * D:2 + (i + 1) * D], WE[:, i:i + 1].to_broadcast([2, P]), WE[:, 3:3 + D], start=True, stop=True)
            for k, (blk, wm) in enumerate([(1, 3), (2, 4), (4, 3), (5, 4)]):
                mm = e.matmul(B[6][:, 256 + k * D:256 + (k + 1) * D], AV[:, 4 + blk:5 + blk].to_broadcast([D, P]), WIN[:, wm, :],
                              start=True, stop=True)
            mm.then_inc(sem("weights_folded"), 1)

        WIDE = [WT + 2] * 3 + [4 * D] * 2 + [2 * D]
        PER = [512 // w for w in WIDE]
        PROJ = [-(-TILES // k) for k in PER]
        PBASE = [sum(PROJ[:k]) for k in range(7)]
        TURNS = -(-TILES // 4)
        XIN = [X, X1, X, X, X1, X]

        def pe_project(e, n):
            e.wait_ge(sem("x_ready"), n + 1)
            for k in range(TURNS):
                if k >= 2:
                    e.wait_ge(sem("xT_copied"), n * TURNS + k - 1)
                for t in range(4 * k, min(4 * k + 4, TILES)):
                    mm = e.transpose(B[k % 2][0:D, (t % 4) * P:(t % 4 + 1) * P], XIN[n][:, t, :], ident[:, :])
                mm.then_inc(sem("xT_on_pe"), 1)
            if n == 0:
                e.wait_ge(sem("weights_ready"), 1)
            for k in range(PROJ[n]):
                last = min((k + 1) * PER[n], TILES) - 1
                e.wait_ge(sem("xT_copied"), n * TURNS + last // 4 + 1)
                if k >= 2:
                    e.wait_ge(sem("proj_copied"), PBASE[n] + k - 1)
                for t in range(k * PER[n], last + 1):
                    o = (t - k * PER[n]) * WIDE[n]
                    mm = e.matmul(B[2 + k % 2][:, o:o + WIDE[n]], XT[:, t * P:(t + 1) * P], WAUG[n][:, :], start=True, stop=True)
                mm.then_inc(sem("proj_on_pe"), 1)

        def act_project(e, n):
            for k in range(TURNS):
                e.wait_ge(sem("xT_on_pe"), n * TURNS + k + 1)
                w = (min(4 * k + 4, TILES) - 4 * k) * P
                e.activation(XT[0:D, k * 4 * P:k * 4 * P + w], B[k % 2][0:D, 0:w], ACT.Copy).then_inc(sem("xT_copied"), 1)

        def dve_project(e, v, n):
            for k in range(PROJ[n]):
                e.wait_ge(sem("proj_on_pe"), PBASE[n] + k + 1)
                t0, t1 = k * PER[n], min((k + 1) * PER[n], TILES)
                bank = B[2 + k % 2][:, 0:(t1 - t0) * WIDE[n]].rearrange("p (t w) -> p t w", w=WIDE[n])
                if KINDS[n] == "A":
                    e.tensor_copy(TB[:, t0:t1, 0:WT], bank[:, :, 0:WT])
                    e.tensor_copy(AS[:, t0:t1], bank[:, :, WT])
                    e.tensor_copy(KF[:, t0:t1, 0:1], bank[:, :, WT + 1:WT + 2]).then_inc(sem("proj_copied"), 1)
                elif KINDS[n] == "B":
                    e.tensor_copy(TB[:, t0:t1, :], bank[:, :, 0:2 * D])
                    e.tensor_copy(KF[:, t0:t1, :], bank[:, :, 2 * D:3 * D])
                    e.tensor_copy(ROOT[:, t0:t1, :], bank[:, :, 3 * D:4 * D]).then_inc(sem("proj_copied"), 1)
                else:
                    e.tensor_copy(TB[:, t0:t1, 0:D], bank[:, :, 0:D])
                    e.tensor_copy(KF[:, t0:t1, :], bank[:, :, D:2 * D]).then_inc(sem("proj_copied"), 1)
            e.wait_ge(sem("proj_copied"), PBASE[n + 1])
            if n == 2:
                moments(e, v)
            w = 1 if KINDS[n] == "A" else D
            r = T1[:, :, 0:w]
            kf = KF[:, :, 0:w]
            v(e.tensor_copy(KS[:, :, 0, 0:w], kf))
            v(e.tensor_tensor(r, kf, KS[:, :, 0, 0:w], ALU.subtract))
            v(e.tensor_copy(KS[:, :, 1, 0:w], r))
            v(e.tensor_tensor(r, r, KS[:, :, 1, 0:w], ALU.subtract))
            v(e.tensor_copy(KS[:, :, 2, 0:w], r))
            if KINDS[n] == "A":
                rs = NV[:, 0, :]
                v(e.tensor_copy(ATB[:, 0, :], AS[:, :]))
                v(e.tensor_tensor(rs, AS[:, :], ATB[:, 0, :], ALU.subtract))
                v(e.tensor_copy(ATB[:, 1, :], rs))
                v(e.tensor_tensor(rs, rs, ATB[:, 1, :], ALU.subtract))
                e.tensor_copy(ATB[:, 2, :], rs)
            e.memset(ACC[:, :, :], 0.0)
            if n == 2:
                e.tensor_scalar(FLD[:, F_XW, :], FLD[:, F_A0, :], WES[:, 0:1], None, ALU.mult).then_inc(sem("edge_term"), 1)
                e.wait_ge(sem("edge_term"), 1)
                e.scalar_tensor_tensor(out=FLD[:, F_XW, :], in0=FLD[:, F_A1, :], scalar=WES[:, 1:2], in1=FLD[:, F_XW, :],
                                       op0=ALU.mult, op1=ALU.add)
            e.memset(CONST[:, :], 0.0).then_inc(sem("parts_ready"), 1)
            e.wait_ge(sem("parts_ready"), n + 1)

        def sp_table(e, n):
            w = TW[n]
            for part in range(TABLE_PARTS):
                k0, k1 = (PROJ[n] * j // TABLE_PARTS for j in (part, part + 1))
                t0, t1 = k0 * PER[n], min(k1 * PER[n], TILES)
                e.wait_ge(sem("proj_copied"), PBASE[n] + k1)
                e.dma_start(tiled(tabs[n][t0 * P:t1 * P, :]), TB[:, t0:t1, 0:w]).then_inc(sem("table_written"), 16)
            e.wait_ge(sem("table_written"), 16 * TABLE_PARTS * (n + 1))

        def side_by_side(bank):
            return bank[:, :].rearrange("p (t d) -> p d t", d=D)

        def sums_pe(e, src, bank, masked):
            for t in range(0, TILES - 1, 8):
                e.matmul(bank[:, :], ones[:, :], src[:, t:t + 8, :].rearrange("p t d -> p (t d)"), start=(t == 0), stop=False)
            e.matmul(bank[:, 0:D], (lastones if masked else ones)[:, :], src[:, TILES - 1, :], start=False, stop=True)\
                .then_inc(sem("summed"), 1)

        def per_node(ap):
            return ap.unsqueeze(2).to_broadcast([P, TILES, D])

        def per_feat(ap):
            return ap.unsqueeze(1).to_broadcast([P, TILES, D])

        Z = TB[:, :, 0:D]

        def pe_moments(e):
            for s in range(2):
                e.wait_ge(sem("weighted_z"), s + 1)
                sums_pe(e, T1, B[s], False)
            for s in range(2):
                e.wait_ge(sem("powers_z"), s + 1)
                sums_pe(e, T2, B[2 + 2 * s], False)
                sums_pe(e, T1, B[3 + 2 * s], False)

        def moments(e, v):
            for s in range(2):
                v(e.tensor_tensor(T1[:, :, :], Z, per_node(CNT[:, s, :]), ALU.mult))
                e.sem_inc(sem("weighted_z"), 1)
                e.wait_ge(sem("summed"), s + 1)
                v(e.tensor_reduce(MU[:, s, :], side_by_side(B[s]), AX.X, ALU.add))
            mu = MU[:, :, :].rearrange("p s d -> p (s d)")
            v(e.tensor_scalar(mu, mu, 1.0 / E, None, ALU.mult))
            for s in range(2):
                v(e.tensor_tensor(T1[:, :, :], Z, per_feat(MU[:, s, :]), ALU.subtract))
                v(e.tensor_tensor(T2[:, :, :], T1[:, :, :], T1[:, :, :], ALU.mult))
                v(e.tensor_tensor(T2[:, :, :], T2[:, :, :], per_node(CNT[:, s, :]), ALU.mult))
                v(e.tensor_tensor(T1[:, :, :], T1[:, :, :], T2[:, :, :], ALU.mult))
                e.sem_inc(sem("powers_z"), 1)
                e.wait_ge(sem("summed"), 2 + 2 * s + 2)
                for k in range(2):
                    v(e.tensor_reduce(MK[:, 2 * s + k, :], side_by_side(B[2 + 2 * s + k]), AX.X, ALU.add))
            mk = MK[:, :, :].rearrange("p s d -> p (s d)")
            a = MK2[:, :, :].rearrange("p s d -> p (s d)")
            b = MK3[:, :, :].rearrange("p s d -> p (s d)")
            v(e.tensor_scalar(mk, mk, 1.0 / E, None, ALU.mult))
            v(e.tensor_scalar(a, mk, -1.0, None, ALU.mult))
            v(e.tensor_tensor(a, a, mk, ALU.max))
            v(e.tensor_scalar(a, a, 1e-18, None, ALU.max))
            e.sem_inc(sem("moments_in"), 1)
            v(e.tensor_scalar(b, mk, 0.0, None, ALU.is_gt))
            v(e.tensor_scalar(mk, mk, 0.0, None, ALU.is_lt))
            v(e.tensor_tensor(b, b, mk, ALU.subtract))
            e.wait_ge(sem("roots_done"), 1)
            v(e.tensor_tensor(b, b, a, ALU.mult))
            v(e.tensor_tensor(b, b, UV[:, :, :].rearrange("p s d -> p (s d)"), ALU.mult))
            v(e.tensor_reduce(CONST[:, :], b, AX.X, ALU.add))
            v(e.tensor_scalar(KF[:, :, 0], KF[:, :, 0], CONST[:, :], None, ALU.add))

        def act_moments(e):
            e.wait_ge(sem("moments_in"), 1)
            a = MK2[:, :, :].rearrange("p (s k) d -> p s k d", k=2)
            e.activation(a[:, :, 0, :], a[:, :, 0, :], ACT.Sqrt)
            e.activation(a[:, :, 1, :], a[:, :, 1, :], ACT.Ln).then_inc(sem("log_done"), 1)
            e.wait_ge(sem("log_done"), 1)
            e.activation(a[:, :, 1, :], a[:, :, 1, :], ACT.Exp, scale=1.0 / 3).then_inc(sem("roots_done"), 1)

        def layernorm(e, v, last_n):
            v(e.tensor_tensor(T1[:, :, :], T1[:, :, :], X[:, :, :], ALU.add))
            v(e.tensor_reduce(NV[:, 0, :], T1[:, :, :], AX.X, ALU.add))
            v(e.tensor_scalar(NV[:, 0, :], NV[:, 0, :], 1.0 / D, None, ALU.mult))
            v(e.tensor_tensor(T1[:, :, :], T1[:, :, :], per_node(NV[:, 0, :]), ALU.subtract))
            v(e.tensor_tensor(T2[:, :, :], T1[:, :, :], T1[:, :, :], ALU.mult))
            v(e.tensor_reduce(NV[:, 1, :], T2[:, :, :], AX.X, ALU.add))
            v(e.tensor_scalar(NV[:, 1, :], NV[:, 1, :], 1.0 / D, LN_EPS, ALU.mult, ALU.add))
            e.sem_inc(sem("ln_var"), 1)
            e.wait_ge(sem("ln_root"), last_n + 1)
            v(e.reciprocal(NV[:, 3, :], NV[:, 2, :]))
            v(e.tensor_tensor(X[:, :, :], T1[:, :, :], per_node(NV[:, 3, :]), ALU.mult))

        def act_layernorm(e, k):
            e.wait_ge(sem("ln_var"), k + 1)
            e.activation(NV[:, 2, :], NV[:, 1, :], ACT.Sqrt).then_inc(sem("ln_root"), 1)

        def dve_finish(e, v, n):
            e.wait_ge(sem("sums_added"), (n + 1) * NG)
            nv = lambda k: NV[:, k, :]
            if n < 2:
                z, r = ACC[:, :, D], NV[:, 1, :]
                v(e.tensor_tensor(nv(0), AS[:, :], KF[:, :, 0], ALU.add))
                v(e.scalar_tensor_tensor(out=nv(0), in0=nv(0), scalar=0.2, in1=nv(0), op0=ALU.mult, op1=ALU.max))
                v(e.tensor_scalar(nv(2), z, 0.0, None, ALU.is_le))
                v(e.tensor_tensor(nv(1), z, nv(2), ALU.add))
                v(e.reciprocal(nv(3), nv(1)))
                v(e.tensor_tensor(nv(1), ACC[:, :, WA - 1], nv(3), ALU.mult))
                v(e.scalar_tensor_tensor(out=nv(2), in0=nv(2), scalar=-BIG, in1=r, op0=ALU.mult, op1=ALU.add))
                v(e.tensor_tensor(nv(3), nv(2), nv(0), ALU.max))
                v(e.tensor_tensor(nv(4), nv(2), nv(3), ALU.subtract))
                v(e.tensor_tensor(nv(5), nv(0), nv(3), ALU.subtract))
                e.sem_inc(sem("self_in"), 1)
                e.wait_ge(sem("self_out"), n + 1)
                v(e.tensor_tensor(nv(1), z, nv(6), ALU.mult))
                v(e.tensor_tensor(nv(1), nv(1), nv(7), ALU.add))
                v(e.tensor_scalar(nv(1), nv(1), 1e-16, None, ALU.add))
                v(e.reciprocal(nv(2), nv(1)))
                v(e.tensor_tensor(T1[:, :, :], ACC[:, :, 0:D], per_node(nv(6)), ALU.mult))
                v(e.tensor_tensor(T2[:, :, :], TB[:, :, 0:D], per_node(nv(7)), ALU.mult))
                v(e.tensor_tensor(T1[:, :, :], T1[:, :, :], T2[:, :, :], ALU.add))
                v(e.tensor_tensor(T1[:, :, :], T1[:, :, :], per_node(nv(2)), ALU.mult))
                v(e.tensor_tensor(T1[:, :, :], T1[:, :, :], per_feat(ROW[:, n, :]), ALU.add))
                if n == 0:
                    v(e.tensor_scalar(X1[:, :, :], T1[:, :, :], 0.0, None, ALU.max))
                else:
                    layernorm(e, v, 0)
            elif n == 2:
                z = ACC[:, :, D]
                v(e.tensor_scalar(nv(0), z, 0.0, None, ALU.is_le))
                v(e.tensor_tensor(nv(0), nv(0), z, ALU.add))
                v(e.reciprocal(nv(1), nv(0)))
                v(e.tensor_copy(T1[:, :, :], ACC[:, :, 0:D]))
                for i in range(2):
                    v(e.tensor_tensor(T2[:, :, :], per_node(ACC[:, :, D + 1 + i]), per_feat(WES[:, 2 + i * D:2 + (i + 1) * D]), ALU.mult))
                    v(e.tensor_tensor(T1[:, :, :], T1[:, :, :], T2[:, :, :], ALU.add))
                v(e.tensor_tensor(T1[:, :, :], T1[:, :, :], per_node(nv(1)), ALU.mult))
                layernorm(e, v, 1)
            elif n < 5:
                l = n - 3
                v(e.tensor_tensor(T1[:, :, :], ACC[:, :, 0:D], ROOT[:, :, :], ALU.add))
                v(e.tensor_scalar(T1[:, :, :], T1[:, :, :], 0.0, None, ALU.max))
                e.sem_inc(sem("bn_in"), 1)
                e.wait_ge(sem("summed"), 6 + 2 * l + 1)
                v(e.tensor_reduce(BN[:, 0, :], side_by_side(B[4]), AX.X, ALU.add))
                v(e.tensor_scalar(BN[:, 0, :], BN[:, 0, :], 1.0 / N, None, ALU.mult))
                v(e.tensor_tensor(T1[:, :, :], T1[:, :, :], per_feat(BN[:, 0, :]), ALU.subtract))
                v(e.tensor_tensor(T2[:, :, :], T1[:, :, :], T1[:, :, :], ALU.mult))
                e.sem_inc(sem("bn_sq"), 1)
                e.wait_ge(sem("summed"), 6 + 2 * l + 2)
                v(e.tensor_reduce(BN[:, 1, :], side_by_side(B[5]), AX.X, ALU.add))
                v(e.tensor_scalar(BN[:, 1, :], BN[:, 1, :], 1.0 / N, BN_EPS, ALU.mult, ALU.add))
                e.sem_inc(sem("bn_var"), 1)
                e.wait_ge(sem("bn_root"), l + 1)
                v(e.reciprocal(BN[:, 3, :], BN[:, 2, :]))
                v(e.tensor_tensor(BN[:, 3, :], BN[:, 3, :], ROW[:, 2 + l, :], ALU.mult))
                v(e.tensor_tensor(T1[:, :, :], T1[:, :, :], per_feat(BN[:, 3, :]), ALU.mult))
                dst = X1 if l == 0 else T1
                v(e.tensor_tensor(dst[:, :, :], T1[:, :, :], per_feat(ROW[:, 4 + l, :]), ALU.add))
                if l == 1:
                    layernorm(e, v, 2)
            else:
                v(e.tensor_scalar(nv(0), CNT[:, 1, :], 0.0, None, ALU.is_gt))
                v(e.tensor_tensor(T1[:, :, :], ACC[:, :, 0:D], per_feat(ROW[:, 6, :]), ALU.add))
                v(e.tensor_tensor(T1[:, :, :], T1[:, :, :], per_node(nv(0)), ALU.mult))
                layernorm(e, v, 3)
            e.sem_inc(sem("x_ready"), 1)

        def pe_finish(e, n):
            if n in (3, 4):
                e.wait_ge(sem("bn_in"), n - 2)
                sums_pe(e, T1, B[4], True)
                e.wait_ge(sem("bn_sq"), n - 2)
                sums_pe(e, T2, B[5], True)

        def act_finish(e, n):
            if n < 2:
                e.wait_ge(sem("self_in"), n + 1)
                e.activation(NV[:, 6, :], NV[:, 4, :], ACT.Exp)
                e.activation(NV[:, 7, :], NV[:, 5, :], ACT.Exp).then_inc(sem("self_out"), 1)
            if n in (3, 4):
                e.wait_ge(sem("bn_var"), n - 2)
                e.activation(BN[:, 2, :], BN[:, 1, :], ACT.Sqrt).then_inc(sem("bn_root"), 1)
            if n in (1, 2, 4, 5):
                act_layernorm(e, {1: 0, 2: 1, 4: 2, 5: 3}[n])

        @block.gpsimd
        def _(e):
            pool_prep(e)
            for n in range(6):
                pool_pass(e, n)

        @block.sync
        def _(e):
            sp_prep(e)
            e.wait_ge(sem("rows_built"), 1)
            for f in range(3):
                e.dma_start(rows_d[f:f + 1, :].rearrange("o (k v i) -> v (o k) i", k=VB, v=P), RB[:, f, :, :]).then_inc(sem("rows_stored"), 16)
            e.wait_ge(sem("rows_stored"), 48)
            for n in range(6):
                sp_table(e, n)
                if n == 1:
                    e.dma_start(FLD[:, F_W, :].bitcast(i32), tv_d[:, :].rearrange("k p -> (k p)").unsqueeze(0).to_broadcast([P, VP]))\
                        .then_inc(sem("tiles_in"), 16)
                sp_stream(e, n)
                if KINDS[n] == "A":
                    sp_kept(e, n)
            e.wait_ge(sem("x_ready"), 7)
            e.dma_start(out[0:(TILES - 1) * P, :].rearrange("(t p) w -> p t w", p=P), X[:, 0:TILES - 1, :]).then_inc(sem("result_out"), 16)
            e.dma_start(out[(TILES - 1) * P:N, :], X[0:LASTN, TILES - 1, :]).then_inc(sem("result_out"), 16)
            e.wait_ge(sem("result_out"), 32)

        @block.tensor
        def _(e):
            pe_prep(e)
            e.wait_ge(sem("walk_in"), 16)
            for n in range(6):
                pe_project(e, n)
                if n == 2:
                    pe_moments(e)
                if KINDS[n] == "A":
                    pe_scores(e, n)
                    pe_segments(e, n)
                pe_pass(e, n)
                pe_finish(e, n)

        @block.scalar
        def _(e):
            act_prep(e)
            for n in range(6):
                act_project(e, n)
                if KINDS[n] == "A":
                    act_ahead(e, n)
                    act_segments(e, n)
                act_pass(e, n)
                act_finish(e, n)

        @block.vector
        def _(e):
            v = Own(e, "dve_done")
            dve_prep(e, v)
            e.wait_ge(sem("x_in"), 32)
            e.wait_ge(sem("walk_in"), 16)
            e.sem_inc(sem("x_ready"), 1)
            for n in range(6):
                dve_project(e, v, n)
                if KINDS[n] == "A":
                    dve_scores(e, v, n)
                    dve_segments(e, v, n)
                dve_pass(e, n)
                dve_finish(e, v, n)


_INS = ["x", "src", "dst", "edge_attr_2", "L0_gnn_W1", "L0_gnn_a_src1", "L0_gnn_a_dst1", "L0_gnn_b1", "L0_gnn_W2",
        "L0_gnn_a_src2", "L0_gnn_a_dst2", "L0_gnn_b2", "L1_gnn_W_fc", "L1_gnn_W_attn", "L1_gnn_W_edge", "L1_gnn_W_e2n",
        "L1_gnn_W_m1", "L1_gnn_W_m2", "L2_gnn_Wk", "L2_gnn_bk", "L2_gnn_Wq", "L2_gnn_bq", "L2_gnn_Wv", "L2_gnn_bv",
        "L2_gnn_Ws", "L2_gnn_bs", "L2_gnn_bias", "L2_gnn_gamma", "L2_gnn_beta", "L3_gnn_W1", "L3_gnn_b1", "L3_gnn_W2",
        "L3_gnn_b2"]


def kernel(**inputs):
    import numpy as _np
    import concourse.bacc as _bacc
    from concourse import mybir as _mybir
    from concourse.bass_utils import run_bass_kernel_spmd as _run

    nc = _bacc.Bacc("TRN2", target_bir_lowering=False, num_devices=1)
    arrays, args = {}, {}
    for name in _INS:
        a = _np.ascontiguousarray(inputs[name])
        arrays[f"in_{name}"] = a
        args[name] = nc.dram_tensor(f"in_{name}", a.shape, _mybir.dt.from_np(a.dtype), kind="ExternalInput").ap()
    result = nc.dram_tensor("out_0", (N, D), _mybir.dt.float32, kind="ExternalOutput").ap()
    build(nc, args, result)
    r = _run(nc, [arrays], core_ids=[0])
    return r.results[0]["out_0"]
```
